# Optimizing a Trainium2 kernel written in Bass

```python
import numpy as np
import jax
import jax.numpy as jnp

def _softmax(x, axis=-1):
    return jax.nn.softmax(x, axis=axis)
def _gelu(x):
    return jax.nn.gelu(x, approximate=True)
def _silu(x):
    return jax.nn.silu(x)
def _sigmoid(x):
    return jax.nn.sigmoid(x)
def _layernorm(x, axis=-1, eps=1e-5):
    m = jnp.mean(x, axis=axis, keepdims=True)
    v = jnp.var(x, axis=axis, keepdims=True)
    return (x - m) / jnp.sqrt(v + eps)
def _scatter_add(tgt, idx, src, axis=0):
    return tgt.at[idx].add(src)
def _segment_sum(src, seg, n):
    return jax.ops.segment_sum(src, seg, n)

kernel_name = 'mk_conv_preact_d2_conv_nchw192_c977af'

def setup_inputs(seed: int = 0):
    np.random.seed(seed)
    _w = jnp.asarray
    def _rec_inputs():
        import jax
        import jax.numpy as jnp
        _gk = jax.random.key(seed)
        x = -0.0001538 + 1 * jax.random.normal(jax.random.fold_in(_gk, 1), (8, 192, 64, 64), jnp.float32)
        return x
    x = _rec_inputs()
    def _L0_conv_setup():
        import jax, jax.numpy as jnp
        import numpy as np
        import math
        K_GROUP = 4
        LN_EPS = 1e-05

        def _ss2d_forward(x, in_proj_w, conv_w, conv_b, x_proj_weight, dt_projs_weight, dt_projs_bias, A_logs, Ds, ln_w, ln_b, out_proj_w):
            B, Dm, H, W = x.shape
            Din = in_proj_w.shape[0]
            K = K_GROUP
            R = dt_projs_weight.shape[2]
            N = A_logs.shape[1]
            L = H * W
            h = jnp.einsum('bchw,dc->bdhw', x, in_proj_w)
            h = jax.lax.conv_general_dilated(h, conv_w, window_strides=(1, 1), padding=((1, 1), (1, 1)), dimension_numbers=('NCHW', 'OIHW', 'NCHW'), feature_group_count=Din)
            h = h + conv_b[None, :, None, None]
            h = jax.nn.silu(h)
            xr = h.reshape(B, Din, L)
            xt = jnp.swapaxes(h, 2, 3).reshape(B, Din, L)
            xs = jnp.stack([xr, xt, xr[..., ::-1], xt[..., ::-1]], axis=1)
            x_dbl = jnp.einsum('bkdl,kcd->bkcl', xs, x_proj_weight)
            dts_r = x_dbl[:, :, :R]
            Bs = x_dbl[:, :, R:R + N]
            Cs = x_dbl[:, :, R + N:R + 2 * N]
            dts = jnp.einsum('bkrl,kdr->bkdl', dts_r, dt_projs_weight)
            delta = jax.nn.softplus(dts + dt_projs_bias[None, :, :, None])
            A = -jnp.exp(A_logs.astype(jnp.float32)).reshape(K, Din, N)
            u = xs
            delta_t = jnp.moveaxis(delta, -1, 0)
            u_t = jnp.moveaxis(u, -1, 0)
            B_t = jnp.moveaxis(Bs, -1, 0)
            C_t = jnp.moveaxis(Cs, -1, 0)

            def step(hstate, inp):
                dl, ul, bl, cl = inp
                hstate = jnp.exp(dl[..., None] * A) * hstate + (dl * ul)[..., None] * bl[:, :, None, :]
                y = jnp.einsum('bkdn,bkn->bkd', hstate, cl)
                return (hstate, y)
            h0 = jnp.zeros((B, K, Din, N), jnp.float32)
            _, ys = jax.lax.scan(step, h0, (delta_t, u_t, B_t, C_t))
            ys = jnp.moveaxis(ys, 0, -1)
            ys = ys + Ds.reshape(K, Din)[None, :, :, None] * u
            y = ys[:, 0] + ys[:, 2, :, ::-1]
            yt = ys[:, 1] + ys[:, 3, :, ::-1]
            y = y + jnp.swapaxes(yt.reshape(B, Din, W, H), 2, 3).reshape(B, Din, L)
            y = y.reshape(B, Din, H, W)
            mu = y.mean(axis=1, keepdims=True)
            var = y.var(axis=1, keepdims=True)
            y = (y - mu) * jax.lax.rsqrt(var + LN_EPS)
            y = y * ln_w[None, :, None, None] + ln_b[None, :, None, None]
            return jnp.einsum('bdhw,md->bmhw', y, out_proj_w)
        key = jax.random.key(seed)
        ks = jax.random.split(key, 8)
        B, Dm, H, W = (8, 192, 64, 64)
        Din, N, R, K = (384, 16, 12, 4)
        x = jax.random.normal(ks[0], (B, Dm, H, W), jnp.float32)
        in_proj_w = jax.random.normal(ks[1], (Din, Dm), jnp.float32) * Dm ** (-0.5)
        conv_w = jax.random.normal(ks[2], (Din, 1, 3, 3), jnp.float32) * (1.0 / 3.0)
        conv_b = jnp.zeros((Din,), jnp.float32)
        x_proj_weight = jax.random.normal(ks[3], (K, R + 2 * N, Din), jnp.float32) * Din ** (-0.5)
        dt_std = R ** (-0.5)
        dt_projs_weight = jax.random.uniform(ks[4], (K, Din, R), jnp.float32, -dt_std, dt_std)
        dt = jnp.exp(jax.random.uniform(ks[5], (K, Din), jnp.float32) * (math.log(0.1) - math.log(0.001)) + math.log(0.001))
        dt = jnp.clip(dt, 0.0001, None)
        dt_projs_bias = dt + jnp.log(-jnp.expm1(-dt))
        A_logs = jnp.log(jnp.tile(jnp.arange(1, N + 1, dtype=jnp.float32)[None, :], (K * Din, 1)))
        Ds = jnp.ones((K * Din,), jnp.float32)
        ln_w = jnp.ones((Din,), jnp.float32)
        ln_b = jnp.zeros((Din,), jnp.float32)
        out_proj_w = jax.random.normal(ks[6], (Dm, Din), jnp.float32) * Din ** (-0.5)
        return {'x': x, 'in_proj_w': in_proj_w, 'conv_w': conv_w, 'conv_b': conv_b, 'x_proj_weight': x_proj_weight, 'dt_projs_weight': dt_projs_weight, 'dt_projs_bias': dt_projs_bias, 'A_logs': A_logs, 'Ds': Ds, 'ln_w': ln_w, 'ln_b': ln_b, 'out_proj_w': out_proj_w}
    _L0_conv_all = _L0_conv_setup()
    _L0_conv_in = {k: v for k, v in _L0_conv_all.items() if k in ('in_proj_w', 'conv_w', 'conv_b', 'x_proj_weight', 'dt_projs_weight', 'dt_projs_bias', 'A_logs', 'Ds', 'ln_w', 'ln_b', 'out_proj_w', )}
    del _L0_conv_all

    def _L1_conv_setup():
        import jax, jax.numpy as jnp
        import numpy as np
        from jax import lax
        B, CI, H, W = (16, 192, 64, 64)
        CO = 192
        CB = CI // 3
        D_STATE, D_CONV, EXPAND = (16, 4, 2)
        D_INNER = EXPAND * CB
        DT_RANK = -(-CB // 16)
        EPS = 1e-05

        def _ln(x, w, b):
            m = jnp.mean(x, -1, keepdims=True)
            v = jnp.mean(jnp.square(x - m), -1, keepdims=True)
            return (x - m) * lax.rsqrt(v + EPS) * w + b

        def _silu(x):
            return x * jax.nn.sigmoid(x)

        def _mamba(u, in_proj_w, convd_w, convd_b, x_proj_w, dt_proj_w, dt_proj_b, A_log, D_param, out_proj_w):
            Bsz, L, _ = u.shape
            xz = u @ in_proj_w.T
            xm, z = jnp.split(xz, 2, axis=-1)
            xp = jnp.pad(xm, ((0, 0), (D_CONV - 1, 0), (0, 0)))
            xc = convd_b
            for k in range(D_CONV):
                xc = xc + xp[:, k:k + L, :] * convd_w[:, k]
            xc = _silu(xc)
            dbl = xc @ x_proj_w.T
            dt = dbl[..., :DT_RANK]
            Bm = dbl[..., DT_RANK:DT_RANK + D_STATE]
            Cm = dbl[..., DT_RANK + D_STATE:]
            dt = jax.nn.softplus(dt @ dt_proj_w.T + dt_proj_b)
            A = -jnp.exp(A_log)

            def step(h, inp):
                dt_t, B_t, C_t, x_t = inp
                dA = jnp.exp(dt_t[..., None] * A)
                h = dA * h + (dt_t * x_t)[..., None] * B_t[:, None, :]
                y = jnp.einsum('bds,bs->bd', h, C_t)
                return (h, y)
            xs = (dt.transpose(1, 0, 2), Bm.transpose(1, 0, 2), Cm.transpose(1, 0, 2), xc.transpose(1, 0, 2))
            h0 = jnp.zeros((Bsz, D_INNER, D_STATE), u.dtype)
            _, ys = lax.scan(step, h0, xs)
            y = ys.transpose(1, 0, 2) + xc * D_param
            y = y * _silu(z)
            return y @ out_proj_w.T
        key = jax.random.key(seed)
        ks = jax.random.split(key, 16)
        s = 0.05
        return {'x': jax.random.normal(ks[0], (B, CI, H, W), jnp.float32), 'conv1_w': jax.random.normal(ks[1], (CB, CI, 3, 3), jnp.float32) * s, 'conv1_b': jnp.zeros((CB,), jnp.float32), 'norm1_w': jnp.ones((CB,), jnp.float32), 'norm1_b': jnp.zeros((CB,), jnp.float32), 'norm_w': jnp.ones((CI,), jnp.float32), 'norm_b': jnp.zeros((CI,), jnp.float32), 'proj_w': jax.random.normal(ks[2], (CO, CI), jnp.float32) * s, 'proj_b': jnp.zeros((CO,), jnp.float32), 'skip_scale': jnp.ones((1,), jnp.float32), 'in_proj_w': jax.random.normal(ks[3], (2 * D_INNER, CB), jnp.float32) * s, 'convd_w': jax.random.normal(ks[4], (D_INNER, D_CONV), jnp.float32) * s, 'convd_b': jnp.zeros((D_INNER,), jnp.float32), 'x_proj_w': jax.random.normal(ks[5], (DT_RANK + 2 * D_STATE, D_INNER), jnp.float32) * s, 'dt_proj_w': jax.random.normal(ks[6], (D_INNER, DT_RANK), jnp.float32) * s, 'dt_proj_b': jax.random.normal(ks[7], (D_INNER,), jnp.float32) * s, 'A_log': jnp.log(jnp.tile(jnp.arange(1, D_STATE + 1, dtype=jnp.float32), (D_INNER, 1))), 'D_param': jnp.ones((D_INNER,), jnp.float32), 'out_proj_w': jax.random.normal(ks[8], (CB, D_INNER), jnp.float32) * s}
    _L1_conv_all = _L1_conv_setup()
    _L1_conv_in = {k: v for k, v in _L1_conv_all.items() if k in ('conv1_w', 'conv1_b', 'norm1_w', 'norm1_b', 'norm_w', 'norm_b', 'proj_w', 'proj_b', 'skip_scale', 'in_proj_w', 'convd_w', 'convd_b', 'x_proj_w', 'dt_proj_w', 'dt_proj_b', 'A_log', 'D_param', 'out_proj_w', )}
    del _L1_conv_all

    return {
        "x": x,
        "L0_conv_in_proj_w": _L0_conv_in["in_proj_w"],
        "L0_conv_conv_w": _L0_conv_in["conv_w"],
        "L0_conv_conv_b": _L0_conv_in["conv_b"],
        "L0_conv_x_proj_weight": _L0_conv_in["x_proj_weight"],
        "L0_conv_dt_projs_weight": _L0_conv_in["dt_projs_weight"],
        "L0_conv_dt_projs_bias": _L0_conv_in["dt_projs_bias"],
        "L0_conv_A_logs": _L0_conv_in["A_logs"],
        "L0_conv_Ds": _L0_conv_in["Ds"],
        "L0_conv_ln_w": _L0_conv_in["ln_w"],
        "L0_conv_ln_b": _L0_conv_in["ln_b"],
        "L0_conv_out_proj_w": _L0_conv_in["out_proj_w"],
        "L1_conv_conv1_w": _L1_conv_in["conv1_w"],
        "L1_conv_conv1_b": _L1_conv_in["conv1_b"],
        "L1_conv_norm1_w": _L1_conv_in["norm1_w"],
        "L1_conv_norm1_b": _L1_conv_in["norm1_b"],
        "L1_conv_norm_w": _L1_conv_in["norm_w"],
        "L1_conv_norm_b": _L1_conv_in["norm_b"],
        "L1_conv_proj_w": _L1_conv_in["proj_w"],
        "L1_conv_proj_b": _L1_conv_in["proj_b"],
        "L1_conv_skip_scale": _L1_conv_in["skip_scale"],
        "L1_conv_in_proj_w": _L1_conv_in["in_proj_w"],
        "L1_conv_convd_w": _L1_conv_in["convd_w"],
        "L1_conv_convd_b": _L1_conv_in["convd_b"],
        "L1_conv_x_proj_w": _L1_conv_in["x_proj_w"],
        "L1_conv_dt_proj_w": _L1_conv_in["dt_proj_w"],
        "L1_conv_dt_proj_b": _L1_conv_in["dt_proj_b"],
        "L1_conv_A_log": _L1_conv_in["A_log"],
        "L1_conv_D_param": _L1_conv_in["D_param"],
        "L1_conv_out_proj_w": _L1_conv_in["out_proj_w"],
    }

def reference(x, L0_conv_in_proj_w, L0_conv_conv_w, L0_conv_conv_b, L0_conv_x_proj_weight, L0_conv_dt_projs_weight, L0_conv_dt_projs_bias, L0_conv_A_logs, L0_conv_Ds, L0_conv_ln_w, L0_conv_ln_b, L0_conv_out_proj_w, L1_conv_conv1_w, L1_conv_conv1_b, L1_conv_norm1_w, L1_conv_norm1_b, L1_conv_norm_w, L1_conv_norm_b, L1_conv_proj_w, L1_conv_proj_b, L1_conv_skip_scale, L1_conv_in_proj_w, L1_conv_convd_w, L1_conv_convd_b, L1_conv_x_proj_w, L1_conv_dt_proj_w, L1_conv_dt_proj_b, L1_conv_A_log, L1_conv_D_param, L1_conv_out_proj_w):
    import jax
    import jax.numpy as jnp
    def _L0_conv_ref(x, in_proj_w, conv_w, conv_b, x_proj_weight, dt_projs_weight, dt_projs_bias, A_logs, Ds, ln_w, ln_b, out_proj_w):
        import jax, jax.numpy as jnp
        import numpy as np
        import math
        K_GROUP = 4
        LN_EPS = 1e-05

        def _ss2d_forward(x, in_proj_w, conv_w, conv_b, x_proj_weight, dt_projs_weight, dt_projs_bias, A_logs, Ds, ln_w, ln_b, out_proj_w):
            B, Dm, H, W = x.shape
            Din = in_proj_w.shape[0]
            K = K_GROUP
            R = dt_projs_weight.shape[2]
            N = A_logs.shape[1]
            L = H * W
            h = jnp.einsum('bchw,dc->bdhw', x, in_proj_w)
            h = jax.lax.conv_general_dilated(h, conv_w, window_strides=(1, 1), padding=((1, 1), (1, 1)), dimension_numbers=('NCHW', 'OIHW', 'NCHW'), feature_group_count=Din)
            h = h + conv_b[None, :, None, None]
            h = jax.nn.silu(h)
            xr = h.reshape(B, Din, L)
            xt = jnp.swapaxes(h, 2, 3).reshape(B, Din, L)
            xs = jnp.stack([xr, xt, xr[..., ::-1], xt[..., ::-1]], axis=1)
            x_dbl = jnp.einsum('bkdl,kcd->bkcl', xs, x_proj_weight)
            dts_r = x_dbl[:, :, :R]
            Bs = x_dbl[:, :, R:R + N]
            Cs = x_dbl[:, :, R + N:R + 2 * N]
            dts = jnp.einsum('bkrl,kdr->bkdl', dts_r, dt_projs_weight)
            delta = jax.nn.softplus(dts + dt_projs_bias[None, :, :, None])
            A = -jnp.exp(A_logs.astype(jnp.float32)).reshape(K, Din, N)
            u = xs
            delta_t = jnp.moveaxis(delta, -1, 0)
            u_t = jnp.moveaxis(u, -1, 0)
            B_t = jnp.moveaxis(Bs, -1, 0)
            C_t = jnp.moveaxis(Cs, -1, 0)

            def step(hstate, inp):
                dl, ul, bl, cl = inp
                hstate = jnp.exp(dl[..., None] * A) * hstate + (dl * ul)[..., None] * bl[:, :, None, :]
                y = jnp.einsum('bkdn,bkn->bkd', hstate, cl)
                return (hstate, y)
            h0 = jnp.zeros((B, K, Din, N), jnp.float32)
            _, ys = jax.lax.scan(step, h0, (delta_t, u_t, B_t, C_t))
            ys = jnp.moveaxis(ys, 0, -1)
            ys = ys + Ds.reshape(K, Din)[None, :, :, None] * u
            y = ys[:, 0] + ys[:, 2, :, ::-1]
            yt = ys[:, 1] + ys[:, 3, :, ::-1]
            y = y + jnp.swapaxes(yt.reshape(B, Din, W, H), 2, 3).reshape(B, Din, L)
            y = y.reshape(B, Din, H, W)
            mu = y.mean(axis=1, keepdims=True)
            var = y.var(axis=1, keepdims=True)
            y = (y - mu) * jax.lax.rsqrt(var + LN_EPS)
            y = y * ln_w[None, :, None, None] + ln_b[None, :, None, None]
            return jnp.einsum('bdhw,md->bmhw', y, out_proj_w)
        return _ss2d_forward(x, in_proj_w, conv_w, conv_b, x_proj_weight, dt_projs_weight, dt_projs_bias, A_logs, Ds, ln_w, ln_b, out_proj_w)

    def _L1_conv_ref(x, conv1_w, conv1_b, norm1_w, norm1_b, norm_w, norm_b, proj_w, proj_b, skip_scale, in_proj_w, convd_w, convd_b, x_proj_w, dt_proj_w, dt_proj_b, A_log, D_param, out_proj_w):
        import jax, jax.numpy as jnp
        import numpy as np
        from jax import lax
        B, CI, H, W = (16, 192, 64, 64)
        CO = 192
        CB = CI // 3
        D_STATE, D_CONV, EXPAND = (16, 4, 2)
        D_INNER = EXPAND * CB
        DT_RANK = -(-CB // 16)
        EPS = 1e-05

        def _ln(x, w, b):
            m = jnp.mean(x, -1, keepdims=True)
            v = jnp.mean(jnp.square(x - m), -1, keepdims=True)
            return (x - m) * lax.rsqrt(v + EPS) * w + b

        def _silu(x):
            return x * jax.nn.sigmoid(x)

        def _mamba(u, in_proj_w, convd_w, convd_b, x_proj_w, dt_proj_w, dt_proj_b, A_log, D_param, out_proj_w):
            Bsz, L, _ = u.shape
            xz = u @ in_proj_w.T
            xm, z = jnp.split(xz, 2, axis=-1)
            xp = jnp.pad(xm, ((0, 0), (D_CONV - 1, 0), (0, 0)))
            xc = convd_b
            for k in range(D_CONV):
                xc = xc + xp[:, k:k + L, :] * convd_w[:, k]
            xc = _silu(xc)
            dbl = xc @ x_proj_w.T
            dt = dbl[..., :DT_RANK]
            Bm = dbl[..., DT_RANK:DT_RANK + D_STATE]
            Cm = dbl[..., DT_RANK + D_STATE:]
            dt = jax.nn.softplus(dt @ dt_proj_w.T + dt_proj_b)
            A = -jnp.exp(A_log)

            def step(h, inp):
                dt_t, B_t, C_t, x_t = inp
                dA = jnp.exp(dt_t[..., None] * A)
                h = dA * h + (dt_t * x_t)[..., None] * B_t[:, None, :]
                y = jnp.einsum('bds,bs->bd', h, C_t)
                return (h, y)
            xs = (dt.transpose(1, 0, 2), Bm.transpose(1, 0, 2), Cm.transpose(1, 0, 2), xc.transpose(1, 0, 2))
            h0 = jnp.zeros((Bsz, D_INNER, D_STATE), u.dtype)
            _, ys = lax.scan(step, h0, xs)
            y = ys.transpose(1, 0, 2) + xc * D_param
            y = y * _silu(z)
            return y @ out_proj_w.T
        def branch(xi):
            h = lax.conv_general_dilated(xi, conv1_w, (1, 1), 'SAME', dimension_numbers=('NCHW', 'OIHW', 'NCHW'))
            h = h + conv1_b[None, :, None, None]
            b, c, hh, ww = h.shape
            seq = h.reshape(b, c, hh * ww).transpose(0, 2, 1)
            xn = _ln(seq, norm1_w, norm1_b)
            ym = _mamba(xn, in_proj_w, convd_w, convd_b, x_proj_w, dt_proj_w, dt_proj_b, A_log, D_param, out_proj_w)
            return ym + skip_scale * xn
        y1 = branch(x)
        y2 = branch(x[:, :, :, ::-1])
        y3 = branch(x[:, :, ::-1, :])
        y = jnp.concatenate([y1, y2, y3], axis=2)
        y = _ln(y, norm_w, norm_b)
        y = y @ proj_w.T + proj_b
        return y.transpose(0, 2, 1).reshape(x.shape[0], CO, H, W)

    def _gn(v, G=32, eps=1e-5):
        B_, C_, H_, W_ = v.shape
        g = v.reshape(B_, G, C_ // G, H_, W_)
        m = jnp.mean(g, axis=(2, 3, 4), keepdims=True)
        s = jnp.var(g, axis=(2, 3, 4), keepdims=True)
        return ((g - m) / jnp.sqrt(s + eps)).reshape(v.shape)

    def _ln_c(v, eps=1e-6):
        m = jnp.mean(v, axis=1, keepdims=True)
        s = jnp.var(v, axis=1, keepdims=True)
        return (v - m) / jnp.sqrt(s + eps)

    def _ln_t(v, eps=1e-5):
        m = jnp.mean(v, axis=-1, keepdims=True)
        s = jnp.var(v, axis=-1, keepdims=True)
        return (v - m) / jnp.sqrt(s + eps)

    def _to_tokens(v):
        B_, C_, H_, W_ = v.shape
        return v.reshape(B_, C_, H_ * W_).transpose(0, 2, 1)
    def _from_tokens(t, like):
        B_, C_, H_, W_ = like.shape
        return t.transpose(0, 2, 1).reshape(B_, C_, H_, W_)

    x = x + _L0_conv_ref(_gn(x), L0_conv_in_proj_w, L0_conv_conv_w, L0_conv_conv_b, L0_conv_x_proj_weight, L0_conv_dt_projs_weight, L0_conv_dt_projs_bias, L0_conv_A_logs, L0_conv_Ds, L0_conv_ln_w, L0_conv_ln_b, L0_conv_out_proj_w)
    x = x + _L1_conv_ref(_gn(x), L1_conv_conv1_w, L1_conv_conv1_b, L1_conv_norm1_w, L1_conv_norm1_b, L1_conv_norm_w, L1_conv_norm_b, L1_conv_proj_w, L1_conv_proj_b, L1_conv_skip_scale, L1_conv_in_proj_w, L1_conv_convd_w, L1_conv_convd_b, L1_conv_x_proj_w, L1_conv_dt_proj_w, L1_conv_dt_proj_b, L1_conv_A_log, L1_conv_D_param, L1_conv_out_proj_w)
    return x


_drawn_inputs = setup_inputs


def setup_inputs(seed=0):
    import zlib

    import numpy as np

    out = dict(_drawn_inputs(seed))
    spreads = {'L0_conv_conv_b': (0.0, 0.1),
     'L0_conv_Ds': (1.0, 0.2),
     'L0_conv_ln_w': (1.0, 0.2),
     'L0_conv_ln_b': (0.0, 0.1),
     'L1_conv_conv1_b': (0.0, 0.379),
     'L1_conv_norm1_w': (1.0, 0.2),
     'L1_conv_norm1_b': (0.0, 0.1),
     'L1_conv_norm_w': (1.0, 0.2),
     'L1_conv_norm_b': (0.0, 0.1),
     'L1_conv_proj_b': (0.0, 0.1),
     'L1_conv_convd_b': (0.0, 0.8),
     'L1_conv_D_param': (1.0, 0.6)}
    factors = {'L0_conv_dt_projs_weight': 5.45,
     'L0_conv_dt_projs_bias': 2.709,
     'L0_conv_A_logs': 4.765,
     'L1_conv_in_proj_w': 8.0,
     'L1_conv_convd_w': 8.0,
     'L1_conv_x_proj_w': 8.0,
     'L1_conv_dt_proj_w': 8.0,
     'L1_conv_dt_proj_b': 8.0,
     'L1_conv_A_log': 8.0,
     'L1_conv_out_proj_w': 8.0}
    for name, (base, spread) in spreads.items():
        noise = np.random.default_rng([zlib.crc32(name.encode()), seed]).standard_normal(out[name].shape)
        drawn = base * np.exp(spread * noise) if base else spread * noise
        out[name] = jnp.asarray(drawn.astype(out[name].dtype))
    for name, factor in factors.items():
        out[name] = (out[name] * factor).astype(out[name].dtype)
    return out
```

```python
from contextlib import ExitStack

import concourse.bass as bass
from concourse import mybir

ACT = mybir.ActivationFunctionType
ALU = mybir.AluOpType

B, CH, H, W = 8, 192, 64, 64
L = H * W
T = 512
NCHUNK = L // T
ROWS = T // W
HALF = CH // 2
GROUP_EPS = 1e-5
LN_EPS = 1e-5
N_STATE = 16
XROWS = 3 * 2 * N_STATE

D0, K0, R0 = 384, 4, 12
ND0 = D0 // 128
CB, D1, R1, NBR = 64, 128, 4, 3
TAPS = 9
DCONV = 4


def wait(eng, semaphore, value):
    if not (isinstance(value, int) and value <= 0):
        eng.wait_ge(semaphore, value)


def over_batches(eng, body):
    body(0)
    with eng.Fori(1, B - 1) as b:
        body(b)
    body(B - 1)


def is_last(b):
    return isinstance(b, int) and b == B - 1


STATS_STEPS, SCALE_STEPS = 4, 4


def group_stats(dve, b, x, stats, mv, packed, sq, steps, passed):
    done = b * STATS_STEPS
    for half in range(2):
        for c in range(NCHUNK):
            last = dve.bn_stats(stats[:, half, c, :], x[:, half, c * T:(c + 1) * T])
    last.then_inc(steps, 1)
    dve.wait_ge(steps, done + 1)
    dve.sem_inc(passed, 1)
    for half in range(2):
        last = dve.bn_aggr(mv[:, half, :], stats[:, half, :, :].rearrange("p c s -> p (c s)"))
    last.then_inc(steps, 1)
    dve.wait_ge(steps, done + 2)
    dve.tensor_copy(packed[:, 0:2], mv[:, :, 0])
    dve.tensor_tensor(sq[:, :], mv[:, :, 0], mv[:, :, 0], ALU.mult).then_inc(steps, 1)
    dve.wait_ge(steps, done + 3)
    dve.tensor_tensor(packed[:, 2:4], sq[:, :], mv[:, :, 1], ALU.add).then_inc(steps, 1)


def group_variance(dve, b, g_ps, gm, sq, var, steps):
    done = b * SCALE_STEPS
    dve.tensor_copy(gm[:, :], g_ps[:, :]).then_inc(steps, 1)
    dve.wait_ge(steps, done + 1)
    dve.tensor_tensor(sq[:, :], gm[:, 0:2], gm[:, 0:2], ALU.mult).then_inc(steps, 1)
    dve.wait_ge(steps, done + 2)
    dve.tensor_tensor(sq[:, :], gm[:, 2:4], sq[:, :], ALU.subtract).then_inc(steps, 1)
    dve.wait_ge(steps, done + 3)
    dve.tensor_scalar(var[:, :], sq[:, :], GROUP_EPS, None, ALU.add).then_inc(steps, 1)


def inverse_root(act, lnv, rstd, var, half_step, half_value):
    act.activation(lnv, var, ACT.Ln).then_inc(half_step, 1)
    act.wait_ge(half_step, half_value)
    return act.activation(rstd, lnv, ACT.Exp, scale=-0.5)


def layer0_features(nc, x, U, gmat_in, w_in_in, taps_in, conv_b_in, ident_in):
    fp32 = mybir.dt.float32
    Uv = U.rearrange("(b k c) p t j -> b k t p c j", b=B, k=K0)
    with ExitStack() as ctx:
        def sb(n, s, dt=fp32):
            return ctx.enter_context(nc.sbuf_tensor(f"f0_{n}", s, dt))

        def pb(n, s):
            return ctx.enter_context(nc.psum_tensor(f"f0_{n}", s, fp32))

        def sem(n):
            return ctx.enter_context(nc.semaphore(f"f0_{n}"))

        xin = sb("xin", [HALF, 2, L])
        pad = [sb(f"pad{t}", [128, H + 2, W + 2]) for t in range(ND0)]
        row = [sb(f"row{t}", [128, L]) for t in range(ND0)]
        col, row_rev, col_rev = sb("col", [128, L]), sb("row_rev", [128, L]), sb("col_rev", [128, L])
        gmat, w_in = sb("gmat", [HALF, HALF]), sb("w_in", [HALF, 2, D0])
        taps, conv_b, ident = sb("taps", [128, ND0, TAPS]), sb("conv_b", [128, ND0]), sb("ident", [128, 128])
        diag = sb("diag", [128, ND0 * TAPS, 128])
        stats, mv = sb("stats", [HALF, 2, NCHUNK, 6]), sb("mv", [HALF, 2, 2])
        packed, sq = sb("packed", [HALF, 4]), sb("sq", [HALF, 2])
        gm, sq2, var, lnv, rstd = (sb("gm", [HALF, 4]), sb("sq2", [HALF, 2]), sb("var", [HALF, 2]),
                                   sb("lnv", [HALF, 2]), sb("rstd", [HALF, 2]))
        in_ps = pb("in_ps", [128, 3, T])
        conv_ps = pb("conv_ps", [128, 4, T])
        g_ps = pb("g_ps", [HALF, 4])

        const_in, x_in, setup, passed = sem("const_in"), sem("x_in"), sem("setup"), sem("passed")
        stat_steps, g_done, scale_steps = sem("stat_steps"), sem("g_done"), sem("scale_steps")
        lnv_ready, rstd_ready, xn_ready = sem("lnv_ready"), sem("rstd_ready"), sem("xn_ready")
        in_done, pad_ready, conv_done, row_ready = sem("in_done"), sem("pad_ready"), sem("conv_done"), sem("row_ready")
        col_ready, rev_ready, col_rev_ready = sem("col_ready"), sem("rev_ready"), sem("col_rev_ready")
        stored = [sem(f"stored{k}") for k in range(ND0 + K0 - 1)]
        block = ctx.enter_context(nc.Block())

        def tile(b, t):
            return b * ND0 + t

        @block.sync
        def _(sp):
            sp.dma_start(gmat[:, :], gmat_in).then_inc(const_in, 16)
            sp.dma_start(w_in[:, :, :], w_in_in).then_inc(const_in, 16)
            sp.dma_start(taps[:, :, :], taps_in).then_inc(const_in, 16)
            sp.dma_start(conv_b[:, :], conv_b_in).then_inc(const_in, 16)
            sp.dma_start(ident[:, :], ident_in).then_inc(const_in, 16)
            sp.dma_start(xin[:, :, :], x[0]).then_inc(x_in, 16)

            def image(b):
                for t in range(ND0):
                    if t == 1 and not is_last(b):
                        sp.wait_ge(in_done, (b + 1) * ND0 * NCHUNK)
                        sp.dma_start(xin[:, :, :], x[b + 1]).then_inc(x_in, 16)
                    for k, src, ready, count in (
                            (0, row[t], row_ready, NCHUNK), (1, col, col_ready, 1),
                            (2, row_rev, rev_ready, 1), (3, col_rev, col_rev_ready, 1)):
                        sp.wait_ge(ready, (tile(b, t) + 1) * count)
                        done = stored[t] if k == 0 else stored[ND0 - 1 + k]
                        sp.dma_start(Uv[b, k, t], src[:, :].rearrange("p (c j) -> p c j", j=T)).then_inc(done, 16)

            over_batches(sp, image)
            for t in range(ND0):
                sp.wait_ge(stored[t], 16 * B)
            for k in range(1, K0):
                sp.wait_ge(stored[ND0 - 1 + k], 16 * B * ND0)

        @block.tensor
        def _(pe):
            pe.wait_ge(const_in, 80)
            pe.wait_ge(setup, 1 + ND0)

            def group_means(b):
                pe.wait_ge(stat_steps, (b + 1) * STATS_STEPS)
                pe.matmul(g_ps[:, :], gmat[:, :], packed[:, :], start=True, stop=True).then_inc(g_done, 1)

            def in_proj(b, t):
                for c in range(NCHUNK):
                    m = tile(b, t) * NCHUNK + c
                    bank = (t * NCHUNK + c) % 3
                    wait(pe, pad_ready, m - 2)
                    for half in range(2):
                        last = pe.matmul(in_ps[:, bank, :], w_in[:, half, t * 128:(t + 1) * 128],
                                         xin[:, half, c * T:(c + 1) * T], start=half == 0, stop=half == 1)
                    last.then_inc(in_done, 1)

            def conv(b, t):
                pe.wait_ge(pad_ready, (tile(b, t) + 1) * NCHUNK)
                for c in range(NCHUNK):
                    wait(pe, row_ready, tile(b, t) * NCHUNK + c - 3)
                    for k in range(TAPS):
                        dy, dx = divmod(k, 3)
                        last = pe.matmul(conv_ps[:, c % 4, :], diag[:, t * TAPS + k, :],
                                         pad[t][:, c * ROWS + dy:c * ROWS + dy + ROWS, dx:dx + W],
                                         start=k == 0, stop=k == TAPS - 1)
                    last.then_inc(conv_done, 1)

            def image(b):
                pe.wait_ge(xn_ready, b + 1)
                in_proj(b, 0)
                in_proj(b, 1)
                conv(b, 0)
                in_proj(b, 2)
                conv(b, 1)
                if not is_last(b):
                    group_means(b + 1)
                conv(b, 2)

            group_means(0)
            over_batches(pe, image)

        @block.scalar
        def _(act):
            act.wait_ge(const_in, 80)

            def scale(b):
                act.wait_ge(scale_steps, b * SCALE_STEPS + 4)
                inverse_root(act, lnv[:, :], rstd[:, :], var[:, :], lnv_ready, b + 1).then_inc(rstd_ready, 1)

            def take_in(b, t):
                for c in range(NCHUNK):
                    act.wait_ge(in_done, tile(b, t) * NCHUNK + c + 1)
                    act.activation(pad[t][:, 1 + c * ROWS:1 + (c + 1) * ROWS, 1:1 + W],
                                   in_ps[:, (t * NCHUNK + c) % 3, :].rearrange("p (r w) -> p r w", w=W),
                                   ACT.Copy).then_inc(pad_ready, 1)

            def take_conv(b, t):
                n = tile(b, t)
                wait(act, stored[t], b * 16)
                wait(act, col_ready, n - 2)
                wait(act, rev_ready, n - 2)
                for c in range(NCHUNK):
                    act.wait_ge(conv_done, n * NCHUNK + c + 1)
                    act.activation(row[t][:, c * T:(c + 1) * T], conv_ps[:, c % 4, :], ACT.Silu,
                                   bias=conv_b[:, t:t + 1]).then_inc(row_ready, 1)

            def image(b):
                take_in(b, 0)
                take_in(b, 1)
                take_conv(b, 0)
                take_in(b, 2)
                take_conv(b, 1)
                if not is_last(b):
                    scale(b + 1)
                take_conv(b, 2)

            act.wait_ge(setup, 1 + ND0)
            scale(0)
            over_batches(act, image)

        @block.vector
        def _(dve):
            dve.wait_ge(const_in, 80)
            for t in range(ND0):
                dve.memset(pad[t][:, :, :], 0.0).then_inc(setup, 1)
            for t in range(ND0):
                for k in range(TAPS):
                    last = dve.tensor_scalar(diag[:, t * TAPS + k, :], ident[:, :], taps[:, t, k:k + 1], None, ALU.mult)
            last.then_inc(setup, 1)

            def measure(b):
                dve.wait_ge(x_in, (b + 1) * 16)
                wait(dve, g_done, b)
                group_stats(dve, b, xin, stats, mv, packed, sq, stat_steps, passed)

            def normalise(b):
                dve.wait_ge(g_done, b + 1)
                group_variance(dve, b, g_ps, gm, sq2, var, scale_steps)
                dve.wait_ge(rstd_ready, b + 1)
                dve.wait_ge(scale_steps, b * SCALE_STEPS + 4)
                for half in range(2):
                    last = dve.tensor_scalar(xin[:, half, :], xin[:, half, :], gm[:, half:half + 1],
                                             rstd[:, half:half + 1], ALU.subtract, ALU.mult)
                last.then_inc(xn_ready, 1)

            def turn(b, t):
                n = tile(b, t)
                dve.wait_ge(row_ready, (n + 1) * NCHUNK)
                wait(dve, stored[ND0], n * 16)
                wait(dve, col_rev_ready, n)
                dve.tensor_copy(col[:, :].rearrange("p (w h) -> p w h", h=H),
                                row[t][:, :].rearrange("p (h w) -> p w h", w=W)).then_inc(col_ready, 1)

            def image(b):
                turn(b, 0)
                if not is_last(b):
                    measure(b + 1)
                turn(b, 1)
                if not is_last(b):
                    normalise(b + 1)
                turn(b, 2)

            measure(0)
            normalise(0)
            over_batches(dve, image)

        @block.gpsimd
        def _(pool):
            def image(b):
                for t in range(ND0):
                    n = tile(b, t)
                    pool.wait_ge(row_ready, (n + 1) * NCHUNK)
                    wait(pool, stored[ND0 + 1], n * 16)
                    pool.sem_inc(passed, 1)
                    pool.tensor_copy(row_rev[:, :], row[t][:, ::-1]).then_inc(rev_ready, 1)
                    pool.wait_ge(col_ready, n + 1)
                    wait(pool, stored[ND0 + 2], n * 16)
                    pool.sem_inc(passed, 1)
                    pool.tensor_copy(col_rev[:, :], col[:, ::-1]).then_inc(col_rev_ready, 1)

            over_batches(pool, image)


def scan_phase(nc, name, shape, U, Y, w_x, w_dt, w_small, keep, ident_in, sel_in):
    outer, K, nd, ng, rank = shape
    J, NS, NCH = nd * ng, N_STATE // ng, L // T
    seqs = outer * K
    units = seqs * NCH
    fp32, bf16 = mybir.dt.float32, mybir.dt.bfloat16
    SM = nd * (2 + N_STATE)
    LOADS = 5
    at = (dict(xproj=5, xd=6, rest1=6, mid=7, rest2=7, low=8, dt=7, act=8, soft=11, delta=12, du=12)
          if nd > 1 else
          dict(xproj=2, xd=2, rest1=3, mid=3, rest2=3, low=4, dt=3, act=4, soft=4, delta=5, du=5))

    with ExitStack() as ctx:
        def sb(n, s, dt=fp32):
            return ctx.enter_context(nc.sbuf_tensor(f"{name}_{n}", s, dt))

        def pb(n, s):
            return ctx.enter_context(nc.psum_tensor(f"{name}_{n}", s, fp32))

        def sem(n):
            return ctx.enter_context(nc.semaphore(f"{name}_{n}"))

        u = [sb(f"u{q}", [128, nd, T]) for q in range(2)]
        wx = [sb(f"wx{q}", [128, nd, XROWS + rank]) for q in range(2)]
        wdt = [sb(f"wdt{q}", [128, nd, 128]) for q in range(2)]
        small = [sb(f"small{q}", [128, SM]) for q in range(2)]
        keep_sb = [sb(f"keep{q}", [128, 1]) for q in range(2)]
        negA = [sb(f"negA{q}", [128, nd * N_STATE]) for q in range(2)]
        delta = [sb(f"delta{q}", [128, nd, T]) for q in range(2)]
        du = [sb(f"du{q}", [128, nd, T]) for q in range(2)]
        bc16 = [sb(f"bc16{q}", [96, T], bf16) for q in range(2)]
        yo = [sb(f"yo{q}", [128, nd, T]) for q in range(2)]
        xd = sb("xd", [XROWS + rank, T])
        rest1 = sb("rest1", [96, T])
        mid16 = sb("mid16", [96, T], bf16)
        rest2 = sb("rest2", [96, T])
        lnx = sb("lnx", [128, nd, T])
        relx = sb("relx", [128, nd, T])
        b_sb = sb("b_sb", [128, 2, ng, T])
        dbu = sb("dbu", [128, 2, J, T])
        h = sb("h", [128, 2, J, T])
        hc = sb("hc", [128, 2, J, T])
        state = sb("state", [128, NS, J])
        ident = sb("ident", [128, 128])
        self32 = sb("self32", [96, 2 * N_STATE * 128])
        sel = sb("sel", [96, 2 * N_STATE, 128], bf16)

        dA_ps = pb("dA_ps", [128, 2, T])
        c_ps = pb("c_ps", [128, ng, T])
        b_ps = pb("b_ps", [128, ng, T])
        y_ps = pb("y_ps", [128, nd, T])
        prep_ps = pb("prep_ps", [128, T])

        const_in, sel_ready = sem("const_in"), sem("sel_ready")
        loaded = [sem(f"loaded{q}") for q in range(2)]
        stored = [sem(f"stored{q}") for q in range(2)]
        xproj_done, xd_ready, dt_done, prep_read = sem("xproj_done"), sem("xd_ready"), sem("dt_done"), sem("prep_read")
        rests, mid_ready, bc_ready = sem("rests"), sem("mid_ready"), sem("bc_ready")
        negA_ready, abs_done, soft_done, delta_ready, du_ready = (
            sem("negA_ready"), sem("abs_done"), sem("soft_done"), sem("delta_ready"), sem("du_ready"))
        b_done, b_copied, c_done = sem("b_done"), sem("b_copied"), sem("c_done")
        dA_ready, dbu_ready, scanned, hc_ready, summed = (
            sem("dA_ready"), sem("dbu_ready"), sem("scanned"), sem("hc_ready"), sem("summed"))
        state_saved, evacuated = sem("state_saved"), sem("evacuated")

        def bias_of(q, t):
            return small[q][:, t:t + 1]

        def D_of(q, t):
            return small[q][:, nd + t:nd + t + 1]

        def over_units(eng, unit):
            unit(0, 0, True)
            unit(1, 1, False)
            with eng.Fori(1, units // 2) as i:
                unit(i * 2, 0, False)
                unit(i * 2 + 1, 1, False)

        block = ctx.enter_context(nc.Block())

        @block.sync
        def _(eng):
            eng.dma_start(ident[:, :], ident_in).then_inc(const_in, 16)
            eng.dma_start(self32[:, :], sel_in).then_inc(const_in, 16)

            def load(g, k, c, q):
                eng.wait_ge(evacuated, g + 1)
                eng.dma_start(u[q][:, :, :], U[g]).then_inc(loaded[q], 16)
                eng.dma_start(wx[q][:, :, :], w_x[k]).then_inc(loaded[q], 16)
                eng.dma_start(wdt[q][XROWS:XROWS + rank, :, :], w_dt[k]).then_inc(loaded[q], 16)
                eng.dma_start(small[q][:, :], w_small[k]).then_inc(loaded[q], 16)
                eng.dma_start(keep_sb[q][:, :], keep[c]).then_inc(loaded[q], 16)

            with eng.Fori(0, outer) as o:
                with eng.Fori(0, K) as k:
                    with eng.Fori(0, NCH // 2) as c2:
                        for q in range(2):
                            load((o * K + k) * NCH + c2 * 2 + q, k, c2 * 2 + q, q)
            eng.wait_ge(evacuated, units + 1)
            eng.dma_start(u[0][:, :, :], U[0]).then_inc(loaded[0], 16)
            eng.dma_start(wx[0][:, :, :], w_x[0]).then_inc(loaded[0], 16)
            eng.dma_start(wdt[0][XROWS:XROWS + rank, :, :], w_dt[0]).then_inc(loaded[0], 16)
            eng.dma_start(small[0][:, :], w_small[0]).then_inc(loaded[0], 16)
            eng.dma_start(keep_sb[0][:, :], keep[0]).then_inc(loaded[0], 16)
            for q in range(2):
                eng.wait_ge(stored[q], 16 * (units // 2))

        def loads_of(g, q):
            half = g // 2 if isinstance(g, int) else (g - q) // 2
            return 16 * LOADS * (half + 1) if isinstance(half, int) else half * (16 * LOADS) + 16 * LOADS

        @block.tensor
        def _(pe):
            def xproj(g, q, lw):
                pe.wait_ge(loaded[q], lw)
                wait(pe, prep_read, g * (1 + nd))
                for t in range(nd):
                    last = pe.matmul(prep_ps[0:XROWS + rank, :], wx[q][:, t, :], u[q][:, t, :],
                                     start=t == 0, stop=t == nd - 1)
                last.then_inc(xproj_done, 1)

            def dt(g, q, t):
                pe.wait_ge(xd_ready, g + 1)
                pe.wait_ge(prep_read, g * (1 + nd) + 1 + t)
                pe.matmul(prep_ps[:, :], wdt[q][XROWS:XROWS + rank, t, :], xd[XROWS:XROWS + rank, :],
                          start=True, stop=True).then_inc(dt_done, 1)

            def b_broadcast(g, q, s):
                n = g * NS + s
                if s == 0:
                    pe.wait_ge(bc_ready, g * 2 + 2)
                wait(pe, b_copied, n)
                for r in range(ng):
                    last = pe.matmul(b_ps[:, r, :], sel[:, s * ng + r, :], bc16[q][:, :], start=True, stop=True)
                last.then_inc(b_done, 1)

            def c_broadcast(g, q, s):
                n = g * NS + s
                wait(pe, hc_ready, n)
                for r in range(ng):
                    last = pe.matmul(c_ps[:, r, :], sel[:, N_STATE + s * ng + r, :], bc16[q][:, :],
                                     start=True, stop=True)
                last.then_inc(c_done, 1)

            def state_sum(g, s):
                n = g * NS + s
                pe.wait_ge(hc_ready, n + 1)
                if s == 0:
                    pe.wait_ge(evacuated, g + 2)
                for j in range(J):
                    r, t = divmod(j, nd)
                    last = pe.matmul(y_ps[:, t, :], ident[:, :], hc[:, s % 2, j, :],
                                     start=s == 0 and r == 0, stop=s == NS - 1 and r == ng - 1)
                last.then_inc(summed, 1)

            def unit(g, q, first):
                o = 1 - q
                for s in range(NS):
                    c_broadcast(g, q, s)
                    if s:
                        state_sum(g, s - 1)
                    elif not first:
                        state_sum(g - 1, NS - 1)
                    if s + 2 < NS:
                        b_broadcast(g, q, s + 2)
                    else:
                        b_broadcast(g + 1, o, s + 2 - NS)
                    if s == at["xproj"]:
                        xproj(g + 1, o, loads_of(g + 1, o))
                    if 0 <= s - at["dt"] < nd:
                        dt(g + 1, o, s - at["dt"])

            pe.wait_ge(const_in, 32)
            pe.wait_ge(sel_ready, 1)
            xproj(0, 0, 16 * LOADS)
            for t in range(nd):
                dt(0, 0, t)
            b_broadcast(0, 0, 0)
            b_broadcast(0, 0, 1)
            over_units(pe, unit)
            state_sum(units - 1, NS - 1)

        @block.scalar
        def _(act):
            act.preload_act_table_set("natural_log_exp_and_others")

            def take_xproj(g, q, lw):
                act.wait_ge(loaded[q], lw)
                act.activation(negA[q][:, :], small[q][:, 2 * nd:], ACT.Exp).then_inc(negA_ready, 1)
                act.wait_ge(negA_ready, g * 2 + 1)
                act.activation(negA[q][:, :], negA[q][:, :], ACT.Copy, scale=-1.0).then_inc(negA_ready, 1)
                act.wait_ge(xproj_done, g + 1)
                act.activation(xd[:, :], prep_ps[0:XROWS + rank, :], ACT.Copy).then_inc(xd_ready, 1)
                act.activation(bc16[q][:, :], prep_ps[0:96, :], ACT.Copy).then_inc(prep_read, 1)

            def take_mid(g, q):
                act.wait_ge(rests, g * 2 + 1)
                act.activation(mid16[:, :], rest1[:, :], ACT.Copy).then_inc(mid_ready, 1)
                act.wait_ge(mid_ready, g + 1)
                act.activation(bc16[q][32:64, :], mid16[32:64, :], ACT.Copy).then_inc(bc_ready, 1)

            def take_low(g, q):
                act.wait_ge(rests, g * 2 + 2)
                act.activation(bc16[q][64:96, :], rest2[64:96, :], ACT.Copy).then_inc(bc_ready, 1)

            def take_dt(g, q, t):
                act.wait_ge(dt_done, g * nd + t + 1)
                wait(act, delta_ready, g)
                act.activation(lnx[:, t, :], prep_ps[:, :], ACT.Abs, bias=bias_of(q, t)).then_inc(abs_done, 1)
                act.activation(relx[:, t, :], prep_ps[:, :], ACT.Relu, bias=bias_of(q, t)).then_inc(prep_read, 1)

            def softplus_log(g):
                act.wait_ge(abs_done, g * (nd + 1) + nd)
                act.activation(lnx[:, :, :], lnx[:, :, :], ACT.Exp, scale=-1.0).then_inc(abs_done, 1)
                act.wait_ge(abs_done, (g + 1) * (nd + 1))
                act.activation(lnx[:, :, :], lnx[:, :, :], ACT.Ln, bias=1.0).then_inc(soft_done, 1)

            def copy_b(g, s):
                n = g * NS + s
                act.wait_ge(b_done, n + 1)
                wait(act, dbu_ready, n - 1)
                act.activation(b_sb[:, s % 2, :, :], b_ps[:, :, :], ACT.Copy).then_inc(b_copied, 1)

            def decay(g, q, s, j):
                r, t = divmod(j, nd)
                n = (g * NS + s) * J + j
                if s == 0 and j == 0:
                    act.wait_ge(delta_ready, g + 1)
                    act.wait_ge(negA_ready, g * 2 + 2)
                wait(act, scanned, n - 1)
                a = t * N_STATE + s * ng + r
                act.activation(dA_ps[:, (s * J + j) % 2, :], delta[q][:, t, :], ACT.Exp,
                               scale=negA[q][:, a:a + 1]).then_inc(dA_ready, 1)

            def save_state(g, q, s):
                n = g * NS + s
                act.wait_ge(scanned, (n + 1) * J)
                act.activation(state[:, s, :], h[:, s % 2, :, T - 1], ACT.Copy,
                               scale=keep_sb[q][:, 0:1]).then_inc(state_saved, 1)

            def store(g, q):
                act.wait_ge(evacuated, g + 3)
                act.dma_start(Y[g], yo[q][:, :, :]).then_inc(stored[q], 16)

            def unit(g, q, first):
                o = 1 - q
                for s in range(NS):
                    for j in range(J):
                        decay(g, q, s, j)
                    if s + 2 < NS:
                        copy_b(g, s + 2)
                    else:
                        copy_b(g + 1, s + 2 - NS)
                    if s:
                        save_state(g, q, s - 1)
                    elif not first:
                        save_state(g - 1, o, NS - 1)
                    if s == 1 and not first:
                        store(g - 1, o)
                    if s == at["xd"]:
                        take_xproj(g + 1, o, loads_of(g + 1, o))
                    if s == at["mid"]:
                        take_mid(g + 1, o)
                    if s == at["low"]:
                        take_low(g + 1, o)
                    if 0 <= s - at["act"] < nd:
                        take_dt(g + 1, o, s - at["act"])
                    if s == at["soft"]:
                        softplus_log(g + 1)

            take_xproj(0, 0, 16 * LOADS)
            take_mid(0, 0)
            take_low(0, 0)
            for t in range(nd):
                take_dt(0, 0, t)
            softplus_log(0)
            copy_b(0, 0)
            copy_b(0, 1)
            over_units(act, unit)
            save_state(units - 1, 1, NS - 1)
            store(units - 1, 1)

        @block.gpsimd
        def _(pool):
            def input_of(g, q, s):
                n = g * NS + s
                pool.wait_ge(b_copied, n + 1)
                if s == 0:
                    pool.wait_ge(du_ready, g + 1)
                wait(pool, scanned, (n - 1) * J)
                a, b = du[q][:, :, :], b_sb[:, s % 2, :, :]
                a, b = (a, b.broadcast_to([128, nd, T])) if ng == 1 else (a.broadcast_to([128, ng, T]), b)
                pool.tensor_tensor(dbu[:, s % 2, :, :], a, b, ALU.mult).then_inc(dbu_ready, 1)

            def unit(g, q, first):
                for s in range(1, NS):
                    input_of(g, q, s)
                input_of(g + 1, 1 - q, 0)

            input_of(0, 0, 0)
            over_units(pool, unit)

        @block.vector
        def _(dve):
            dve.sem_inc(evacuated, 2)
            dve.wait_ge(const_in, 32)
            dve.tensor_copy(sel[:, :, :].rearrange("p a b -> p (a b)"), self32[:, :]).then_inc(sel_ready, 1)

            def take_rest1(g, q):
                dve.wait_ge(prep_read, g * (1 + nd) + 1)
                dve.wait_ge(xd_ready, g + 1)
                dve.tensor_tensor(rest1[:, :], xd[0:96, :], bc16[q][:, :], ALU.subtract).then_inc(rests, 1)

            def take_rest2(g):
                dve.wait_ge(mid_ready, g + 1)
                dve.wait_ge(rests, g * 2 + 1)
                dve.tensor_tensor(rest2[:, :], rest1[:, :], mid16[:, :], ALU.subtract).then_inc(rests, 1)

            def take_delta(g, q):
                dve.wait_ge(soft_done, g + 1)
                dve.wait_ge(prep_read, (g + 1) * (1 + nd))
                dve.tensor_tensor(delta[q][:, :, :], relx[:, :, :], lnx[:, :, :], ALU.add).then_inc(delta_ready, 1)

            def take_du(g, q):
                dve.wait_ge(delta_ready, g + 1)
                dve.tensor_tensor(du[q][:, :, :], delta[q][:, :, :], u[q][:, :, :], ALU.mult).then_inc(du_ready, 1)

            def scan(g, q, s, j, initial):
                n = g * NS + s
                if j == 0:
                    dve.wait_ge(dbu_ready, n + 1)
                    wait(dve, hc_ready, n - 1)
                    wait(dve, state_saved, n - 1)
                dve.wait_ge(dA_ready, n * J + j + 1)
                dve.tensor_tensor_scan(h[:, s % 2, j, :], dA_ps[:, (s * J + j) % 2, :], dbu[:, s % 2, j, :],
                                       initial, ALU.mult, ALU.add).then_inc(scanned, 1)

            def times_c(g, s):
                n = g * NS + s
                dve.wait_ge(scanned, (n + 1) * J)
                dve.wait_ge(c_done, n + 1)
                wait(dve, summed, n - 1)
                c = c_ps[:, :, :]
                if ng == 1:
                    c = c.broadcast_to([128, nd, T])
                dve.tensor_tensor(hc[:, s % 2, :, :], h[:, s % 2, :, :], c, ALU.mult).then_inc(hc_ready, 1)

            def evacuate(g, q, i):
                dve.wait_ge(state_saved, (g + 1) * NS)
                dve.wait_ge(summed, (g + 1) * NS)
                wait(dve, stored[q], i)
                for t in range(nd):
                    last = dve.scalar_tensor_tensor(yo[q][:, t, :], u[q][:, t, :], D_of(q, t), y_ps[:, t, :],
                                                    ALU.mult, ALU.add)
                last.then_inc(evacuated, 1)

            def earlier_stores(g, q):
                return 16 * (g // 2) if isinstance(g, int) else (g - q) * 8

            def unit(g, q, first):
                o = 1 - q
                for s in range(NS):
                    for j in range(J):
                        scan(g, q, s, j, 0.0 if first else state[:, s, j:j + 1])
                    times_c(g, s)
                    if s == 0 and not first:
                        evacuate(g - 1, o, earlier_stores(g - 1, o))
                    if s == at["rest1"]:
                        take_rest1(g + 1, o)
                    if s == at["rest2"]:
                        take_rest2(g + 1)
                    if s == at["delta"]:
                        take_delta(g + 1, o)
                    if s == at["du"]:
                        take_du(g + 1, o)

            take_rest1(0, 0)
            take_rest2(0)
            take_delta(0, 0)
            take_du(0, 0)
            over_units(dve, unit)
            evacuate(units - 1, 1, earlier_stores(units - 1, 1))


def layer0_output(nc, Y, x, x1, ln_in, ln_w_in, ln_b_in, w_out_in):
    fp32 = mybir.dt.float32
    Yv = Y.rearrange("(b k c) p t j -> b k t p c j", b=B, k=K0)
    with ExitStack() as ctx:
        def sb(n, s, dt=fp32):
            return ctx.enter_context(nc.sbuf_tensor(f"m0_{n}", s, dt))

        def pb(n, s):
            return ctx.enter_context(nc.psum_tensor(f"m0_{n}", s, fp32))

        def sem(n):
            return ctx.enter_context(nc.semaphore(f"m0_{n}"))

        yk = [sb(f"y{k}", [128, L]) for k in range(K0)]
        ysum = sb("ysum", [128, ND0, L])
        xin = sb("xin", [HALF, 2, L])
        cen, sq = sb("cen", [128, 2, ND0, T]), sb("sq", [128, ND0, T])
        yn = sb("yn", [128, ND0, T])
        lnv, rstd = sb("lnv", [128, T]), sb("rstd", [128, T])
        res = sb("res", [HALF, 2, 2, T])
        ones, w_out = sb("ones", [128, 128]), sb("w_out", [128, ND0, CH])
        ln_w, ln_b, eps = sb("ln_w", [128, ND0]), sb("ln_b", [128, ND0]), sb("eps", [128, 1])
        mean_ps, var_ps, out_ps = pb("mean_ps", [128, 2, T]), pb("var_ps", [128, 2, T]), pb("out_ps", [HALF, 2, 2, T])

        const_in, x_in, passed = sem("const_in"), sem("x_in"), sem("passed")
        y_in = [sem(f"y_in{k}") for k in range(K0)]
        rows_added, cols_added, sum_ready = sem("rows_added"), sem("cols_added"), sem("sum_ready")
        mean_done, cen_ready, sq_ready, var_done = sem("mean_done"), sem("cen_ready"), sem("sq_ready"), sem("var_done")
        lnv_ready, rstd_ready, scaled = sem("lnv_ready"), sem("rstd_ready"), sem("scaled")
        yn_ready, out_done, res_ready, eps_set = sem("yn_ready"), sem("out_done"), sem("res_ready"), sem("eps_set")
        stored = [sem(f"stored{p}") for p in range(2)]
        block = ctx.enter_context(nc.Block())

        @block.sync
        def _(sp):
            for dst, src in ((ones[:, :], ln_in), (w_out[:, :, :], w_out_in), (ln_w[:, :], ln_w_in), (ln_b[:, :], ln_b_in)):
                sp.dma_start(dst, src).then_inc(const_in, 16)

            def image(b):
                for t in range(ND0):
                    n = b * ND0 + t
                    for k in (1, 3, 0, 2):
                        wait(sp, sum_ready if k < 2 else rows_added if k == 2 else cols_added, n)
                        sp.sem_inc(passed, 1)
                        sp.dma_start(yk[k][:, :].rearrange("p (c j) -> p c j", j=T), Yv[b, k, t]).then_inc(y_in[k], 16)
                    if t == 0:
                        wait(sp, res_ready, b * NCHUNK)
                        sp.dma_start(xin[:, :, :], x[b]).then_inc(x_in, 16)

            over_batches(sp, image)
            for p in range(2):
                sp.wait_ge(stored[p], 16 * B * NCHUNK // 2)

        def lagged(body, lag):
            for c in range(NCHUNK + lag):
                body(c)

        @block.tensor
        def _(pe):
            pe.wait_ge(const_in, 64)

            def mean(b, c):
                m = b * NCHUNK + c
                wait(pe, cen_ready, m - 1)
                for t in range(ND0):
                    last = pe.matmul(mean_ps[:, c % 2, :], ones[:, :], ysum[:, t, c * T:(c + 1) * T],
                                     start=t == 0, stop=t == ND0 - 1)
                last.then_inc(mean_done, 1)

            def variance(b, c):
                m = b * NCHUNK + c
                pe.wait_ge(sq_ready, m + 1)
                wait(pe, rstd_ready, m - 1)
                for t in range(ND0):
                    last = pe.matmul(var_ps[:, c % 2, :], ones[:, :], sq[:, t, :], start=t == 0, stop=t == ND0 - 1)
                last.then_inc(var_done, 1)

            def project(b, c):
                m = b * NCHUNK + c
                pe.wait_ge(yn_ready, m + 1)
                wait(pe, res_ready, m - 1)
                for half in range(2):
                    for t in range(ND0):
                        last = pe.matmul(out_ps[:, c % 2, half, :], w_out[:, t, half * HALF:(half + 1) * HALF],
                                         yn[:, t, :], start=t == 0, stop=t == ND0 - 1)
                last.then_inc(out_done, 1)

            def image(b):
                pe.wait_ge(sum_ready, (b + 1) * ND0)
                for c in range(NCHUNK + 2):
                    if c < NCHUNK:
                        mean(b, c)
                    if 1 <= c <= NCHUNK:
                        variance(b, c - 1)
                    if c >= 2:
                        project(b, c - 2)

            over_batches(pe, image)

        @block.scalar
        def _(act):
            act.wait_ge(const_in, 64)
            act.wait_ge(eps_set, 1)

            def squares(b, c):
                m = b * NCHUNK + c
                act.wait_ge(cen_ready, m + 1)
                wait(act, var_done, m)
                act.activation(sq[:, :, :], cen[:, c % 2, :, :], ACT.Square).then_inc(sq_ready, 1)

            def root(b, c):
                m = b * NCHUNK + c
                act.wait_ge(var_done, m + 1)
                act.activation(lnv[:, :], var_ps[:, c % 2, :], ACT.Ln, bias=eps[:, :]).then_inc(lnv_ready, 1)
                act.wait_ge(lnv_ready, m + 1)
                wait(act, scaled, m)
                act.activation(rstd[:, :], lnv[:, :], ACT.Exp, scale=-0.5).then_inc(rstd_ready, 1)

            def affine(b, c):
                m = b * NCHUNK + c
                act.wait_ge(scaled, m + 1)
                wait(act, out_done, m)
                for t in range(ND0):
                    last = act.activation(yn[:, t, :], cen[:, c % 2, t, :], ACT.Identity,
                                          scale=ln_w[:, t:t + 1], bias=ln_b[:, t:t + 1])
                last.then_inc(yn_ready, 1)

            def store(b, c):
                m = b * NCHUNK + c
                act.wait_ge(res_ready, m + 1)
                act.dma_start(x1[b][:, :, c * T:(c + 1) * T], res[:, c % 2, :, :]).then_inc(stored[c % 2], 16)

            def image(b):
                for c in range(NCHUNK + 3):
                    if c < NCHUNK:
                        squares(b, c)
                    if 1 <= c <= NCHUNK:
                        root(b, c - 1)
                        affine(b, c - 1)
                    if c >= 3:
                        store(b, c - 3)

            over_batches(act, image)

        @block.vector
        def _(dve):
            dve.memset(eps[:, :], LN_EPS).then_inc(eps_set, 1)

            def add_rows(b, t):
                n = b * ND0 + t
                dve.wait_ge(y_in[0], (n + 1) * 16)
                dve.wait_ge(y_in[2], (n + 1) * 16)
                dve.tensor_tensor(yk[0][:, :], yk[0][:, :], yk[2][:, ::-1], ALU.add).then_inc(rows_added, 1)

            def add_columns(b, t):
                n = b * ND0 + t
                dve.wait_ge(rows_added, n + 1)
                dve.wait_ge(cols_added, n + 1)
                wait(dve, cen_ready, b * NCHUNK)
                dve.tensor_tensor(ysum[:, t, :].rearrange("p (h w) -> p h w", w=W),
                                  yk[0][:, :].rearrange("p (h w) -> p h w", w=W),
                                  yk[1][:, :].rearrange("p (w h) -> p h w", h=H), ALU.add).then_inc(sum_ready, 1)

            def centre(b, c):
                m = b * NCHUNK + c
                dve.wait_ge(mean_done, m + 1)
                wait(dve, yn_ready, m - 1)
                dve.tensor_tensor(cen[:, c % 2, :, :], ysum[:, :, c * T:(c + 1) * T],
                                  mean_ps[:, c % 2, :].unsqueeze(1).broadcast_to([128, ND0, T]),
                                  ALU.subtract).then_inc(cen_ready, 1)

            def scale(b, c):
                m = b * NCHUNK + c
                dve.wait_ge(rstd_ready, m + 1)
                dve.wait_ge(sq_ready, m + 1)
                dve.wait_ge(cen_ready, m + 1)
                dve.tensor_tensor(cen[:, c % 2, :, :], cen[:, c % 2, :, :],
                                  rstd[:, :].unsqueeze(1).broadcast_to([128, ND0, T]), ALU.mult).then_inc(scaled, 1)

            def residual(b, c):
                m = b * NCHUNK + c
                dve.wait_ge(out_done, m + 1)
                wait(dve, stored[c % 2], b * (16 * NCHUNK // 2) + (c // 2) * 16)
                dve.tensor_tensor(res[:, c % 2, :, :], out_ps[:, c % 2, :, :], xin[:, :, c * T:(c + 1) * T],
                                  ALU.add).then_inc(res_ready, 1)

            def image(b):
                for t in range(ND0):
                    add_rows(b, t)
                    add_columns(b, t)
                dve.wait_ge(x_in, (b + 1) * 16)
                for c in range(NCHUNK + 2):
                    if c < NCHUNK:
                        centre(b, c)
                    if 1 <= c <= NCHUNK:
                        scale(b, c - 1)
                    if c >= 2:
                        residual(b, c - 2)

            over_batches(dve, image)

        @block.gpsimd
        def _(pool):
            def image(b):
                for t in range(ND0):
                    n = b * ND0 + t
                    pool.wait_ge(y_in[1], (n + 1) * 16)
                    pool.wait_ge(y_in[3], (n + 1) * 16)
                    pool.tensor_tensor(yk[1][:, :], yk[1][:, :], yk[3][:, ::-1], ALU.add).then_inc(cols_added, 1)

            over_batches(pool, image)


def layer1_features(nc, x1, U, Z, XN, gmat_in, w_pair_in, w_third_in, conv_b_in, ones_in, ln_w_in, ln_b_in,
                    w_in_in, w_conv_in, conv1d_b_in):
    fp32 = mybir.dt.float32
    Uv = U.rearrange("(b r c) p o j -> b r p (o c) j", b=B, r=NBR)
    Zv = Z.rearrange("(b r c) p o j -> b r p (o c) j", b=B, r=NBR)
    with ExitStack() as ctx:
        def sb(n, s, dt=fp32):
            return ctx.enter_context(nc.sbuf_tensor(f"f1_{n}", s, dt))

        def pb(n, s):
            return ctx.enter_context(nc.psum_tensor(f"f1_{n}", s, fp32))

        def sem(n):
            return ctx.enter_context(nc.semaphore(f"f1_{n}"))

        xin = sb("xin", [HALF, 2, L])
        pad = sb("pad", [HALF, 2, H + 2, W + 2])
        seq = sb("seq", [128, 2, 2, T])
        cen = sb("cen", [128, 2, 2, T])
        sq_sb = sb("sq_sb", [128, 2, T])
        lnr, rstd_sb = sb("lnr", [128, 2, T]), sb("rstd_sb", [128, 2, T])
        xn = sb("xn", [128, 2, DCONV - 1 + L])
        u_sb, z_sb = sb("u_sb", [128, 2, L // 2]), sb("z_sb", [128, 2, L // 2])
        gmat, ones = sb("gmat", [HALF, HALF]), sb("ones", [128, 128])
        w_pair, w_third = sb("w_pair", [HALF, 2, TAPS, 2 * CB]), sb("w_third", [HALF, 2, TAPS, CB])
        w_in, w_conv = sb("w_in", [128, 2 * D1]), sb("w_conv", [128, DCONV, D1])
        w_fold = sb("w_fold", [128, DCONV, D1])
        conv_b, conv1d_b = sb("conv_b", [128, 1]), sb("conv1d_b", [128, 1])
        ln_w, ln_b, eps = sb("ln_w", [128, 2]), sb("ln_b", [128, 2]), sb("eps", [128, 1])
        stats, mv = sb("stats", [HALF, 2, NCHUNK, 6]), sb("mv", [HALF, 2, 2])
        packed, sq = sb("packed", [HALF, 4]), sb("sq", [HALF, 2])
        gm, sq2, var, lnv, rstd = (sb("gm", [HALF, 4]), sb("sq2", [HALF, 2]), sb("var", [HALF, 2]),
                                   sb("lnv", [HALF, 2]), sb("rstd", [HALF, 2]))
        conv_ps = pb("conv_ps", [128, 2, T])
        stat_ps = pb("stat_ps", [128, 2, T])
        proj_ps = pb("proj_ps", [128, 3, T])
        g_ps = pb("g_ps", [HALF, 4])

        const_in, x_in, setup, passed = sem("const_in"), sem("x_in"), sem("setup"), sem("passed")
        stat_steps, g_done, scale_steps = sem("stat_steps"), sem("g_done"), sem("scale_steps")
        lnv_ready, rstd_ready, pad_ready = sem("lnv_ready"), sem("rstd_ready"), sem("pad_ready")
        conv_done, seq_ready, mean_done, cen_ready = sem("conv_done"), sem("seq_ready"), sem("mean_done"), sem("cen_ready")
        sq_ready, var_done, lnr_ready, root_ready = sem("sq_ready"), sem("var_done"), sem("lnr_ready"), sem("root_ready")
        scaled, xn_ready = sem("scaled"), sem("xn_ready")
        proj_done, proj_read = sem("proj_done"), sem("proj_read")
        xn_stored = sem("xn_stored")
        u_stored = [sem(f"u_stored{p}") for p in range(2)]
        z_stored = [sem(f"z_stored{p}") for p in range(2)]
        block = ctx.enter_context(nc.Block())
        PARTS = 2 * NBR
        PC = NCHUNK // 2

        def over_parts(body):
            for r in range(NBR):
                for hf in range(2):
                    body(r, hf)

        @block.sync
        def _(sp):
            for dst, src in ((gmat[:, :], gmat_in), (ones[:, :], ones_in), (w_pair[:, :, :, :], w_pair_in),
                             (w_third[:, :, :, :], w_third_in), (w_in[:, :], w_in_in), (w_conv[:, :, :], w_conv_in),
                             (conv_b[:, :], conv_b_in), (conv1d_b[:, :], conv1d_b_in), (ln_w[:, :], ln_w_in),
                             (ln_b[:, :], ln_b_in)):
                sp.dma_start(dst, src).then_inc(const_in, 16)
            sp.dma_start(xin[:, :, :], x1[0]).then_inc(x_in, 16)

            def image(b):
                if not is_last(b):
                    sp.wait_ge(pad_ready, b + 1)
                    sp.dma_start(xin[:, :, :], x1[b + 1]).then_inc(x_in, 16)
                sp.wait_ge(xn_ready, (b + 1) * NCHUNK)
                sp.dma_start(XN[b], xn[:, :, DCONV - 1:]).then_inc(xn_stored, 16)

                def part(r, hf):
                    i = r * 2 + hf
                    sp.wait_ge(proj_read, ((b * PARTS) + i + 1) * 2 * PC)
                    sp.dma_start(Uv[b, r][:, hf * PC:(hf + 1) * PC, :],
                                 u_sb[:, i % 2, :].rearrange("p (c j) -> p c j", j=T)).then_inc(u_stored[i % 2], 16)
                    sp.dma_start(Zv[b, r][:, hf * PC:(hf + 1) * PC, :],
                                 z_sb[:, i % 2, :].rearrange("p (c j) -> p c j", j=T)).then_inc(z_stored[i % 2], 16)

                over_parts(part)

            over_batches(sp, image)
            sp.wait_ge(xn_stored, 16 * B)
            for p in range(2):
                sp.wait_ge(u_stored[p], 16 * B * PARTS // 2)
                sp.wait_ge(z_stored[p], 16 * B * PARTS // 2)

        @block.tensor
        def _(pe):
            pe.wait_ge(const_in, 160)
            pe.wait_ge(setup, 5)

            def group_means(b):
                pe.wait_ge(stat_steps, (b + 1) * STATS_STEPS)
                pe.matmul(g_ps[:, :], gmat[:, :], packed[:, :], start=True, stop=True).then_inc(g_done, 1)

            def conv(b, c):
                m = b * NCHUNK + c
                wait(pe, seq_ready, m)
                for w, slot, rows in ((w_pair, 0, 2 * CB), (w_third, 1, CB)):
                    for half in range(2):
                        for k in range(TAPS):
                            dy, dx = divmod(k, 3)
                            last = pe.matmul(conv_ps[0:rows, slot, :], w[:, half, k, :],
                                             pad[:, half, c * ROWS + dy:c * ROWS + dy + ROWS, dx:dx + W],
                                             start=half == 0 and k == 0, stop=half == 1 and k == TAPS - 1)
                last.then_inc(conv_done, 1)

            def mean(b, c):
                m = b * NCHUNK + c
                pe.wait_ge(seq_ready, m + 1)
                wait(pe, lnr_ready, m)
                for slot in range(2):
                    last = pe.matmul(stat_ps[:, slot, :], ones[:, :], seq[:, c % 2, slot, :], start=True, stop=True)
                last.then_inc(mean_done, 1)

            def variance(b, c):
                m = b * NCHUNK + c
                pe.wait_ge(sq_ready, m + 1)
                for slot in range(2):
                    last = pe.matmul(stat_ps[:, slot, :], ones[:, :], sq_sb[:, slot, :], start=True, stop=True)
                last.then_inc(var_done, 1)

            def project(b, r, hf):
                lo, slot = (CB if r == 1 else 0), (1 if r == 2 else 0)
                for c in range(PC):
                    m = (b * PARTS + r * 2 + hf) * 2 * PC + 2 * c
                    first = (hf * PC + c) * T
                    wait(pe, proj_read, m - 2)
                    bank = ((r * 2 + hf) * 2 * PC + 2 * c) % 3
                    for k in range(DCONV):
                        last = pe.matmul(proj_ps[:, bank, :], w_fold[lo:lo + CB, k, :],
                                         xn[lo:lo + CB, slot, first + k:first + k + T],
                                         start=k == 0, stop=k == DCONV - 1)
                    last.then_inc(proj_done, 1)
                    wait(pe, proj_read, m - 1)
                    bank = ((r * 2 + hf) * 2 * PC + 2 * c + 1) % 3
                    first += DCONV - 1
                    pe.matmul(proj_ps[:, bank, :], w_in[lo:lo + CB, D1:], xn[lo:lo + CB, slot, first:first + T],
                              start=True, stop=True).then_inc(proj_done, 1)

            def image(b):
                pe.wait_ge(pad_ready, b + 1)
                for c in range(NCHUNK + 1):
                    if c < NCHUNK:
                        conv(b, c)
                    if c >= 1:
                        mean(b, c - 1)
                        variance(b, c - 1)
                if not is_last(b):
                    group_means(b + 1)
                pe.wait_ge(xn_ready, (b + 1) * NCHUNK)
                over_parts(lambda r, hf: project(b, r, hf))

            group_means(0)
            over_batches(pe, image)

        @block.scalar
        def _(act):
            act.wait_ge(const_in, 160)
            act.wait_ge(setup, 5)

            def scale(b):
                act.wait_ge(scale_steps, b * SCALE_STEPS + 4)
                inverse_root(act, lnv[:, :], rstd[:, :], var[:, :], lnv_ready, b + 1).then_inc(rstd_ready, 1)

            def take_conv(b, c):
                m = b * NCHUNK + c
                act.wait_ge(conv_done, m + 1)
                wait(act, cen_ready, m - 1)
                src = conv_ps[:, :, :].rearrange("p s (r w) -> p s r w", w=W)
                dst = seq[:, c % 2, :, :].rearrange("p s (r w) -> p s r w", w=W)
                act.activation(dst[0:CB, 0], src[0:CB, 0], ACT.Identity, bias=conv_b[0:CB, :])
                act.activation(dst[CB:, 0], src[CB:, 0][:, :, ::-1], ACT.Identity, bias=conv_b[CB:, :])
                act.activation(dst[0:CB, 1], src[0:CB, 1][:, ::-1, :], ACT.Identity,
                               bias=conv_b[0:CB, :]).then_inc(seq_ready, 1)

            def squares(b, c):
                m = b * NCHUNK + c
                act.wait_ge(cen_ready, m + 1)
                wait(act, var_done, m)
                act.activation(sq_sb[:, :, :], cen[:, c % 2, :, :], ACT.Square).then_inc(sq_ready, 1)

            def root(b, c):
                m = b * NCHUNK + c
                act.wait_ge(var_done, m + 1)
                act.activation(lnr[:, :, :], stat_ps[:, :, :], ACT.Ln, bias=eps[:, :]).then_inc(lnr_ready, 1)
                act.wait_ge(lnr_ready, m + 1)
                wait(act, scaled, m)
                act.activation(rstd_sb[:, :, :], lnr[:, :, :], ACT.Exp, scale=-0.5).then_inc(root_ready, 1)

            def affine(b, c):
                m = b * NCHUNK + c
                act.wait_ge(scaled, m + 1)
                if c == 0:
                    wait(act, xn_stored, b * 16)
                    wait(act, proj_done, b * PARTS * 2 * PC)
                for slot, at in ((0, c), (1, NCHUNK - 1 - c)):
                    first = DCONV - 1 + at * T
                    last = act.activation(xn[:, slot, first:first + T], cen[:, c % 2, slot, :], ACT.Identity,
                                          scale=ln_w[:, slot:slot + 1], bias=ln_b[:, slot:slot + 1])
                last.then_inc(xn_ready, 1)

            def take_proj(b, r, hf):
                i = r * 2 + hf
                stores = b * (PARTS // 2) + r
                wait(act, u_stored[i % 2], stores * 16)
                wait(act, z_stored[i % 2], stores * 16)
                for c in range(PC):
                    m = (b * PARTS + i) * 2 * PC + 2 * c
                    base = i * 2 * PC + 2 * c
                    act.wait_ge(proj_done, m + 1)
                    act.activation(u_sb[:, i % 2, c * T:(c + 1) * T], proj_ps[:, base % 3, :], ACT.Silu,
                                   bias=conv1d_b[:, :]).then_inc(proj_read, 1)
                    act.wait_ge(proj_done, m + 2)
                    act.activation(z_sb[:, i % 2, c * T:(c + 1) * T], proj_ps[:, (base + 1) % 3, :],
                                   ACT.Silu).then_inc(proj_read, 1)

            def image(b):
                for c in range(NCHUNK + 1):
                    if c < NCHUNK:
                        take_conv(b, c)
                    if c >= 1:
                        squares(b, c - 1)
                        root(b, c - 1)
                        affine(b, c - 1)
                if not is_last(b):
                    scale(b + 1)
                over_parts(lambda r, hf: take_proj(b, r, hf))

            scale(0)
            over_batches(act, image)

        @block.vector
        def _(dve):
            dve.wait_ge(const_in, 160)
            dve.memset(eps[:, :], LN_EPS).then_inc(setup, 1)
            dve.memset(pad[:, :, :, :], 0.0).then_inc(setup, 1)
            dve.memset(seq[CB:, :, 1, :], 0.0).then_inc(setup, 1)
            dve.memset(xn[:, :, 0:DCONV - 1], 0.0).then_inc(setup, 1)
            for k in range(DCONV):
                last = dve.tensor_tensor(w_fold[:, k, :], w_in[:, 0:D1], w_conv[:, k, :], ALU.mult)
            last.then_inc(setup, 1)

            def measure(b):
                dve.wait_ge(x_in, (b + 1) * 16)
                wait(dve, g_done, b)
                group_stats(dve, b, xin, stats, mv, packed, sq, stat_steps, passed)

            def normalise(b):
                dve.wait_ge(g_done, b + 1)
                group_variance(dve, b, g_ps, gm, sq2, var, scale_steps)
                dve.wait_ge(rstd_ready, b + 1)
                dve.wait_ge(scale_steps, b * SCALE_STEPS + 4)
                dve.wait_ge(setup, 5)
                wait(dve, conv_done, b * NCHUNK)
                for half in range(2):
                    last = dve.tensor_scalar(pad[:, half, 1:1 + H, 1:1 + W],
                                             xin[:, half, :].rearrange("p (h w) -> p h w", w=W),
                                             gm[:, half:half + 1], rstd[:, half:half + 1], ALU.subtract, ALU.mult)
                last.then_inc(pad_ready, 1)

            def centre(b, c):
                m = b * NCHUNK + c
                dve.wait_ge(mean_done, m + 1)
                wait(dve, xn_ready, m - 1)
                dve.tensor_tensor(cen[:, c % 2, :, :], seq[:, c % 2, :, :], stat_ps[:, :, :],
                                  ALU.subtract).then_inc(cen_ready, 1)

            def scale(b, c):
                m = b * NCHUNK + c
                dve.wait_ge(root_ready, m + 1)
                dve.wait_ge(cen_ready, m + 1)
                dve.tensor_tensor(cen[:, c % 2, :, :], cen[:, c % 2, :, :], rstd_sb[:, :, :],
                                  ALU.mult).then_inc(scaled, 1)

            def image(b):
                for c in range(NCHUNK):
                    centre(b, c)
                    scale(b, c)
                if not is_last(b):
                    measure(b + 1)
                    normalise(b + 1)

            measure(0)
            normalise(0)
            over_batches(dve, image)


def layer1_output(nc, Y, Z, XN, x1, out, skip_in, w_out_in, mean_in, ln_w_in, ln_b_in, w_proj_in, proj_b_in):
    fp32 = mybir.dt.float32
    Yv = Y.rearrange("(b r c) p o j -> b c p (o r) j", b=B, r=NBR)
    Zv = Z.rearrange("(b r c) p o j -> b c p (o r) j", b=B, r=NBR)
    out_v = out.rearrange("b (s p) l -> b p s l", p=HALF)
    with ExitStack() as ctx:
        def sb(n, s, dt=fp32):
            return ctx.enter_context(nc.sbuf_tensor(f"m1_{n}", s, dt))

        def pb(n, s):
            return ctx.enter_context(nc.psum_tensor(f"m1_{n}", s, fp32))

        def sem(n):
            return ctx.enter_context(nc.semaphore(f"m1_{n}"))

        yb, zb, gated = sb("yb", [128, 2, NBR, T]), sb("zb", [128, 2, NBR, T]), sb("gated", [128, 2, NBR, T])
        xnb, x1b = sb("xnb", [128, 4, 2, T]), sb("x1b", [HALF, 4, 2, T])
        v, cen, sq = sb("v", [128, 2, 2, T]), sb("cen", [128, 2, 2, T]), sb("sq", [128, 2, T])
        yn = sb("yn", [128, 2, T])
        lnv, rstd = sb("lnv", [128, T]), sb("rstd", [128, T])
        res = sb("res", [HALF, 2, 2, T])
        skip, w_out, mean_w = sb("skip", [128, 1]), sb("w_out", [128, 2, 2 * CB]), sb("mean_w", [128, 2, 128])
        ln_w, ln_b, eps = sb("ln_w", [128, 2]), sb("ln_b", [128, 2]), sb("eps", [128, 1])
        w_proj, proj_b = sb("w_proj", [128, 2, CH]), sb("proj_b", [HALF, 2])
        op_ps, mean_ps, var_ps = pb("op_ps", [128, 2, T]), pb("mean_ps", [128, T]), pb("var_ps", [128, T])
        out_ps = pb("out_ps", [HALF, 2, 2, T])

        const_in, eps_set = sem("const_in"), sem("eps_set")
        yz_in = [sem(f"yz_in{p}") for p in range(2)]
        x_in = [sem(f"x_in{p}") for p in range(4)]
        gated_ready, op_done, v_ready, mean_done, cen_ready = (
            sem("gated_ready"), sem("op_done"), sem("v_ready"), sem("mean_done"), sem("cen_ready"))
        sq_ready, var_done, lnv_ready, rstd_ready, scaled = (
            sem("sq_ready"), sem("var_done"), sem("lnv_ready"), sem("rstd_ready"), sem("scaled"))
        yn_ready, out_done, res_ready = sem("yn_ready"), sem("out_done"), sem("res_ready")
        stored = [sem(f"stored{p}") for p in range(2)]
        block = ctx.enter_context(nc.Block())
        CONSTS = 16 * 7

        @block.sync
        def _(sp):
            for dst, src in ((skip[:, :], skip_in), (w_out[:, :, :], w_out_in), (mean_w[:, :, :], mean_in),
                             (ln_w[:, :], ln_w_in), (ln_b[:, :], ln_b_in), (w_proj[:, :, :], w_proj_in),
                             (proj_b[:, :], proj_b_in)):
                sp.dma_start(dst, src).then_inc(const_in, 16)

            def image(b):
                for c in range(NCHUNK):
                    m = b * NCHUNK + c
                    wait(sp, gated_ready, m - 1)
                    sp.dma_start(yb[:, c % 2, :, :], Yv[b, c]).then_inc(yz_in[c % 2], 16)
                    sp.dma_start(zb[:, c % 2, :, :], Zv[b, c]).then_inc(yz_in[c % 2], 16)
                    wait(sp, res_ready, m - 3)
                    sp.dma_start(xnb[:, c % 4, :, :], XN[b][:, :, c * T:(c + 1) * T]).then_inc(x_in[c % 4], 16)
                    sp.dma_start(x1b[:, c % 4, :, :], x1[b][:, :, c * T:(c + 1) * T]).then_inc(x_in[c % 4], 16)

            over_batches(sp, image)
            for p in range(2):
                sp.wait_ge(stored[p], 16 * B * NCHUNK // 2)

        @block.tensor
        def _(pe):
            pe.wait_ge(const_in, CONSTS)

            def out_proj(b, c):
                m = b * NCHUNK + c
                pe.wait_ge(gated_ready, m + 1)
                wait(pe, v_ready, m)
                for lo, hi, slot, r in ((0, CB, 0, 0), (CB, 2 * CB, 0, 1), (0, 2 * CB, 1, 2)):
                    last = pe.matmul(op_ps[lo:hi, slot, :], w_out[:, 1 if r == 2 else 0, 0:hi - lo],
                                     gated[:, c % 2, r, :], start=True, stop=True)
                last.then_inc(op_done, 1)

            def mean(b, c):
                m = b * NCHUNK + c
                pe.wait_ge(v_ready, m + 1)
                wait(pe, cen_ready, m)
                for slot in range(2):
                    last = pe.matmul(mean_ps[:, :], mean_w[:, slot, :], v[:, c % 2, slot, :], start=slot == 0, stop=slot == 1)
                last.then_inc(mean_done, 1)

            def variance(b, c):
                m = b * NCHUNK + c
                pe.wait_ge(sq_ready, m + 1)
                wait(pe, lnv_ready, m)
                for slot in range(2):
                    last = pe.matmul(var_ps[:, :], mean_w[:, slot, :], sq[:, slot, :], start=slot == 0, stop=slot == 1)
                last.then_inc(var_done, 1)

            def project(b, c):
                m = b * NCHUNK + c
                pe.wait_ge(yn_ready, m + 1)
                wait(pe, res_ready, m - 1)
                for half in range(2):
                    for slot in range(2):
                        last = pe.matmul(out_ps[:, c % 2, half, :], w_proj[:, slot, half * HALF:(half + 1) * HALF],
                                         yn[:, slot, :], start=slot == 0, stop=slot == 1)
                last.then_inc(out_done, 1)

            def image(b):
                for c in range(NCHUNK + 3):
                    if c < NCHUNK:
                        out_proj(b, c)
                    if 1 <= c <= NCHUNK:
                        mean(b, c - 1)
                    if 2 <= c <= NCHUNK + 1:
                        variance(b, c - 2)
                    if c >= 3:
                        project(b, c - 3)

            over_batches(pe, image)

        @block.scalar
        def _(act):
            act.wait_ge(const_in, CONSTS)
            act.wait_ge(eps_set, 1)

            def squares(b, c):
                m = b * NCHUNK + c
                act.wait_ge(cen_ready, m + 1)
                wait(act, var_done, m)
                act.activation(sq[:, :, :], cen[:, c % 2, :, :], ACT.Square).then_inc(sq_ready, 1)

            def root(b, c):
                m = b * NCHUNK + c
                act.wait_ge(var_done, m + 1)
                act.activation(lnv[:, :], var_ps[:, :], ACT.Ln, bias=eps[:, :]).then_inc(lnv_ready, 1)
                act.wait_ge(lnv_ready, m + 1)
                wait(act, scaled, m)
                act.activation(rstd[:, :], lnv[:, :], ACT.Exp, scale=-0.5).then_inc(rstd_ready, 1)

            def affine(b, c):
                m = b * NCHUNK + c
                act.wait_ge(scaled, m + 1)
                wait(act, out_done, m)
                for slot in range(2):
                    last = act.activation(yn[:, slot, :], cen[:, c % 2, slot, :], ACT.Identity,
                                          scale=ln_w[:, slot:slot + 1], bias=ln_b[:, slot:slot + 1])
                last.then_inc(yn_ready, 1)

            def store(b, c):
                m = b * NCHUNK + c
                act.wait_ge(res_ready, m + 1)
                act.dma_start(out_v[b][:, :, c * T:(c + 1) * T], res[:, c % 2, :, :]).then_inc(stored[c % 2], 16)

            def image(b):
                for c in range(NCHUNK + 3):
                    if 1 <= c <= NCHUNK:
                        squares(b, c - 1)
                    if 2 <= c <= NCHUNK + 1:
                        root(b, c - 2)
                        affine(b, c - 2)
                    if c >= 3:
                        store(b, c - 3)

            over_batches(act, image)

        @block.vector
        def _(dve):
            dve.memset(eps[:, :], LN_EPS).then_inc(eps_set, 1)
            dve.wait_ge(const_in, CONSTS)

            def add_skip(b, c):
                m = b * NCHUNK + c
                dve.wait_ge(op_done, m + 1)
                dve.wait_ge(x_in[c % 4], b * (32 * NCHUNK // 4) + (c // 4 + 1) * 32)
                wait(dve, cen_ready, m - 1)
                dve.scalar_tensor_tensor(v[:, c % 2, :, :], xnb[:, c % 4, :, :], skip[:, 0:1], op_ps[:, :, :],
                                         ALU.mult, ALU.add).then_inc(v_ready, 1)

            def centre(b, c):
                m = b * NCHUNK + c
                dve.wait_ge(mean_done, m + 1)
                wait(dve, yn_ready, m - 1)
                dve.tensor_tensor(cen[:, c % 2, :, :], v[:, c % 2, :, :],
                                  mean_ps[:, :].unsqueeze(1).broadcast_to([128, 2, T]), ALU.subtract).then_inc(cen_ready, 1)

            def scale(b, c):
                m = b * NCHUNK + c
                dve.wait_ge(rstd_ready, m + 1)
                dve.wait_ge(cen_ready, m + 1)
                dve.tensor_tensor(cen[:, c % 2, :, :], cen[:, c % 2, :, :],
                                  rstd[:, :].unsqueeze(1).broadcast_to([128, 2, T]), ALU.mult).then_inc(scaled, 1)

            def residual(b, c):
                m = b * NCHUNK + c
                dve.wait_ge(out_done, m + 1)
                wait(dve, stored[c % 2], b * (16 * NCHUNK // 2) + (c // 2) * 16)
                for half in range(2):
                    last = dve.scalar_tensor_tensor(res[:, c % 2, half, :], out_ps[:, c % 2, half, :],
                                                    proj_b[:, half:half + 1], x1b[:, c % 4, half, :], ALU.add, ALU.add)
                last.then_inc(res_ready, 1)

            def image(b):
                for c in range(NCHUNK + 3):
                    if c < NCHUNK:
                        add_skip(b, c)
                    if 1 <= c <= NCHUNK:
                        centre(b, c - 1)
                    if 2 <= c <= NCHUNK + 1:
                        scale(b, c - 2)
                    if c >= 3:
                        residual(b, c - 3)

            over_batches(dve, image)

        @block.gpsimd
        def _(pool):
            def image(b):
                for c in range(NCHUNK):
                    m = b * NCHUNK + c
                    pool.wait_ge(yz_in[c % 2], b * (32 * NCHUNK // 2) + (c // 2 + 1) * 32)
                    wait(pool, op_done, m - 1)
                    pool.tensor_tensor(gated[:, c % 2, :, :], yb[:, c % 2, :, :], zb[:, c % 2, :, :],
                                       ALU.mult).then_inc(gated_ready, 1)

            over_batches(pool, image)


def build(nc, arg, out):
    fp32 = mybir.dt.float32

    def scratch(name, shape):
        return nc.dram_tensor(name, shape, fp32, kind="Internal").ap()

    units0, units1 = B * K0 * NCHUNK, B * NBR * NCHUNK
    U0, Y0 = scratch("U0", (units0, 128, ND0, T)), scratch("Y0", (units0, 128, ND0, T))
    x1 = scratch("x1", (B, HALF, 2, L))
    U1, Y1, Z1 = (scratch(n, (units1, 128, 1, T)) for n in ("U1", "Y1", "Z1"))
    XN = scratch("XN", (B, 128, 2, L))
    x = arg["x"].rearrange("b (s p) l -> b p s l", p=HALF)

    layer0_features(nc, x, U0, arg["group_mean"], arg["a_in"], arg["a_taps"], arg["a_conv_b"], arg["ident"])
    scan_phase(nc, "s0", (B, K0, ND0, 1, R0), U0, Y0, arg["a_xproj"], arg["a_dt"], arg["a_small"],
               arg["keep"], arg["ident"], arg["select"])
    layer0_output(nc, Y0, x, x1, arg["mean_384"], arg["a_ln_w"], arg["a_ln_b"], arg["a_out"])
    layer1_features(nc, x1, U1, Z1, XN, arg["group_mean"], arg["b_pair"], arg["b_third"], arg["b_conv_b"],
                    arg["mean_64"], arg["b_ln1_w"], arg["b_ln1_b"], arg["b_in"], arg["b_conv1d"], arg["b_conv1d_b"])
    scan_phase(nc, "s1", (B * NBR, 1, 1, 2, R1), U1, Y1, arg["b_xproj"], arg["b_dt"], arg["b_small"],
               arg["keep"], arg["ident"], arg["select"])
    layer1_output(nc, Y1, Z1, XN, x1, out, arg["b_skip"], arg["b_out"], arg["mean_192"], arg["b_ln_w"],
                  arg["b_ln_b"], arg["b_proj"], arg["b_proj_b"])


def kernel(**inputs):
    import numpy as np
    import concourse.bacc as _bacc
    from concourse.bass_utils import run_bass_kernel_spmd as _run

    a = {k: np.asarray(v) for k, v in inputs.items()}
    la = {k[len("L0_conv_"):]: v for k, v in a.items() if k.startswith("L0_conv_")}
    lb = {k[len("L1_conv_"):]: v for k, v in a.items() if k.startswith("L1_conv_")}
    f = a["x"].dtype

    def columns(v, n):
        return np.swapaxes(v.reshape(*v.shape[:-1], n, 128), -1, -2)

    def xproj(w, rank, nd):
        bc = w[:, rank:]
        w = np.concatenate([bc, bc, bc, w[:, :rank]], 1)
        return w.reshape(len(w), XROWS + rank, nd, 128).transpose(0, 3, 2, 1)

    def small(bias, D, A_log, nd):
        k = len(bias)
        logs = A_log.reshape(k, nd, 128, N_STATE).transpose(0, 2, 1, 3).reshape(k, 128, nd * N_STATE)
        return np.concatenate([columns(bias, nd), columns(D, nd), logs], 2)

    def pair(v):
        return np.stack([np.concatenate([v, v]), np.concatenate([v, np.zeros_like(v)])], 1)

    def slots(v):
        return np.stack([v[:128], np.concatenate([v[128:], np.zeros_like(v[:64])])], 1)

    ident = np.eye(128, dtype=f)
    select = np.zeros((XROWS, 2 * N_STATE, 128), f)
    for n in range(2 * N_STATE):
        select[n::2 * N_STATE, n] = 1
    keep = np.ones((NCHUNK, 128, 1), f)
    keep[-1] = 0
    group_mean, mean_64 = np.zeros((HALF, HALF), f), np.zeros((128, 128), f)
    for g in range(0, HALF, CH // 32):
        group_mean[g:g + CH // 32, g:g + CH // 32] = 32 / CH
    for g in range(0, 128, CB):
        mean_64[g:g + CB, g:g + CB] = 1 / CB
    mean_192 = np.zeros((128, 2, 128), f)
    mean_192[:, 0] = 1 / CH
    mean_192[:CH - 128, 1] = 1 / CH

    taps = lb["conv1_w"].reshape(CB, 2, HALF, 3, 3).transpose(2, 1, 3, 4, 0)
    w_out = lb["out_proj_w"].T
    arrays = {
        "x": a["x"].reshape(B, CH, L),
        "ident": ident, "select": select.reshape(XROWS, -1), "keep": keep, "group_mean": group_mean,
        "mean_384": np.full((128, 128), 1 / D0, f), "mean_64": mean_64, "mean_192": mean_192,
        "a_in": la["in_proj_w"].T.reshape(2, HALF, D0).transpose(1, 0, 2),
        "a_taps": la["conv_w"].reshape(ND0, 128, TAPS).transpose(1, 0, 2),
        "a_conv_b": columns(la["conv_b"], ND0),
        "a_xproj": xproj(la["x_proj_weight"], R0, ND0),
        "a_dt": la["dt_projs_weight"].reshape(K0, ND0, 128, R0).transpose(0, 3, 1, 2),
        "a_small": small(la["dt_projs_bias"], la["Ds"].reshape(K0, D0), la["A_logs"], ND0),
        "a_ln_w": columns(la["ln_w"], ND0), "a_ln_b": columns(la["ln_b"], ND0),
        "a_out": la["out_proj_w"].T.reshape(ND0, 128, CH).transpose(1, 0, 2),
        "b_pair": np.concatenate([taps, taps[:, :, :, ::-1]], 4).reshape(HALF, 2, TAPS, 2 * CB),
        "b_third": taps[:, :, ::-1].reshape(HALF, 2, TAPS, CB),
        "b_conv_b": np.concatenate([lb["conv1_b"]] * 2)[:, None],
        "b_ln1_w": pair(lb["norm1_w"]), "b_ln1_b": pair(lb["norm1_b"]),
        "b_in": np.concatenate([lb["in_proj_w"].T] * 2),
        "b_conv1d": np.broadcast_to(lb["convd_w"].T[None], (128, DCONV, D1)),
        "b_conv1d_b": lb["convd_b"][:, None],
        "b_xproj": xproj(lb["x_proj_w"][None], R1, 1),
        "b_dt": lb["dt_proj_w"].T[None, :, None, :],
        "b_small": small(lb["dt_proj_b"][None], lb["D_param"][None], lb["A_log"], 1),
        "b_skip": np.broadcast_to(lb["skip_scale"][None], (128, 1)),
        "b_out": np.stack([np.concatenate([w_out, np.zeros_like(w_out)], 1)] * 2, 1),
        "b_ln_w": slots(lb["norm_w"]), "b_ln_b": slots(lb["norm_b"]),
        "b_proj": slots(lb["proj_w"].T), "b_proj_b": lb["proj_b"].reshape(2, HALF).T,
    }
    nc = _bacc.Bacc("TRN2", target_bir_lowering=False, num_devices=1)
    arrays = {f"in_{k}": np.ascontiguousarray(v) for k, v in arrays.items()}
    arg = {k[3:]: nc.dram_tensor(k, v.shape, mybir.dt.from_np(v.dtype), kind="ExternalInput").ap()
           for k, v in arrays.items()}
    out = nc.dram_tensor("out", (B, CH, L), mybir.dt.float32, kind="ExternalOutput").ap()
    build(nc, arg, out)
    r = _run(nc, [arrays], core_ids=[0])
    return r.results[0]["out"].reshape(B, CH, H, W)
```

```python
from contextlib import ExitStack

import concourse.bass as bass
from concourse import mybir

ACT = mybir.ActivationFunctionType
ALU = mybir.AluOpType

B, CH, H, W = 8, 192, 64, 64
L = H * W
T = 512
NCHUNK = L // T
ROWS = T // W
HALF = CH // 2
GROUP_EPS = 1e-5
LN_EPS = 1e-5
N_STATE = 16
XROWS = 3 * 2 * N_STATE

D0, K0, R0 = 384, 4, 12
ND0 = D0 // 128
CB, D1, R1, NBR = 64, 128, 4, 3
TAPS = 9
DCONV = 4


def wait(eng, semaphore, value):
    if not (isinstance(value, int) and value <= 0):
        eng.wait_ge(semaphore, value)


def over_batches(eng, body):
    body(0)
    with eng.Fori(1, B - 1) as b:
        body(b)
    body(B - 1)


def is_last(b):
    return isinstance(b, int) and b == B - 1


STATS_STEPS, SCALE_STEPS = 4, 4


def group_stats(dve, b, x, stats, mv, packed, sq, steps, passed):
    done = b * STATS_STEPS
    for half in range(2):
        for c in range(NCHUNK):
            last = dve.bn_stats(stats[:, half, c, :], x[:, half, c * T:(c + 1) * T])
    last.then_inc(steps, 1)
    dve.wait_ge(steps, done + 1)
    dve.sem_inc(passed, 1)
    for half in range(2):
        last = dve.bn_aggr(mv[:, half, :], stats[:, half, :, :].rearrange("p c s -> p (c s)"))
    last.then_inc(steps, 1)
    dve.wait_ge(steps, done + 2)
    dve.tensor_copy(packed[:, 0:2], mv[:, :, 0])
    dve.tensor_tensor(sq[:, :], mv[:, :, 0], mv[:, :, 0], ALU.mult).then_inc(steps, 1)
    dve.wait_ge(steps, done + 3)
    dve.tensor_tensor(packed[:, 2:4], sq[:, :], mv[:, :, 1], ALU.add).then_inc(steps, 1)


def group_variance(dve, b, g_ps, gm, sq, var, steps):
    done = b * SCALE_STEPS
    dve.tensor_copy(gm[:, :], g_ps[:, :]).then_inc(steps, 1)
    dve.wait_ge(steps, done + 1)
    dve.tensor_tensor(sq[:, :], gm[:, 0:2], gm[:, 0:2], ALU.mult).then_inc(steps, 1)
    dve.wait_ge(steps, done + 2)
    dve.tensor_tensor(sq[:, :], gm[:, 2:4], sq[:, :], ALU.subtract).then_inc(steps, 1)
    dve.wait_ge(steps, done + 3)
    dve.tensor_scalar(var[:, :], sq[:, :], GROUP_EPS, None, ALU.add).then_inc(steps, 1)


def inverse_root(act, lnv, rstd, var, half_step, half_value):
    act.activation(lnv, var, ACT.Ln).then_inc(half_step, 1)
    act.wait_ge(half_step, half_value)
    return act.activation(rstd, lnv, ACT.Exp, scale=-0.5)


def layer0_features(nc, x, U, gmat_in, w_in_in, taps_in, conv_b_in, ident_in):
    fp32 = mybir.dt.float32
    Uv = U.rearrange("(b k c) p t j -> b k t p c j", b=B, k=K0)
    with ExitStack() as ctx:
        ctx.enter_context(nc.cleanup_on_exit())
        def sb(n, s, dt=fp32):
            return ctx.enter_context(nc.sbuf_tensor(f"f0_{n}", s, dt))

        def pb(n, s):
            return ctx.enter_context(nc.psum_tensor(f"f0_{n}", s, fp32))

        def sem(n):
            return nc.alloc_semaphore(f"f0_{n}")

        xin = sb("xin", [HALF, 2, L])
        pad = [sb(f"pad{t}", [128, H + 2, W + 2]) for t in range(ND0)]
        row = [sb(f"row{t}", [128, L]) for t in range(ND0)]
        col, row_rev, col_rev = sb("col", [128, L]), sb("row_rev", [128, L]), sb("col_rev", [128, L])
        gmat, w_in = sb("gmat", [HALF, HALF]), sb("w_in", [HALF, 2, D0])
        taps, conv_b, ident = sb("taps", [128, ND0, TAPS]), sb("conv_b", [128, ND0]), sb("ident", [128, 128])
        diag = sb("diag", [128, ND0 * TAPS, 128])
        stats, mv = sb("stats", [HALF, 2, NCHUNK, 6]), sb("mv", [HALF, 2, 2])
        packed, sq = sb("packed", [HALF, 4]), sb("sq", [HALF, 2])
        gm, sq2, var, lnv, rstd = (sb("gm", [HALF, 4]), sb("sq2", [HALF, 2]), sb("var", [HALF, 2]),
                                   sb("lnv", [HALF, 2]), sb("rstd", [HALF, 2]))
        in_ps = pb("in_ps", [128, 3, T])
        conv_ps = pb("conv_ps", [128, 4, T])
        g_ps = pb("g_ps", [HALF, 4])

        const_in, x_in, setup, passed = sem("const_in"), sem("x_in"), sem("setup"), sem("passed")
        stat_steps, g_done, scale_steps = sem("stat_steps"), sem("g_done"), sem("scale_steps")
        lnv_ready, rstd_ready, xn_ready = sem("lnv_ready"), sem("rstd_ready"), sem("xn_ready")
        in_done, pad_ready, conv_done, row_ready = sem("in_done"), sem("pad_ready"), sem("conv_done"), sem("row_ready")
        col_ready, rev_ready, col_rev_ready = sem("col_ready"), sem("rev_ready"), sem("col_rev_ready")
        stored = [sem(f"stored{k}") for k in range(ND0 + K0 - 1)]
        block = ctx.enter_context(nc.Block())

        def tile(b, t):
            return b * ND0 + t

        @block.sync
        def _(sp):
            sp.dma_start(gmat[:, :], gmat_in).then_inc(const_in, 16)
            sp.dma_start(w_in[:, :, :], w_in_in).then_inc(const_in, 16)
            sp.dma_start(taps[:, :, :], taps_in).then_inc(const_in, 16)
            sp.dma_start(conv_b[:, :], conv_b_in).then_inc(const_in, 16)
            sp.dma_start(ident[:, :], ident_in).then_inc(const_in, 16)
            sp.dma_start(xin[:, :, :], x[0]).then_inc(x_in, 16)

            def image(b):
                for t in range(ND0):
                    if t == 1 and not is_last(b):
                        sp.wait_ge(in_done, (b + 1) * ND0 * NCHUNK)
                        sp.dma_start(xin[:, :, :], x[b + 1]).then_inc(x_in, 16)
                    for k, src, ready, count in (
                            (0, row[t], row_ready, NCHUNK), (1, col, col_ready, 1),
                            (2, row_rev, rev_ready, 1), (3, col_rev, col_rev_ready, 1)):
                        sp.wait_ge(ready, (tile(b, t) + 1) * count)
                        done = stored[t] if k == 0 else stored[ND0 - 1 + k]
                        sp.dma_start(Uv[b, k, t], src[:, :].rearrange("p (c j) -> p c j", j=T)).then_inc(done, 16)

            over_batches(sp, image)
            for t in range(ND0):
                sp.wait_ge(stored[t], 16 * B)
            for k in range(1, K0):
                sp.wait_ge(stored[ND0 - 1 + k], 16 * B * ND0)

        @block.tensor
        def _(pe):
            pe.wait_ge(const_in, 80)
            pe.wait_ge(setup, 1 + ND0)

            def group_means(b):
                pe.wait_ge(stat_steps, (b + 1) * STATS_STEPS)
                pe.matmul(g_ps[:, :], gmat[:, :], packed[:, :], start=True, stop=True).then_inc(g_done, 1)

            def in_proj(b, t):
                for c in range(NCHUNK):
                    m = tile(b, t) * NCHUNK + c
                    bank = (t * NCHUNK + c) % 3
                    wait(pe, pad_ready, m - 2)
                    for half in range(2):
                        last = pe.matmul(in_ps[:, bank, :], w_in[:, half, t * 128:(t + 1) * 128],
                                         xin[:, half, c * T:(c + 1) * T], start=half == 0, stop=half == 1)
                    last.then_inc(in_done, 1)

            def conv(b, t):
                pe.wait_ge(pad_ready, (tile(b, t) + 1) * NCHUNK)
                for c in range(NCHUNK):
                    wait(pe, row_ready, tile(b, t) * NCHUNK + c - 3)
                    for k in range(TAPS):
                        dy, dx = divmod(k, 3)
                        last = pe.matmul(conv_ps[:, c % 4, :], diag[:, t * TAPS + k, :],
                                         pad[t][:, c * ROWS + dy:c * ROWS + dy + ROWS, dx:dx + W],
                                         start=k == 0, stop=k == TAPS - 1)
                    last.then_inc(conv_done, 1)

            def image(b):
                pe.wait_ge(xn_ready, b + 1)
                in_proj(b, 0)
                in_proj(b, 1)
                conv(b, 0)
                in_proj(b, 2)
                conv(b, 1)
                if not is_last(b):
                    group_means(b + 1)
                conv(b, 2)

            group_means(0)
            over_batches(pe, image)

        @block.scalar
        def _(act):
            act.wait_ge(const_in, 80)

            def scale(b):
                act.wait_ge(scale_steps, b * SCALE_STEPS + 4)
                inverse_root(act, lnv[:, :], rstd[:, :], var[:, :], lnv_ready, b + 1).then_inc(rstd_ready, 1)

            def take_in(b, t):
                for c in range(NCHUNK):
                    act.wait_ge(in_done, tile(b, t) * NCHUNK + c + 1)
                    act.activation(pad[t][:, 1 + c * ROWS:1 + (c + 1) * ROWS, 1:1 + W],
                                   in_ps[:, (t * NCHUNK + c) % 3, :].rearrange("p (r w) -> p r w", w=W),
                                   ACT.Copy).then_inc(pad_ready, 1)

            def take_conv(b, t):
                n = tile(b, t)
                wait(act, stored[t], b * 16)
                wait(act, col_ready, n - 2)
                wait(act, rev_ready, n - 2)
                for c in range(NCHUNK):
                    act.wait_ge(conv_done, n * NCHUNK + c + 1)
                    act.activation(row[t][:, c * T:(c + 1) * T], conv_ps[:, c % 4, :], ACT.Silu,
                                   bias=conv_b[:, t:t + 1]).then_inc(row_ready, 1)

            def image(b):
                take_in(b, 0)
                take_in(b, 1)
                take_conv(b, 0)
                take_in(b, 2)
                take_conv(b, 1)
                if not is_last(b):
                    scale(b + 1)
                take_conv(b, 2)

            act.wait_ge(setup, 1 + ND0)
            scale(0)
            over_batches(act, image)

        @block.vector
        def _(dve):
            dve.wait_ge(const_in, 80)
            for t in range(ND0):
                dve.memset(pad[t][:, :, :], 0.0).then_inc(setup, 1)
            for t in range(ND0):
                for k in range(TAPS):
                    last = dve.tensor_scalar(diag[:, t * TAPS + k, :], ident[:, :], taps[:, t, k:k + 1], None, ALU.mult)
            last.then_inc(setup, 1)

            def measure(b):
                dve.wait_ge(x_in, (b + 1) * 16)
                wait(dve, g_done, b)
                group_stats(dve, b, xin, stats, mv, packed, sq, stat_steps, passed)

            def normalise(b):
                dve.wait_ge(g_done, b + 1)
                group_variance(dve, b, g_ps, gm, sq2, var, scale_steps)
                dve.wait_ge(rstd_ready, b + 1)
                dve.wait_ge(scale_steps, b * SCALE_STEPS + 4)
                for half in range(2):
                    last = dve.tensor_scalar(xin[:, half, :], xin[:, half, :], gm[:, half:half + 1],
                                             rstd[:, half:half + 1], ALU.subtract, ALU.mult)
                last.then_inc(xn_ready, 1)

            def turn(b, t):
                n = tile(b, t)
                dve.wait_ge(row_ready, (n + 1) * NCHUNK)
                wait(dve, stored[ND0], n * 16)
                wait(dve, col_rev_ready, n)
                dve.tensor_copy(col[:, :].rearrange("p (w h) -> p w h", h=H),
                                row[t][:, :].rearrange("p (h w) -> p w h", w=W)).then_inc(col_ready, 1)

            def image(b):
                turn(b, 0)
                if not is_last(b):
                    measure(b + 1)
                turn(b, 1)
                if not is_last(b):
                    normalise(b + 1)
                turn(b, 2)

            measure(0)
            normalise(0)
            over_batches(dve, image)

        @block.gpsimd
        def _(pool):
            def image(b):
                for t in range(ND0):
                    n = tile(b, t)
                    pool.wait_ge(row_ready, (n + 1) * NCHUNK)
                    wait(pool, stored[ND0 + 1], n * 16)
                    pool.sem_inc(passed, 1)
                    pool.tensor_copy(row_rev[:, :], row[t][:, ::-1]).then_inc(rev_ready, 1)
                    pool.wait_ge(col_ready, n + 1)
                    wait(pool, stored[ND0 + 2], n * 16)
                    pool.sem_inc(passed, 1)
                    pool.tensor_copy(col_rev[:, :], col[:, ::-1]).then_inc(col_rev_ready, 1)

            over_batches(pool, image)


def scan_phase(nc, name, shape, U, Y, w_x, w_dt, w_small, keep, ident_in, sel_in):
    outer, K, nd, ng, rank = shape
    J, NS, NCH = nd * ng, N_STATE // ng, L // T
    seqs = outer * K
    units = seqs * NCH
    fp32, bf16 = mybir.dt.float32, mybir.dt.bfloat16
    SM = nd * (2 + N_STATE)
    LOADS = 5
    AHEAD = 4
    DECAYS = 2 * J
    GROUP = 2 if nd > 1 else 4
    GROUPS = NS // GROUP
    LEAD, COPY_LEAD = (4, 3) if nd > 1 else (3, 2)
    B_BANKS = 2 if nd > 1 else 1
    at = (dict(xproj=0, dt=(1, 2, 3), take=1, take_dt=(2, 3, 4), ex=(3, 4, 5), series=(5, 6, 8), log=(6, 7, 8),
               direct=(11, 12, 13), rest1=2, mid=3, rest2=4, low=5, near=(7, 9, 10), pick=(8, 10, 11),
               delta=(13, 14, 15))
          if nd > 1 else
          dict(xproj=0, dt=(1,), take=1, take_dt=(2,), ex=(2,), series=(3,), log=(3,),
               direct=(6,), rest1=2, mid=2, rest2=3, low=3, near=(5,), pick=(5,), delta=(7,)))
    SMALL, ROOT_A, ROOT_B, ROOT_C = 1 / 64, 3 ** -0.5, 3 ** 0.5 / 4, 13 / 16

    with ExitStack() as ctx:
        ctx.enter_context(nc.cleanup_on_exit())
        def sb(n, s, dt=fp32):
            return ctx.enter_context(nc.sbuf_tensor(f"{name}_{n}", s, dt))

        def pb(n, s):
            return ctx.enter_context(nc.psum_tensor(f"{name}_{n}", s, fp32))

        def sem(n):
            return nc.alloc_semaphore(f"{name}_{n}")

        u = [sb(f"u{q}", [128, nd, T]) for q in range(2)]
        wx = [sb(f"wx{q}", [128, nd, XROWS + rank]) for q in range(2)]
        wdt = [sb(f"wdt{q}", [128, nd, 128]) for q in range(2)]
        small = [sb(f"small{q}", [128, SM]) for q in range(2)]
        keep_in = [sb(f"keep_in{q}", [128, 1]) for q in range(2)]
        keep_sb = [sb(f"keep{q}", [128, 1]) for q in range(2)]
        negA = [sb(f"negA{q}", [128, nd * N_STATE]) for q in range(2)]
        delta = [sb(f"delta{q}", [128, nd, T]) for q in range(2)]
        du = [sb(f"du{q}", [128, nd, T]) for q in range(2)]
        bc16 = [sb(f"bc16{q}", [96, T], bf16) for q in range(2)]
        yo = [sb(f"yo{q}", [128, nd, T]) for q in range(2)]
        xd = sb("xd", [XROWS + rank, T])
        rest1 = sb("rest1", [96, T])
        mid16 = sb("mid16", [96, T], bf16)
        rest2 = sb("rest2", [96, T])
        work = sb("work", [128, 5, max(nd * T, 2 * N_STATE * 128 // 5 + 1)])
        ex, lnx, near, is_small, relx = (
            work[:, i, 0:nd * T].rearrange("p (t j) -> p t j", j=T) for i in range(5))
        b_sb = sb("b_sb", [128, AHEAD, ng, T])
        dbu = sb("dbu", [128, AHEAD, J, T])
        dA = sb("dA", [128, DECAYS, T])
        h = sb("h", [128, 2 * GROUP, J, T])
        hc = sb("hc", [128, 2, J, T])
        state = sb("state", [128, NS, J])
        ident = sb("ident", [128, 128])
        self32 = work[0:96].rearrange("p a b -> p (a b)")[:, 0:2 * N_STATE * 128]
        sel = sb("sel", [96, 2 * N_STATE, 128], bf16)

        consts = sb("consts", [128, 2])
        c_ps = pb("c_ps", [128, 2, ng, T])
        b_ps = pb("b_ps", [128, B_BANKS, ng, T])
        y_ps = pb("y_ps", [128, nd, T])
        prep_ps = pb("prep_ps", [128, T])

        const_in, sel_ready, passed = sem("const_in"), sem("sel_ready"), sem("passed")
        loaded = [sem(f"loaded{q}") for q in range(2)]
        stored = [sem(f"stored{q}") for q in range(2)]
        xproj_done, xd_ready, dt_done, prep_read = sem("xproj_done"), sem("xd_ready"), sem("dt_done"), sem("prep_read")
        rests, mid_ready, bc_ready = sem("rests"), sem("mid_ready"), sem("bc_ready")
        ex_ready, near_ready, log_ready, consts_set, square_done = sem("ex_ready"), sem("near_ready"), sem("log_ready"), sem("consts_set"), sem("square_done")
        negA_ready, abs_done, soft_done, delta_ready, du_ready = (
            sem("negA_ready"), sem("abs_done"), sem("soft_done"), sem("delta_ready"), sem("du_ready"))
        b_done, b_copied, c_done = sem("b_done"), sem("b_copied"), sem("c_done")
        dA_ready, dbu_ready, scanned, hc_ready, summed = (
            sem("dA_ready"), sem("dbu_ready"), sem("scanned"), sem("hc_ready"), sem("summed"))
        state_saved, evacuated, direct_ready = sem("state_saved"), sem("evacuated"), sem("direct_ready")

        def bias_of(q, t):
            return small[q][:, t:t + 1]

        def D_of(q, t):
            return small[q][:, nd + t:nd + t + 1]

        def earlier_stores(g, q):
            return 16 * (g // 2) if isinstance(g, int) else (g - q) * 8

        def over_units(eng, unit):
            unit(0, 0, True)
            unit(1, 1, False)
            with eng.Fori(1, units // 2) as i:
                unit(i * 2, 0, False)
                unit(i * 2 + 1, 1, False)

        block = ctx.enter_context(nc.Block())

        @block.sync
        def _(eng):
            eng.dma_start(ident[:, :], ident_in).then_inc(const_in, 16)
            eng.dma_start(self32, sel_in).then_inc(const_in, 16)

            def load(g, k, c, q):
                eng.wait_ge(du_ready, (g + 1) * nd)
                eng.wait_ge(direct_ready, (g + 1) * nd)
                eng.dma_start(u[q][:, :, :], U[g]).then_inc(loaded[q], 16)
                eng.dma_start(wx[q][:, :, :], w_x[k]).then_inc(loaded[q], 16)
                eng.dma_start(wdt[q][XROWS:XROWS + rank, :, :], w_dt[k]).then_inc(loaded[q], 16)
                eng.dma_start(small[q][:, :], w_small[k]).then_inc(loaded[q], 16)
                eng.dma_start(keep_in[q][:, :], keep[c]).then_inc(loaded[q], 16)

            with eng.Fori(0, outer) as o:
                with eng.Fori(0, K) as k:
                    with eng.Fori(0, NCH // 2) as c2:
                        for q in range(2):
                            load((o * K + k) * NCH + c2 * 2 + q, k, c2 * 2 + q, q)
            eng.wait_ge(du_ready, (units + 1) * nd)
            eng.wait_ge(direct_ready, (units + 1) * nd)
            eng.dma_start(u[0][:, :, :], U[0]).then_inc(loaded[0], 16)
            eng.dma_start(wx[0][:, :, :], w_x[0]).then_inc(loaded[0], 16)
            eng.dma_start(wdt[0][XROWS:XROWS + rank, :, :], w_dt[0]).then_inc(loaded[0], 16)
            eng.dma_start(small[0][:, :], w_small[0]).then_inc(loaded[0], 16)
            eng.dma_start(keep_in[0][:, :], keep[0]).then_inc(loaded[0], 16)
            for q in range(2):
                eng.wait_ge(stored[q], 16 * (units // 2))

        def loads_of(g, q):
            half = g // 2 if isinstance(g, int) else (g - q) // 2
            return 16 * LOADS * (half + 1) if isinstance(half, int) else half * (16 * LOADS) + 16 * LOADS

        @block.tensor
        def _(pe):
            def xproj(g, q, lw):
                pe.wait_ge(loaded[q], lw)
                wait(pe, prep_read, g * (1 + nd))
                for t in range(nd):
                    last = pe.matmul(prep_ps[0:XROWS + rank], wx[q][:, t, :], u[q][:, t, :],
                                     start=t == 0, stop=t == nd - 1)
                last.then_inc(xproj_done, 1)

            def dt(g, q, t):
                pe.wait_ge(xd_ready, g + 1)
                pe.wait_ge(prep_read, g * (1 + nd) + 1 + t)
                pe.matmul(prep_ps[:, :], wdt[q][XROWS:XROWS + rank, t, :], xd[XROWS:XROWS + rank, :],
                          start=True, stop=True).then_inc(dt_done, 1)

            def b_broadcast(g, q, s):
                n = g * NS + s
                if s == 0:
                    pe.wait_ge(bc_ready, g * 2 + 2)
                wait(pe, b_copied, n - B_BANKS + 1)
                for r in range(ng):
                    last = pe.matmul(b_ps[:, s % B_BANKS, r, :], sel[:, s * ng + r, :], bc16[q][:, :],
                                     start=True, stop=True)
                last.then_inc(b_done, 1)

            def c_broadcast(g, q, s):
                n = g * NS + s
                wait(pe, hc_ready, n - 1)
                for r in range(ng):
                    last = pe.matmul(c_ps[:, s % 2, r, :], sel[:, N_STATE + s * ng + r, :], bc16[q][:, :],
                                     start=True, stop=True)
                last.then_inc(c_done, 1)

            def state_sum(g, s):
                n = g * NS + s
                pe.wait_ge(hc_ready, n + 1)
                if s == 0:
                    wait(pe, evacuated, g)
                for j in range(J):
                    r, t = divmod(j, nd)
                    last = pe.matmul(y_ps[:, t, :], ident[:, :], hc[:, s % 2, j, :],
                                     start=s == 0 and r == 0, stop=s == NS - 1 and r == ng - 1)
                last.then_inc(summed, 1)

            def unit(g, q, first):
                o = 1 - q
                for s in range(NS):
                    if s + LEAD < NS:
                        b_broadcast(g, q, s + LEAD)
                    else:
                        b_broadcast(g + 1, o, s + LEAD - NS)
                    if s + 1 < NS:
                        c_broadcast(g, q, s + 1)
                    else:
                        c_broadcast(g + 1, o, 0)
                    if s:
                        state_sum(g, s - 1)
                    elif not first:
                        state_sum(g - 1, NS - 1)
                    if s == at["xproj"]:
                        xproj(g + 1, o, loads_of(g + 1, o))
                    for t in range(nd):
                        if s == at["dt"][t]:
                            dt(g + 1, o, t)

            pe.wait_ge(const_in, 32)
            pe.wait_ge(sel_ready, 1)
            xproj(0, 0, 16 * LOADS)
            for t in range(nd):
                dt(0, 0, t)
            for s in range(LEAD):
                b_broadcast(0, 0, s)
            c_broadcast(0, 0, 0)
            over_units(pe, unit)
            state_sum(units - 1, NS - 1)

        @block.scalar
        def _(act):
            act.preload_act_table_set("natural_log_exp_and_others")
            act.wait_ge(consts_set, 2)
            act.sem_inc(direct_ready, 2 * nd)

            def take_xproj(g, q, lw):
                act.wait_ge(loaded[q], lw)
                act.activation(negA[q][:, :], small[q][:, 2 * nd:], ACT.Exp).then_inc(negA_ready, 1)
                act.wait_ge(negA_ready, g * 3 + 1)
                act.activation(negA[q][:, :], negA[q][:, :], ACT.Copy, scale=-1.0).then_inc(negA_ready, 1)
                act.activation(keep_sb[q][:, :], keep_in[q][:, :], ACT.Copy).then_inc(negA_ready, 1)
                act.wait_ge(xproj_done, g + 1)
                act.activation(xd[:, :], prep_ps[0:XROWS + rank, :], ACT.Copy).then_inc(xd_ready, 1)
                act.activation(bc16[q][:, :], prep_ps[0:96, :], ACT.Copy).then_inc(prep_read, 1)

            def take_direct(g, q, t, stores):
                if t == 0:
                    wait(act, stored[q], stores)
                act.activation(yo[q][:, t, :], u[q][:, t, :], ACT.Copy, scale=D_of(q, t)).then_inc(direct_ready, 1)

            def take_dt(g, q, t):
                n = g * nd + t
                act.wait_ge(dt_done, n + 1)
                wait(act, delta_ready, n - nd + 1)
                act.activation(lnx[:, t, :], prep_ps[:, :], ACT.Abs, bias=bias_of(q, t)).then_inc(abs_done, 1)
                act.activation(relx[:, t, :], prep_ps[:, :], ACT.Relu, bias=bias_of(q, t)).then_inc(prep_read, 1)

            def take_ex(g, t):
                n = g * nd + t
                act.wait_ge(abs_done, n + 1)
                wait(act, log_ready, n - nd + 1)
                act.activation(ex[:, t, :], lnx[:, t, :], ACT.Exp, scale=-1.0).then_inc(ex_ready, 1)

            def take_series(g, t):
                n = g * nd + t
                act.wait_ge(ex_ready, n + 1)
                act.activation(near[:, t, :], ex[:, t, :], ACT.Square, scale=ROOT_A, bias=consts[:, 0:1]).then_inc(square_done, 1)
                act.activation(is_small[:, t, :], ex[:, t, :], ACT.Relu, scale=-1.0, bias=consts[:, 1:2]).then_inc(square_done, 1)

            def take_log(g, t):
                act.wait_ge(ex_ready, g * nd + t + 1)
                act.activation(lnx[:, t, :], ex[:, t, :], ACT.Ln, bias=1.0).then_inc(soft_done, 1)

            def copy_b(g, s):
                n = g * NS + s
                act.wait_ge(b_done, n + 1)
                wait(act, dbu_ready, n - AHEAD + 1)
                act.activation(b_sb[:, s % AHEAD, :, :], b_ps[:, s % B_BANKS, :, :], ACT.Copy).then_inc(b_copied, 1)

            def decay(g, q, s, j):
                r, t = divmod(j, nd)
                n = (g * NS + s) * J + j
                if s == 0 and j == 0:
                    act.wait_ge(delta_ready, (g + 1) * nd)
                    act.wait_ge(negA_ready, g * 3 + 3)
                wait(act, scanned, n - DECAYS + 1)
                a = t * N_STATE + s * ng + r
                act.activation(dA[:, (s * J + j) % DECAYS, :], delta[q][:, t, :], ACT.Exp,
                               scale=negA[q][:, a:a + 1]).then_inc(dA_ready, 1)

            def save_states(g, q, i):
                act.wait_ge(scanned, (g * NS + (i + 1) * GROUP) * J)
                slots = slice(i % 2 * GROUP, (i % 2 + 1) * GROUP)
                act.activation(state[:, i * GROUP:(i + 1) * GROUP, :], h[:, slots, :, T - 1], ACT.Copy,
                               scale=keep_sb[q][:, 0:1]).then_inc(state_saved, 1)

            def store(g, q):
                act.wait_ge(evacuated, g + 1)
                act.dma_start(Y[g], yo[q][:, :, :]).then_inc(stored[q], 16)

            def unit(g, q, first):
                o = 1 - q
                for s in range(NS):
                    if s == 1 and not first:
                        save_states(g - 1, o, GROUPS - 1)
                    elif s > 1 and s % GROUP == 1:
                        save_states(g, q, s // GROUP - 1)
                    for j in range(J):
                        decay(g, q, s, j)
                    if s + COPY_LEAD < NS:
                        copy_b(g, s + COPY_LEAD)
                    else:
                        copy_b(g + 1, s + COPY_LEAD - NS)
                    if s == at["take"]:
                        take_xproj(g + 1, o, loads_of(g + 1, o))
                    for t in range(nd):
                        if s == at["take_dt"][t]:
                            take_dt(g + 1, o, t)
                        if s == at["ex"][t]:
                            take_ex(g + 1, t)
                        if s == at["series"][t]:
                            take_series(g + 1, t)
                        if s == at["log"][t]:
                            take_log(g + 1, t)
                        if s == at["direct"][t]:
                            take_direct(g + 1, o, t, earlier_stores(g + 1, o))
                    if s == 4 and not first:
                        store(g - 1, o)

            act.wait_ge(sel_ready, 1)
            take_xproj(0, 0, 16 * LOADS)
            for t in range(nd):
                take_dt(0, 0, t)
            for t in range(nd):
                take_ex(0, t)
            for t in range(nd):
                take_series(0, t)
                take_log(0, t)
                take_direct(0, 0, t, 0)
            for s in range(COPY_LEAD):
                copy_b(0, s)
            over_units(act, unit)
            save_states(units - 1, 1, GROUPS - 1)
            store(units - 1, 1)

        @block.gpsimd
        def _(pool):
            pool.sem_inc(du_ready, 2 * nd)

            def input_of(g, q, s):
                n = g * NS + s
                pool.wait_ge(b_copied, n + 1)
                if s == 0:
                    pool.wait_ge(du_ready, (g + 3) * nd)
                wait(pool, scanned, (n - AHEAD + 1) * J)
                a, b = du[q][:, :, :], b_sb[:, s % AHEAD, :, :]
                a, b = (a, b.broadcast_to([128, nd, T])) if ng == 1 else (a.broadcast_to([128, ng, T]), b)
                pool.tensor_tensor(dbu[:, s % AHEAD, :, :], a, b, ALU.mult).then_inc(dbu_ready, 1)

            def take_delta(g, q, t):
                n = g * nd + t
                pool.wait_ge(log_ready, n + 1)
                pool.wait_ge(prep_read, g * (1 + nd) + 2 + t)
                if t == 0:
                    wait(pool, dA_ready, (g - 1) * NS * J)
                    wait(pool, dbu_ready, (g - 1) * NS)
                pool.tensor_tensor(delta[q][:, t, :], relx[:, t, :], lnx[:, t, :], ALU.add).then_inc(delta_ready, 1)
                pool.wait_ge(delta_ready, n + 1)
                pool.tensor_tensor(du[q][:, t, :], delta[q][:, t, :], u[q][:, t, :], ALU.mult).then_inc(du_ready, 1)

            def unit(g, q, first):
                for s in range(1, NS):
                    input_of(g, q, s)
                    for t in range(nd):
                        if s == at["delta"][t]:
                            take_delta(g + 1, 1 - q, t)
                input_of(g + 1, 1 - q, 0)

            for t in range(nd):
                take_delta(0, 0, t)
            input_of(0, 0, 0)
            over_units(pool, unit)

        @block.vector
        def _(dve):
            dve.wait_ge(const_in, 32)
            dve.memset(consts[:, 0:1], -ROOT_B).then_inc(consts_set, 1)
            dve.memset(consts[:, 1:2], SMALL).then_inc(consts_set, 1)
            dve.tensor_copy(sel[:, :, :].rearrange("p a b -> p (a b)"), self32).then_inc(sel_ready, 1)

            def take_rest1(g, q):
                dve.wait_ge(prep_read, g * (1 + nd) + 1)
                dve.wait_ge(xd_ready, g + 1)
                dve.tensor_tensor(rest1[:, :], xd[0:96, :], bc16[q][:, :], ALU.subtract).then_inc(rests, 1)

            def take_mid(g, q):
                dve.wait_ge(rests, g * 2 + 1)
                dve.tensor_copy(mid16[:, :], rest1[:, :]).then_inc(mid_ready, 1)
                dve.tensor_copy(bc16[q][32:64, :], rest1[32:64, :]).then_inc(bc_ready, 1)

            def take_rest2(g, q):
                dve.wait_ge(mid_ready, g + 1)
                dve.tensor_tensor(rest2[:, :], rest1[:, :], mid16[:, :], ALU.subtract).then_inc(rests, 1)

            def take_low(g, q):
                dve.wait_ge(rests, g * 2 + 2)
                dve.tensor_copy(bc16[q][64:96, :], rest2[64:96, :]).then_inc(bc_ready, 1)

            def take_near(g, t):
                n = g * nd + t
                dve.wait_ge(square_done, 2 * n + 2)
                dve.scalar_tensor_tensor(near[:, t, :], near[:, t, :], ROOT_C, ex[:, t, :],
                                         ALU.add, ALU.mult).then_inc(near_ready, 1)

            def pick(g, t):
                n = g * nd + t
                dve.wait_ge(near_ready, n + 1)
                dve.wait_ge(soft_done, n + 1)
                dve.sem_inc(passed, 1)
                dve.copy_predicated(lnx[:, t, :], is_small[:, t, :].bitcast(mybir.dt.uint32),
                                    near[:, t, :]).then_inc(log_ready, 1)

            def scan(g, q, s, j, initial):
                n = g * NS + s
                if j == 0:
                    dve.wait_ge(dbu_ready, n + 1)
                    wait(dve, hc_ready, n - 2 * GROUP + 1)
                    if s % GROUP == 0:
                        wait(dve, state_saved, g * GROUPS + s // GROUP - 1)
                dve.wait_ge(dA_ready, n * J + j + 1)
                dve.tensor_tensor_scan(h[:, s % (2 * GROUP), j, :], dA[:, (s * J + j) % DECAYS, :],
                                       dbu[:, s % AHEAD, j, :], initial, ALU.mult, ALU.add).then_inc(scanned, 1)

            def times_c(g, s):
                n = g * NS + s
                dve.wait_ge(scanned, (n + 1) * J)
                dve.wait_ge(c_done, n + 1)
                wait(dve, summed, n - 1)
                c = c_ps[:, s % 2, :, :]
                if ng == 1:
                    c = c.broadcast_to([128, nd, T])
                dve.tensor_tensor(hc[:, s % 2, :, :], h[:, s % (2 * GROUP), :, :], c, ALU.mult).then_inc(hc_ready, 1)

            def evacuate(g, q):
                dve.wait_ge(direct_ready, (g + 3) * nd)
                dve.wait_ge(summed, (g + 1) * NS)
                dve.tensor_tensor(yo[q][:, :, :], yo[q][:, :, :], y_ps[:, :, :], ALU.add).then_inc(evacuated, 1)

            def unit(g, q, first):
                o = 1 - q
                for s in range(NS):
                    for j in range(J):
                        scan(g, q, s, j, 0.0 if first else state[:, s, j:j + 1])
                        if j == 0 and s:
                            times_c(g, s - 1)
                        elif j == 0 and not first:
                            times_c(g - 1, NS - 1)
                        if j == 1 and s == 1 and not first:
                            evacuate(g - 1, o)
                    if s == at["rest1"]:
                        take_rest1(g + 1, o)
                    if s == at["mid"]:
                        take_mid(g + 1, o)
                    if s == at["rest2"]:
                        take_rest2(g + 1, o)
                    if s == at["low"]:
                        take_low(g + 1, o)
                    for t in range(nd):
                        if s == at["near"][t]:
                            take_near(g + 1, t)
                        if s == at["pick"][t]:
                            pick(g + 1, t)

            take_rest1(0, 0)
            take_mid(0, 0)
            take_rest2(0, 0)
            take_low(0, 0)
            for t in range(nd):
                take_near(0, t)
                pick(0, t)
            over_units(dve, unit)
            times_c(units - 1, NS - 1)
            evacuate(units - 1, 1)


def layer0_output(nc, Y, x, x1, ln_in, ln_w_in, ln_b_in, w_out_in):
    fp32 = mybir.dt.float32
    Yv = Y.rearrange("(b k c) p t j -> b k t p c j", b=B, k=K0)
    with ExitStack() as ctx:
        ctx.enter_context(nc.cleanup_on_exit())
        def sb(n, s, dt=fp32):
            return ctx.enter_context(nc.sbuf_tensor(f"m0_{n}", s, dt))

        def pb(n, s):
            return ctx.enter_context(nc.psum_tensor(f"m0_{n}", s, fp32))

        def sem(n):
            return nc.alloc_semaphore(f"m0_{n}")

        yk = [sb(f"y{k}", [128, L]) for k in range(K0)]
        ysum = sb("ysum", [128, ND0, L])
        xin = sb("xin", [HALF, 2, L])
        cen, sq = sb("cen", [128, 2, ND0, T]), sb("sq", [128, ND0, T])
        yn = sb("yn", [128, ND0, T])
        lnv, rstd = sb("lnv", [128, T]), sb("rstd", [128, T])
        res = sb("res", [HALF, 2, 2, T])
        ones, w_out = sb("ones", [128, 128]), sb("w_out", [128, ND0, CH])
        ln_w, ln_b, eps = sb("ln_w", [128, ND0]), sb("ln_b", [128, ND0]), sb("eps", [128, 1])
        mean_ps, var_ps, out_ps = pb("mean_ps", [128, 2, T]), pb("var_ps", [128, 2, T]), pb("out_ps", [HALF, 2, 2, T])

        const_in, x_in, passed = sem("const_in"), sem("x_in"), sem("passed")
        y_in = [sem(f"y_in{k}") for k in range(K0)]
        rows_added, cols_added, sum_ready = sem("rows_added"), sem("cols_added"), sem("sum_ready")
        mean_done, cen_ready, sq_ready, var_done = sem("mean_done"), sem("cen_ready"), sem("sq_ready"), sem("var_done")
        lnv_ready, rstd_ready, scaled = sem("lnv_ready"), sem("rstd_ready"), sem("scaled")
        yn_ready, out_done, res_ready, eps_set = sem("yn_ready"), sem("out_done"), sem("res_ready"), sem("eps_set")
        stored = [sem(f"stored{p}") for p in range(2)]
        block = ctx.enter_context(nc.Block())

        @block.sync
        def _(sp):
            for dst, src in ((ones[:, :], ln_in), (w_out[:, :, :], w_out_in), (ln_w[:, :], ln_w_in), (ln_b[:, :], ln_b_in)):
                sp.dma_start(dst, src).then_inc(const_in, 16)

            def image(b):
                for t in range(ND0):
                    n = b * ND0 + t
                    for k in (1, 3, 0, 2):
                        wait(sp, sum_ready if k < 2 else rows_added if k == 2 else cols_added, n)
                        sp.sem_inc(passed, 1)
                        sp.dma_start(yk[k][:, :].rearrange("p (c j) -> p c j", j=T), Yv[b, k, t]).then_inc(y_in[k], 16)
                    if t == 0:
                        wait(sp, res_ready, b * NCHUNK)
                        sp.dma_start(xin[:, :, :], x[b]).then_inc(x_in, 16)

            over_batches(sp, image)
            for p in range(2):
                sp.wait_ge(stored[p], 16 * B * NCHUNK // 2)

        def lagged(body, lag):
            for c in range(NCHUNK + lag):
                body(c)

        @block.tensor
        def _(pe):
            pe.wait_ge(const_in, 64)

            def mean(b, c):
                m = b * NCHUNK + c
                wait(pe, cen_ready, m - 1)
                for t in range(ND0):
                    last = pe.matmul(mean_ps[:, c % 2, :], ones[:, :], ysum[:, t, c * T:(c + 1) * T],
                                     start=t == 0, stop=t == ND0 - 1)
                last.then_inc(mean_done, 1)

            def variance(b, c):
                m = b * NCHUNK + c
                pe.wait_ge(sq_ready, m + 1)
                wait(pe, rstd_ready, m - 1)
                for t in range(ND0):
                    last = pe.matmul(var_ps[:, c % 2, :], ones[:, :], sq[:, t, :], start=t == 0, stop=t == ND0 - 1)
                last.then_inc(var_done, 1)

            def project(b, c):
                m = b * NCHUNK + c
                pe.wait_ge(yn_ready, m + 1)
                wait(pe, res_ready, m - 1)
                for half in range(2):
                    for t in range(ND0):
                        last = pe.matmul(out_ps[:, c % 2, half, :], w_out[:, t, half * HALF:(half + 1) * HALF],
                                         yn[:, t, :], start=t == 0, stop=t == ND0 - 1)
                last.then_inc(out_done, 1)

            def image(b):
                pe.wait_ge(sum_ready, (b + 1) * ND0)
                for c in range(NCHUNK + 2):
                    if c < NCHUNK:
                        mean(b, c)
                    if 1 <= c <= NCHUNK:
                        variance(b, c - 1)
                    if c >= 2:
                        project(b, c - 2)

            over_batches(pe, image)

        @block.scalar
        def _(act):
            act.wait_ge(const_in, 64)
            act.wait_ge(eps_set, 1)

            def squares(b, c):
                m = b * NCHUNK + c
                act.wait_ge(cen_ready, m + 1)
                wait(act, var_done, m)
                act.activation(sq[:, :, :], cen[:, c % 2, :, :], ACT.Square).then_inc(sq_ready, 1)

            def root(b, c):
                m = b * NCHUNK + c
                act.wait_ge(var_done, m + 1)
                act.activation(lnv[:, :], var_ps[:, c % 2, :], ACT.Ln, bias=eps[:, :]).then_inc(lnv_ready, 1)
                act.wait_ge(lnv_ready, m + 1)
                wait(act, scaled, m)
                act.activation(rstd[:, :], lnv[:, :], ACT.Exp, scale=-0.5).then_inc(rstd_ready, 1)

            def affine(b, c):
                m = b * NCHUNK + c
                act.wait_ge(scaled, m + 1)
                wait(act, out_done, m)
                for t in range(ND0):
                    last = act.activation(yn[:, t, :], cen[:, c % 2, t, :], ACT.Identity,
                                          scale=ln_w[:, t:t + 1], bias=ln_b[:, t:t + 1])
                last.then_inc(yn_ready, 1)

            def store(b, c):
                m = b * NCHUNK + c
                act.wait_ge(res_ready, m + 1)
                act.dma_start(x1[b][:, :, c * T:(c + 1) * T], res[:, c % 2, :, :]).then_inc(stored[c % 2], 16)

            def image(b):
                for c in range(NCHUNK + 3):
                    if c < NCHUNK:
                        squares(b, c)
                    if 1 <= c <= NCHUNK:
                        root(b, c - 1)
                        affine(b, c - 1)
                    if c >= 3:
                        store(b, c - 3)

            over_batches(act, image)

        @block.vector
        def _(dve):
            dve.memset(eps[:, :], LN_EPS).then_inc(eps_set, 1)

            def add_rows(b, t):
                n = b * ND0 + t
                dve.wait_ge(y_in[0], (n + 1) * 16)
                dve.wait_ge(y_in[2], (n + 1) * 16)
                dve.tensor_tensor(yk[0][:, :], yk[0][:, :], yk[2][:, ::-1], ALU.add).then_inc(rows_added, 1)

            def add_columns(b, t):
                n = b * ND0 + t
                dve.wait_ge(rows_added, n + 1)
                dve.wait_ge(cols_added, n + 1)
                wait(dve, cen_ready, b * NCHUNK)
                dve.tensor_tensor(ysum[:, t, :].rearrange("p (h w) -> p h w", w=W),
                                  yk[0][:, :].rearrange("p (h w) -> p h w", w=W),
                                  yk[1][:, :].rearrange("p (w h) -> p h w", h=H), ALU.add).then_inc(sum_ready, 1)

            def centre(b, c):
                m = b * NCHUNK + c
                dve.wait_ge(mean_done, m + 1)
                wait(dve, yn_ready, m - 1)
                dve.tensor_tensor(cen[:, c % 2, :, :], ysum[:, :, c * T:(c + 1) * T],
                                  mean_ps[:, c % 2, :].unsqueeze(1).broadcast_to([128, ND0, T]),
                                  ALU.subtract).then_inc(cen_ready, 1)

            def scale(b, c):
                m = b * NCHUNK + c
                dve.wait_ge(rstd_ready, m + 1)
                dve.wait_ge(sq_ready, m + 1)
                dve.wait_ge(cen_ready, m + 1)
                dve.tensor_tensor(cen[:, c % 2, :, :], cen[:, c % 2, :, :],
                                  rstd[:, :].unsqueeze(1).broadcast_to([128, ND0, T]), ALU.mult).then_inc(scaled, 1)

            def residual(b, c):
                m = b * NCHUNK + c
                dve.wait_ge(out_done, m + 1)
                wait(dve, stored[c % 2], b * (16 * NCHUNK // 2) + (c // 2) * 16)
                dve.tensor_tensor(res[:, c % 2, :, :], out_ps[:, c % 2, :, :], xin[:, :, c * T:(c + 1) * T],
                                  ALU.add).then_inc(res_ready, 1)

            def image(b):
                for t in range(ND0):
                    add_rows(b, t)
                    add_columns(b, t)
                dve.wait_ge(x_in, (b + 1) * 16)
                for c in range(NCHUNK + 2):
                    if c < NCHUNK:
                        centre(b, c)
                    if 1 <= c <= NCHUNK:
                        scale(b, c - 1)
                    if c >= 2:
                        residual(b, c - 2)

            over_batches(dve, image)

        @block.gpsimd
        def _(pool):
            def image(b):
                for t in range(ND0):
                    n = b * ND0 + t
                    pool.wait_ge(y_in[1], (n + 1) * 16)
                    pool.wait_ge(y_in[3], (n + 1) * 16)
                    pool.tensor_tensor(yk[1][:, :], yk[1][:, :], yk[3][:, ::-1], ALU.add).then_inc(cols_added, 1)

            over_batches(pool, image)


def layer1_features(nc, x1, U, Z, XN, gmat_in, w_pair_in, w_third_in, conv_b_in, ones_in, ln_w_in, ln_b_in,
                    w_in_in, w_conv_in, conv1d_b_in):
    fp32 = mybir.dt.float32
    Uv = U.rearrange("(b r c) p o j -> b r p (o c) j", b=B, r=NBR)
    Zv = Z.rearrange("(b r c) p o j -> b r p (o c) j", b=B, r=NBR)
    with ExitStack() as ctx:
        ctx.enter_context(nc.cleanup_on_exit())
        def sb(n, s, dt=fp32):
            return ctx.enter_context(nc.sbuf_tensor(f"f1_{n}", s, dt))

        def pb(n, s):
            return ctx.enter_context(nc.psum_tensor(f"f1_{n}", s, fp32))

        def sem(n):
            return nc.alloc_semaphore(f"f1_{n}")

        xin = sb("xin", [HALF, 2, L])
        pad = sb("pad", [HALF, 2, H + 2, W + 2])
        seq = sb("seq", [128, 2, 2, T])
        cen = sb("cen", [128, 2, 2, T])
        sq_sb = sb("sq_sb", [128, 2, T])
        lnr, rstd_sb = sb("lnr", [128, 2, T]), sb("rstd_sb", [128, 2, T])
        xn = sb("xn", [128, 2, DCONV - 1 + L])
        u_sb, z_sb = sb("u_sb", [128, 2, L // 2]), sb("z_sb", [128, 2, L // 2])
        gmat, ones = sb("gmat", [HALF, HALF]), sb("ones", [128, 128])
        w_pair, w_third = sb("w_pair", [HALF, 2, TAPS, 2 * CB]), sb("w_third", [HALF, 2, TAPS, CB])
        w_in, w_conv = sb("w_in", [128, 2 * D1]), sb("w_conv", [128, DCONV, D1])
        w_fold = sb("w_fold", [128, DCONV, D1])
        conv_b, conv1d_b = sb("conv_b", [128, 1]), sb("conv1d_b", [128, 1])
        ln_w, ln_b, eps = sb("ln_w", [128, 2]), sb("ln_b", [128, 2]), sb("eps", [128, 1])
        stats, mv = sb("stats", [HALF, 2, NCHUNK, 6]), sb("mv", [HALF, 2, 2])
        packed, sq = sb("packed", [HALF, 4]), sb("sq", [HALF, 2])
        gm, sq2, var, lnv, rstd = (sb("gm", [HALF, 4]), sb("sq2", [HALF, 2]), sb("var", [HALF, 2]),
                                   sb("lnv", [HALF, 2]), sb("rstd", [HALF, 2]))
        conv_ps = pb("conv_ps", [128, 2, T])
        stat_ps = pb("stat_ps", [128, 2, T])
        proj_ps = pb("proj_ps", [128, 3, T])
        g_ps = pb("g_ps", [HALF, 4])

        const_in, x_in, setup, passed = sem("const_in"), sem("x_in"), sem("setup"), sem("passed")
        stat_steps, g_done, scale_steps = sem("stat_steps"), sem("g_done"), sem("scale_steps")
        lnv_ready, rstd_ready, pad_ready = sem("lnv_ready"), sem("rstd_ready"), sem("pad_ready")
        conv_done, seq_ready, mean_done, cen_ready = sem("conv_done"), sem("seq_ready"), sem("mean_done"), sem("cen_ready")
        sq_ready, var_done, lnr_ready, root_ready = sem("sq_ready"), sem("var_done"), sem("lnr_ready"), sem("root_ready")
        scaled, xn_ready = sem("scaled"), sem("xn_ready")
        proj_done, proj_read = sem("proj_done"), sem("proj_read")
        xn_stored = sem("xn_stored")
        u_stored = [sem(f"u_stored{p}") for p in range(2)]
        z_stored = [sem(f"z_stored{p}") for p in range(2)]
        block = ctx.enter_context(nc.Block())
        PARTS = 2 * NBR
        PC = NCHUNK // 2

        def over_parts(body):
            for r in range(NBR):
                for hf in range(2):
                    body(r, hf)

        @block.sync
        def _(sp):
            for dst, src in ((gmat[:, :], gmat_in), (ones[:, :], ones_in), (w_pair[:, :, :, :], w_pair_in),
                             (w_third[:, :, :, :], w_third_in), (w_in[:, :], w_in_in), (w_conv[:, :, :], w_conv_in),
                             (conv_b[:, :], conv_b_in), (conv1d_b[:, :], conv1d_b_in), (ln_w[:, :], ln_w_in),
                             (ln_b[:, :], ln_b_in)):
                sp.dma_start(dst, src).then_inc(const_in, 16)
            sp.dma_start(xin[:, :, :], x1[0]).then_inc(x_in, 16)

            def image(b):
                if not is_last(b):
                    sp.wait_ge(pad_ready, b + 1)
                    sp.dma_start(xin[:, :, :], x1[b + 1]).then_inc(x_in, 16)
                sp.wait_ge(xn_ready, (b + 1) * NCHUNK)
                sp.dma_start(XN[b], xn[:, :, DCONV - 1:]).then_inc(xn_stored, 16)

                def part(r, hf):
                    i = r * 2 + hf
                    sp.wait_ge(proj_read, ((b * PARTS) + i + 1) * 2 * PC)
                    sp.dma_start(Uv[b, r][:, hf * PC:(hf + 1) * PC, :],
                                 u_sb[:, i % 2, :].rearrange("p (c j) -> p c j", j=T)).then_inc(u_stored[i % 2], 16)
                    sp.dma_start(Zv[b, r][:, hf * PC:(hf + 1) * PC, :],
                                 z_sb[:, i % 2, :].rearrange("p (c j) -> p c j", j=T)).then_inc(z_stored[i % 2], 16)

                over_parts(part)

            over_batches(sp, image)
            sp.wait_ge(xn_stored, 16 * B)
            for p in range(2):
                sp.wait_ge(u_stored[p], 16 * B * PARTS // 2)
                sp.wait_ge(z_stored[p], 16 * B * PARTS // 2)

        @block.tensor
        def _(pe):
            pe.wait_ge(const_in, 160)
            pe.wait_ge(setup, 5)

            def group_means(b):
                pe.wait_ge(stat_steps, (b + 1) * STATS_STEPS)
                pe.matmul(g_ps[:, :], gmat[:, :], packed[:, :], start=True, stop=True).then_inc(g_done, 1)

            def conv(b, c):
                m = b * NCHUNK + c
                wait(pe, seq_ready, m)
                for w, slot, rows in ((w_pair, 0, 2 * CB), (w_third, 1, CB)):
                    for half in range(2):
                        for k in range(TAPS):
                            dy, dx = divmod(k, 3)
                            last = pe.matmul(conv_ps[0:rows, slot, :], w[:, half, k, :],
                                             pad[:, half, c * ROWS + dy:c * ROWS + dy + ROWS, dx:dx + W],
                                             start=half == 0 and k == 0, stop=half == 1 and k == TAPS - 1)
                last.then_inc(conv_done, 1)

            def mean(b, c):
                m = b * NCHUNK + c
                pe.wait_ge(seq_ready, m + 1)
                wait(pe, lnr_ready, m)
                for slot in range(2):
                    last = pe.matmul(stat_ps[:, slot, :], ones[:, :], seq[:, c % 2, slot, :], start=True, stop=True)
                last.then_inc(mean_done, 1)

            def variance(b, c):
                m = b * NCHUNK + c
                pe.wait_ge(sq_ready, m + 1)
                for slot in range(2):
                    last = pe.matmul(stat_ps[:, slot, :], ones[:, :], sq_sb[:, slot, :], start=True, stop=True)
                last.then_inc(var_done, 1)

            def project(b, r, hf):
                lo, slot = (CB if r == 1 else 0), (1 if r == 2 else 0)
                for c in range(PC):
                    m = (b * PARTS + r * 2 + hf) * 2 * PC + 2 * c
                    first = (hf * PC + c) * T
                    wait(pe, proj_read, m - 2)
                    bank = ((r * 2 + hf) * 2 * PC + 2 * c) % 3
                    for k in range(DCONV):
                        last = pe.matmul(proj_ps[:, bank, :], w_fold[lo:lo + CB, k, :],
                                         xn[lo:lo + CB, slot, first + k:first + k + T],
                                         start=k == 0, stop=k == DCONV - 1)
                    last.then_inc(proj_done, 1)
                    wait(pe, proj_read, m - 1)
                    bank = ((r * 2 + hf) * 2 * PC + 2 * c + 1) % 3
                    first += DCONV - 1
                    pe.matmul(proj_ps[:, bank, :], w_in[lo:lo + CB, D1:], xn[lo:lo + CB, slot, first:first + T],
                              start=True, stop=True).then_inc(proj_done, 1)

            def image(b):
                pe.wait_ge(pad_ready, b + 1)
                for c in range(NCHUNK + 1):
                    if c < NCHUNK:
                        conv(b, c)
                    if c >= 1:
                        mean(b, c - 1)
                        variance(b, c - 1)
                if not is_last(b):
                    group_means(b + 1)
                pe.wait_ge(xn_ready, (b + 1) * NCHUNK)
                over_parts(lambda r, hf: project(b, r, hf))

            group_means(0)
            over_batches(pe, image)

        @block.scalar
        def _(act):
            act.wait_ge(const_in, 160)
            act.wait_ge(setup, 5)

            def scale(b):
                act.wait_ge(scale_steps, b * SCALE_STEPS + 4)
                inverse_root(act, lnv[:, :], rstd[:, :], var[:, :], lnv_ready, b + 1).then_inc(rstd_ready, 1)

            def take_conv(b, c):
                m = b * NCHUNK + c
                act.wait_ge(conv_done, m + 1)
                wait(act, cen_ready, m - 1)
                src = conv_ps[:, :, :].rearrange("p s (r w) -> p s r w", w=W)
                dst = seq[:, c % 2, :, :].rearrange("p s (r w) -> p s r w", w=W)
                act.activation(dst[0:CB, 0], src[0:CB, 0], ACT.Identity, bias=conv_b[0:CB, :])
                act.activation(dst[CB:, 0], src[CB:, 0][:, :, ::-1], ACT.Identity, bias=conv_b[CB:, :])
                act.activation(dst[0:CB, 1], src[0:CB, 1][:, ::-1, :], ACT.Identity,
                               bias=conv_b[0:CB, :]).then_inc(seq_ready, 1)

            def squares(b, c):
                m = b * NCHUNK + c
                act.wait_ge(cen_ready, m + 1)
                wait(act, var_done, m)
                act.activation(sq_sb[:, :, :], cen[:, c % 2, :, :], ACT.Square).then_inc(sq_ready, 1)

            def root(b, c):
                m = b * NCHUNK + c
                act.wait_ge(var_done, m + 1)
                act.activation(lnr[:, :, :], stat_ps[:, :, :], ACT.Ln, bias=eps[:, :]).then_inc(lnr_ready, 1)
                act.wait_ge(lnr_ready, m + 1)
                wait(act, scaled, m)
                act.activation(rstd_sb[:, :, :], lnr[:, :, :], ACT.Exp, scale=-0.5).then_inc(root_ready, 1)

            def affine(b, c):
                m = b * NCHUNK + c
                act.wait_ge(scaled, m + 1)
                if c == 0:
                    wait(act, xn_stored, b * 16)
                    wait(act, proj_done, b * PARTS * 2 * PC)
                for slot, at in ((0, c), (1, NCHUNK - 1 - c)):
                    first = DCONV - 1 + at * T
                    last = act.activation(xn[:, slot, first:first + T], cen[:, c % 2, slot, :], ACT.Identity,
                                          scale=ln_w[:, slot:slot + 1], bias=ln_b[:, slot:slot + 1])
                last.then_inc(xn_ready, 1)

            def take_proj(b, r, hf):
                i = r * 2 + hf
                stores = b * (PARTS // 2) + r
                wait(act, u_stored[i % 2], stores * 16)
                wait(act, z_stored[i % 2], stores * 16)
                for c in range(PC):
                    m = (b * PARTS + i) * 2 * PC + 2 * c
                    base = i * 2 * PC + 2 * c
                    act.wait_ge(proj_done, m + 1)
                    act.activation(u_sb[:, i % 2, c * T:(c + 1) * T], proj_ps[:, base % 3, :], ACT.Silu,
                                   bias=conv1d_b[:, :]).then_inc(proj_read, 1)
                    act.wait_ge(proj_done, m + 2)
                    act.activation(z_sb[:, i % 2, c * T:(c + 1) * T], proj_ps[:, (base + 1) % 3, :],
                                   ACT.Silu).then_inc(proj_read, 1)

            def image(b):
                for c in range(NCHUNK + 1):
                    if c < NCHUNK:
                        take_conv(b, c)
                    if c >= 1:
                        squares(b, c - 1)
                        root(b, c - 1)
                        affine(b, c - 1)
                if not is_last(b):
                    scale(b + 1)
                over_parts(lambda r, hf: take_proj(b, r, hf))

            scale(0)
            over_batches(act, image)

        @block.vector
        def _(dve):
            dve.wait_ge(const_in, 160)
            dve.memset(eps[:, :], LN_EPS).then_inc(setup, 1)
            dve.memset(pad[:, :, :, :], 0.0).then_inc(setup, 1)
            dve.memset(seq[CB:, :, 1, :], 0.0).then_inc(setup, 1)
            dve.memset(xn[:, :, 0:DCONV - 1], 0.0).then_inc(setup, 1)
            for k in range(DCONV):
                last = dve.tensor_tensor(w_fold[:, k, :], w_in[:, 0:D1], w_conv[:, k, :], ALU.mult)
            last.then_inc(setup, 1)

            def measure(b):
                dve.wait_ge(x_in, (b + 1) * 16)
                wait(dve, g_done, b)
                group_stats(dve, b, xin, stats, mv, packed, sq, stat_steps, passed)

            def normalise(b):
                dve.wait_ge(g_done, b + 1)
                group_variance(dve, b, g_ps, gm, sq2, var, scale_steps)
                dve.wait_ge(rstd_ready, b + 1)
                dve.wait_ge(scale_steps, b * SCALE_STEPS + 4)
                dve.wait_ge(setup, 5)
                wait(dve, conv_done, b * NCHUNK)
                for half in range(2):
                    last = dve.tensor_scalar(pad[:, half, 1:1 + H, 1:1 + W],
                                             xin[:, half, :].rearrange("p (h w) -> p h w", w=W),
                                             gm[:, half:half + 1], rstd[:, half:half + 1], ALU.subtract, ALU.mult)
                last.then_inc(pad_ready, 1)

            def centre(b, c):
                m = b * NCHUNK + c
                dve.wait_ge(mean_done, m + 1)
                wait(dve, xn_ready, m - 1)
                dve.tensor_tensor(cen[:, c % 2, :, :], seq[:, c % 2, :, :], stat_ps[:, :, :],
                                  ALU.subtract).then_inc(cen_ready, 1)

            def scale(b, c):
                m = b * NCHUNK + c
                dve.wait_ge(root_ready, m + 1)
                dve.wait_ge(cen_ready, m + 1)
                dve.tensor_tensor(cen[:, c % 2, :, :], cen[:, c % 2, :, :], rstd_sb[:, :, :],
                                  ALU.mult).then_inc(scaled, 1)

            def image(b):
                for c in range(NCHUNK):
                    centre(b, c)
                    scale(b, c)
                if not is_last(b):
                    measure(b + 1)
                    normalise(b + 1)

            measure(0)
            normalise(0)
            over_batches(dve, image)


def layer1_output(nc, Y, Z, XN, x1, out, skip_in, w_out_in, mean_in, ln_w_in, ln_b_in, w_proj_in, proj_b_in):
    fp32 = mybir.dt.float32
    Yv = Y.rearrange("(b r c) p o j -> b c p (o r) j", b=B, r=NBR)
    Zv = Z.rearrange("(b r c) p o j -> b c p (o r) j", b=B, r=NBR)
    out_v = out.rearrange("b (s p) l -> b p s l", p=HALF)
    with ExitStack() as ctx:
        ctx.enter_context(nc.cleanup_on_exit())
        def sb(n, s, dt=fp32):
            return ctx.enter_context(nc.sbuf_tensor(f"m1_{n}", s, dt))

        def pb(n, s):
            return ctx.enter_context(nc.psum_tensor(f"m1_{n}", s, fp32))

        def sem(n):
            return nc.alloc_semaphore(f"m1_{n}")

        yb, zb, gated = sb("yb", [128, 2, NBR, T]), sb("zb", [128, 2, NBR, T]), sb("gated", [128, 2, NBR, T])
        xnb, x1b = sb("xnb", [128, 4, 2, T]), sb("x1b", [HALF, 4, 2, T])
        v, cen, sq = sb("v", [128, 2, 2, T]), sb("cen", [128, 2, 2, T]), sb("sq", [128, 2, T])
        yn = sb("yn", [128, 2, T])
        lnv, rstd = sb("lnv", [128, T]), sb("rstd", [128, T])
        res = sb("res", [HALF, 2, 2, T])
        skip, w_out, mean_w = sb("skip", [128, 1]), sb("w_out", [128, 2, 2 * CB]), sb("mean_w", [128, 2, 128])
        ln_w, ln_b, eps = sb("ln_w", [128, 2]), sb("ln_b", [128, 2]), sb("eps", [128, 1])
        w_proj, proj_b = sb("w_proj", [128, 2, CH]), sb("proj_b", [HALF, 2])
        op_ps, mean_ps, var_ps = pb("op_ps", [128, 2, T]), pb("mean_ps", [128, T]), pb("var_ps", [128, T])
        out_ps = pb("out_ps", [HALF, 2, 2, T])

        const_in, eps_set = sem("const_in"), sem("eps_set")
        yz_in = [sem(f"yz_in{p}") for p in range(2)]
        x_in = [sem(f"x_in{p}") for p in range(4)]
        gated_ready, op_done, v_ready, mean_done, cen_ready = (
            sem("gated_ready"), sem("op_done"), sem("v_ready"), sem("mean_done"), sem("cen_ready"))
        sq_ready, var_done, lnv_ready, rstd_ready, scaled = (
            sem("sq_ready"), sem("var_done"), sem("lnv_ready"), sem("rstd_ready"), sem("scaled"))
        yn_ready, out_done, res_ready = sem("yn_ready"), sem("out_done"), sem("res_ready")
        stored = [sem(f"stored{p}") for p in range(2)]
        block = ctx.enter_context(nc.Block())
        CONSTS = 16 * 7

        @block.sync
        def _(sp):
            for dst, src in ((skip[:, :], skip_in), (w_out[:, :, :], w_out_in), (mean_w[:, :, :], mean_in),
                             (ln_w[:, :], ln_w_in), (ln_b[:, :], ln_b_in), (w_proj[:, :, :], w_proj_in),
                             (proj_b[:, :], proj_b_in)):
                sp.dma_start(dst, src).then_inc(const_in, 16)

            def image(b):
                for c in range(NCHUNK):
                    m = b * NCHUNK + c
                    wait(sp, gated_ready, m - 1)
                    sp.dma_start(yb[:, c % 2, :, :], Yv[b, c]).then_inc(yz_in[c % 2], 16)
                    sp.dma_start(zb[:, c % 2, :, :], Zv[b, c]).then_inc(yz_in[c % 2], 16)
                    wait(sp, res_ready, m - 3)
                    sp.dma_start(xnb[:, c % 4, :, :], XN[b][:, :, c * T:(c + 1) * T]).then_inc(x_in[c % 4], 16)
                    sp.dma_start(x1b[:, c % 4, :, :], x1[b][:, :, c * T:(c + 1) * T]).then_inc(x_in[c % 4], 16)

            over_batches(sp, image)
            for p in range(2):
                sp.wait_ge(stored[p], 16 * B * NCHUNK // 2)

        @block.tensor
        def _(pe):
            pe.wait_ge(const_in, CONSTS)

            def out_proj(b, c):
                m = b * NCHUNK + c
                pe.wait_ge(gated_ready, m + 1)
                wait(pe, v_ready, m)
                for lo, hi, slot, r in ((0, CB, 0, 0), (CB, 2 * CB, 0, 1), (0, 2 * CB, 1, 2)):
                    last = pe.matmul(op_ps[lo:hi, slot, :], w_out[:, 1 if r == 2 else 0, 0:hi - lo],
                                     gated[:, c % 2, r, :], start=True, stop=True)
                last.then_inc(op_done, 1)

            def mean(b, c):
                m = b * NCHUNK + c
                pe.wait_ge(v_ready, m + 1)
                wait(pe, cen_ready, m)
                for slot in range(2):
                    last = pe.matmul(mean_ps[:, :], mean_w[:, slot, :], v[:, c % 2, slot, :], start=slot == 0, stop=slot == 1)
                last.then_inc(mean_done, 1)

            def variance(b, c):
                m = b * NCHUNK + c
                pe.wait_ge(sq_ready, m + 1)
                wait(pe, lnv_ready, m)
                for slot in range(2):
                    last = pe.matmul(var_ps[:, :], mean_w[:, slot, :], sq[:, slot, :], start=slot == 0, stop=slot == 1)
                last.then_inc(var_done, 1)

            def project(b, c):
                m = b * NCHUNK + c
                pe.wait_ge(yn_ready, m + 1)
                wait(pe, res_ready, m - 1)
                for half in range(2):
                    for slot in range(2):
                        last = pe.matmul(out_ps[:, c % 2, half, :], w_proj[:, slot, half * HALF:(half + 1) * HALF],
                                         yn[:, slot, :], start=slot == 0, stop=slot == 1)
                last.then_inc(out_done, 1)

            def image(b):
                for c in range(NCHUNK + 3):
                    if c < NCHUNK:
                        out_proj(b, c)
                    if 1 <= c <= NCHUNK:
                        mean(b, c - 1)
                    if 2 <= c <= NCHUNK + 1:
                        variance(b, c - 2)
                    if c >= 3:
                        project(b, c - 3)

            over_batches(pe, image)

        @block.scalar
        def _(act):
            act.wait_ge(const_in, CONSTS)
            act.wait_ge(eps_set, 1)

            def squares(b, c):
                m = b * NCHUNK + c
                act.wait_ge(cen_ready, m + 1)
                wait(act, var_done, m)
                act.activation(sq[:, :, :], cen[:, c % 2, :, :], ACT.Square).then_inc(sq_ready, 1)

            def root(b, c):
                m = b * NCHUNK + c
                act.wait_ge(var_done, m + 1)
                act.activation(lnv[:, :], var_ps[:, :], ACT.Ln, bias=eps[:, :]).then_inc(lnv_ready, 1)
                act.wait_ge(lnv_ready, m + 1)
                wait(act, scaled, m)
                act.activation(rstd[:, :], lnv[:, :], ACT.Exp, scale=-0.5).then_inc(rstd_ready, 1)

            def affine(b, c):
                m = b * NCHUNK + c
                act.wait_ge(scaled, m + 1)
                wait(act, out_done, m)
                for slot in range(2):
                    last = act.activation(yn[:, slot, :], cen[:, c % 2, slot, :], ACT.Identity,
                                          scale=ln_w[:, slot:slot + 1], bias=ln_b[:, slot:slot + 1])
                last.then_inc(yn_ready, 1)

            def store(b, c):
                m = b * NCHUNK + c
                act.wait_ge(res_ready, m + 1)
                act.dma_start(out_v[b][:, :, c * T:(c + 1) * T], res[:, c % 2, :, :]).then_inc(stored[c % 2], 16)

            def image(b):
                for c in range(NCHUNK + 3):
                    if 1 <= c <= NCHUNK:
                        squares(b, c - 1)
                    if 2 <= c <= NCHUNK + 1:
                        root(b, c - 2)
                        affine(b, c - 2)
                    if c >= 3:
                        store(b, c - 3)

            over_batches(act, image)

        @block.vector
        def _(dve):
            dve.memset(eps[:, :], LN_EPS).then_inc(eps_set, 1)
            dve.wait_ge(const_in, CONSTS)

            def add_skip(b, c):
                m = b * NCHUNK + c
                dve.wait_ge(op_done, m + 1)
                dve.wait_ge(x_in[c % 4], b * (32 * NCHUNK // 4) + (c // 4 + 1) * 32)
                wait(dve, cen_ready, m - 1)
                dve.scalar_tensor_tensor(v[:, c % 2, :, :], xnb[:, c % 4, :, :], skip[:, 0:1], op_ps[:, :, :],
                                         ALU.mult, ALU.add).then_inc(v_ready, 1)

            def centre(b, c):
                m = b * NCHUNK + c
                dve.wait_ge(mean_done, m + 1)
                wait(dve, yn_ready, m - 1)
                dve.tensor_tensor(cen[:, c % 2, :, :], v[:, c % 2, :, :],
                                  mean_ps[:, :].unsqueeze(1).broadcast_to([128, 2, T]), ALU.subtract).then_inc(cen_ready, 1)

            def scale(b, c):
                m = b * NCHUNK + c
                dve.wait_ge(rstd_ready, m + 1)
                dve.wait_ge(cen_ready, m + 1)
                dve.tensor_tensor(cen[:, c % 2, :, :], cen[:, c % 2, :, :],
                                  rstd[:, :].unsqueeze(1).broadcast_to([128, 2, T]), ALU.mult).then_inc(scaled, 1)

            def residual(b, c):
                m = b * NCHUNK + c
                dve.wait_ge(out_done, m + 1)
                wait(dve, stored[c % 2], b * (16 * NCHUNK // 2) + (c // 2) * 16)
                for half in range(2):
                    last = dve.scalar_tensor_tensor(res[:, c % 2, half, :], out_ps[:, c % 2, half, :],
                                                    proj_b[:, half:half + 1], x1b[:, c % 4, half, :], ALU.add, ALU.add)
                last.then_inc(res_ready, 1)

            def image(b):
                for c in range(NCHUNK + 3):
                    if c < NCHUNK:
                        add_skip(b, c)
                    if 1 <= c <= NCHUNK:
                        centre(b, c - 1)
                    if 2 <= c <= NCHUNK + 1:
                        scale(b, c - 2)
                    if c >= 3:
                        residual(b, c - 3)

            over_batches(dve, image)

        @block.gpsimd
        def _(pool):
            def image(b):
                for c in range(NCHUNK):
                    m = b * NCHUNK + c
                    pool.wait_ge(yz_in[c % 2], b * (32 * NCHUNK // 2) + (c // 2 + 1) * 32)
                    wait(pool, op_done, m - 1)
                    pool.tensor_tensor(gated[:, c % 2, :, :], yb[:, c % 2, :, :], zb[:, c % 2, :, :],
                                       ALU.mult).then_inc(gated_ready, 1)

            over_batches(pool, image)


def build(nc, arg, out):
    fp32 = mybir.dt.float32

    def scratch(name, shape):
        return nc.dram_tensor(name, shape, fp32, kind="Internal").ap()

    units0, units1 = B * K0 * NCHUNK, B * NBR * NCHUNK
    U0, Y0 = scratch("U0", (units0, 128, ND0, T)), scratch("Y0", (units0, 128, ND0, T))
    x1 = scratch("x1", (B, HALF, 2, L))
    U1, Y1, Z1 = (scratch(n, (units1, 128, 1, T)) for n in ("U1", "Y1", "Z1"))
    XN = scratch("XN", (B, 128, 2, L))
    x = arg["x"].rearrange("b (s p) l -> b p s l", p=HALF)

    layer0_features(nc, x, U0, arg["group_mean"], arg["a_in"], arg["a_taps"], arg["a_conv_b"], arg["ident"])
    scan_phase(nc, "s0", (B, K0, ND0, 1, R0), U0, Y0, arg["a_xproj"], arg["a_dt"], arg["a_small"],
               arg["keep"], arg["ident"], arg["select"])
    layer0_output(nc, Y0, x, x1, arg["mean_384"], arg["a_ln_w"], arg["a_ln_b"], arg["a_out"])
    layer1_features(nc, x1, U1, Z1, XN, arg["group_mean"], arg["b_pair"], arg["b_third"], arg["b_conv_b"],
                    arg["mean_64"], arg["b_ln1_w"], arg["b_ln1_b"], arg["b_in"], arg["b_conv1d"], arg["b_conv1d_b"])
    scan_phase(nc, "s1", (B * NBR, 1, 1, 2, R1), U1, Y1, arg["b_xproj"], arg["b_dt"], arg["b_small"],
               arg["keep"], arg["ident"], arg["select"])
    layer1_output(nc, Y1, Z1, XN, x1, out, arg["b_skip"], arg["b_out"], arg["mean_192"], arg["b_ln_w"],
                  arg["b_ln_b"], arg["b_proj"], arg["b_proj_b"])


def kernel(**inputs):
    import numpy as np
    import concourse.bacc as _bacc
    from concourse.bass_utils import run_bass_kernel_spmd as _run

    a = {k: np.asarray(v) for k, v in inputs.items()}
    la = {k[len("L0_conv_"):]: v for k, v in a.items() if k.startswith("L0_conv_")}
    lb = {k[len("L1_conv_"):]: v for k, v in a.items() if k.startswith("L1_conv_")}
    f = a["x"].dtype

    def columns(v, n):
        return np.swapaxes(v.reshape(*v.shape[:-1], n, 128), -1, -2)

    def xproj(w, rank, nd):
        bc = w[:, rank:]
        w = np.concatenate([bc, bc, bc, w[:, :rank]], 1)
        return w.reshape(len(w), XROWS + rank, nd, 128).transpose(0, 3, 2, 1)

    def small(bias, D, A_log, nd):
        k = len(bias)
        logs = A_log.reshape(k, nd, 128, N_STATE).transpose(0, 2, 1, 3).reshape(k, 128, nd * N_STATE)
        return np.concatenate([columns(bias, nd), columns(D, nd), logs], 2)

    def pair(v):
        return np.stack([np.concatenate([v, v]), np.concatenate([v, np.zeros_like(v)])], 1)

    def slots(v):
        return np.stack([v[:128], np.concatenate([v[128:], np.zeros_like(v[:64])])], 1)

    ident = np.eye(128, dtype=f)
    select = np.zeros((XROWS, 2 * N_STATE, 128), f)
    for n in range(2 * N_STATE):
        select[n::2 * N_STATE, n] = 1
    keep = np.ones((NCHUNK, 128, 1), f)
    keep[-1] = 0
    group_mean, mean_64 = np.zeros((HALF, HALF), f), np.zeros((128, 128), f)
    for g in range(0, HALF, CH // 32):
        group_mean[g:g + CH // 32, g:g + CH // 32] = 32 / CH
    for g in range(0, 128, CB):
        mean_64[g:g + CB, g:g + CB] = 1 / CB
    mean_192 = np.zeros((128, 2, 128), f)
    mean_192[:, 0] = 1 / CH
    mean_192[:CH - 128, 1] = 1 / CH

    taps = lb["conv1_w"].reshape(CB, 2, HALF, 3, 3).transpose(2, 1, 3, 4, 0)
    w_out = lb["out_proj_w"].T
    arrays = {
        "x": a["x"].reshape(B, CH, L),
        "ident": ident, "select": select.reshape(XROWS, -1), "keep": keep, "group_mean": group_mean,
        "mean_384": np.full((128, 128), 1 / D0, f), "mean_64": mean_64, "mean_192": mean_192,
        "a_in": la["in_proj_w"].T.reshape(2, HALF, D0).transpose(1, 0, 2),
        "a_taps": la["conv_w"].reshape(ND0, 128, TAPS).transpose(1, 0, 2),
        "a_conv_b": columns(la["conv_b"], ND0),
        "a_xproj": xproj(la["x_proj_weight"], R0, ND0),
        "a_dt": la["dt_projs_weight"].reshape(K0, ND0, 128, R0).transpose(0, 3, 1, 2),
        "a_small": small(la["dt_projs_bias"], la["Ds"].reshape(K0, D0), la["A_logs"], ND0),
        "a_ln_w": columns(la["ln_w"], ND0), "a_ln_b": columns(la["ln_b"], ND0),
        "a_out": la["out_proj_w"].T.reshape(ND0, 128, CH).transpose(1, 0, 2),
        "b_pair": np.concatenate([taps, taps[:, :, :, ::-1]], 4).reshape(HALF, 2, TAPS, 2 * CB),
        "b_third": taps[:, :, ::-1].reshape(HALF, 2, TAPS, CB),
        "b_conv_b": np.concatenate([lb["conv1_b"]] * 2)[:, None],
        "b_ln1_w": pair(lb["norm1_w"]), "b_ln1_b": pair(lb["norm1_b"]),
        "b_in": np.concatenate([lb["in_proj_w"].T] * 2),
        "b_conv1d": np.broadcast_to(lb["convd_w"].T[None], (128, DCONV, D1)),
        "b_conv1d_b": lb["convd_b"][:, None],
        "b_xproj": xproj(lb["x_proj_w"][None], R1, 1),
        "b_dt": lb["dt_proj_w"].T[None, :, None, :],
        "b_small": small(lb["dt_proj_b"][None], lb["D_param"][None], lb["A_log"], 1),
        "b_skip": np.broadcast_to(lb["skip_scale"][None], (128, 1)),
        "b_out": np.stack([np.concatenate([w_out, np.zeros_like(w_out)], 1)] * 2, 1),
        "b_ln_w": slots(lb["norm_w"]), "b_ln_b": slots(lb["norm_b"]),
        "b_proj": slots(lb["proj_w"].T), "b_proj_b": lb["proj_b"].reshape(2, HALF).T,
    }
    nc = _bacc.Bacc("TRN2", target_bir_lowering=False, num_devices=1)
    arrays = {f"in_{k}": np.ascontiguousarray(v) for k, v in arrays.items()}
    arg = {k[3:]: nc.dram_tensor(k, v.shape, mybir.dt.from_np(v.dtype), kind="ExternalInput").ap()
           for k, v in arrays.items()}
    out = nc.dram_tensor("out", (B, CH, L), mybir.dt.float32, kind="ExternalOutput").ap()
    build(nc, arg, out)
    r = _run(nc, [arrays], core_ids=[0])
    return r.results[0]["out"].reshape(B, CH, H, W)
```

```python
from contextlib import ExitStack

import concourse.bass as bass
from concourse import mybir

ACT = mybir.ActivationFunctionType
ALU = mybir.AluOpType

B, CH, H, W = 8, 192, 64, 64
L = H * W
T = 512
NCHUNK = L // T
ROWS = T // W
HALF = CH // 2
GROUP_EPS = 1e-5
LN_EPS = 1e-5
N_STATE = 16
XROWS = 3 * 2 * N_STATE

D0, K0, R0 = 384, 4, 12
ND0 = D0 // 128
CB, D1, R1, NBR = 64, 128, 4, 3
TAPS = 9
DCONV = 4


def wait(eng, semaphore, value):
    if not (isinstance(value, int) and value <= 0):
        eng.wait_ge(semaphore, value)


def over_batches(eng, body):
    body(0)
    with eng.Fori(1, B - 1) as b:
        body(b)
    body(B - 1)


def is_last(b):
    return isinstance(b, int) and b == B - 1


STATS_STEPS, SCALE_STEPS = 4, 4


def group_stats(dve, b, x, stats, mv, packed, sq, steps, passed):
    done = b * STATS_STEPS
    for half in range(2):
        for c in range(NCHUNK):
            last = dve.bn_stats(stats[:, half, c, :], x[:, half, c * T:(c + 1) * T])
    last.then_inc(steps, 1)
    dve.wait_ge(steps, done + 1)
    dve.sem_inc(passed, 1)
    for half in range(2):
        last = dve.bn_aggr(mv[:, half, :], stats[:, half, :, :].rearrange("p c s -> p (c s)"))
    last.then_inc(steps, 1)
    dve.wait_ge(steps, done + 2)
    dve.tensor_copy(packed[:, 0:2], mv[:, :, 0])
    dve.tensor_tensor(sq[:, :], mv[:, :, 0], mv[:, :, 0], ALU.mult).then_inc(steps, 1)
    dve.wait_ge(steps, done + 3)
    dve.tensor_tensor(packed[:, 2:4], sq[:, :], mv[:, :, 1], ALU.add).then_inc(steps, 1)


def group_variance(dve, b, g_ps, gm, sq, var, steps):
    done = b * SCALE_STEPS
    dve.tensor_copy(gm[:, :], g_ps[:, :]).then_inc(steps, 1)
    dve.wait_ge(steps, done + 1)
    dve.tensor_tensor(sq[:, :], gm[:, 0:2], gm[:, 0:2], ALU.mult).then_inc(steps, 1)
    dve.wait_ge(steps, done + 2)
    dve.tensor_tensor(sq[:, :], gm[:, 2:4], sq[:, :], ALU.subtract).then_inc(steps, 1)
    dve.wait_ge(steps, done + 3)
    dve.tensor_scalar(var[:, :], sq[:, :], GROUP_EPS, None, ALU.add).then_inc(steps, 1)


def inverse_root(act, lnv, rstd, var, half_step, half_value):
    act.activation(lnv, var, ACT.Ln).then_inc(half_step, 1)
    act.wait_ge(half_step, half_value)
    return act.activation(rstd, lnv, ACT.Exp, scale=-0.5)


def layer0_features(nc, x, U, gmat_in, w_in_in, taps_in, conv_b_in, ident_in):
    fp32 = mybir.dt.float32
    Uv = U.rearrange("(b k c) p t j -> b k t p c j", b=B, k=K0)
    with ExitStack() as ctx:
        ctx.enter_context(nc.cleanup_on_exit())
        def sb(n, s, dt=fp32):
            return ctx.enter_context(nc.sbuf_tensor(f"f0_{n}", s, dt))

        def pb(n, s):
            return ctx.enter_context(nc.psum_tensor(f"f0_{n}", s, fp32))

        def sem(n):
            return nc.alloc_semaphore(f"f0_{n}")

        xin = sb("xin", [HALF, 2, L])
        pad = [sb(f"pad{t}", [128, H + 2, W + 2]) for t in range(ND0)]
        row = [sb(f"row{t}", [128, L]) for t in range(ND0)]
        col, row_rev, col_rev = sb("col", [128, L]), sb("row_rev", [128, L]), sb("col_rev", [128, L])
        gmat, w_in = sb("gmat", [HALF, HALF]), sb("w_in", [HALF, 2, D0])
        taps, conv_b, ident = sb("taps", [128, ND0, TAPS]), sb("conv_b", [128, ND0]), sb("ident", [128, 128])
        diag = sb("diag", [128, TAPS, 128])
        stats, mv = sb("stats", [HALF, 2, NCHUNK, 6]), sb("mv", [HALF, 2, 2])
        packed, sq = sb("packed", [HALF, 4]), sb("sq", [HALF, 2])
        gm, sq2, var, lnv, rstd = (sb("gm", [HALF, 4]), sb("sq2", [HALF, 2]), sb("var", [HALF, 2]),
                                   sb("lnv", [HALF, 2]), sb("rstd", [HALF, 2]))
        in_ps = pb("in_ps", [128, 3, T])
        conv_ps = pb("conv_ps", [128, 4, T])
        g_ps = pb("g_ps", [HALF, 4])

        const_in, x_in, setup, passed = sem("const_in"), sem("x_in"), sem("setup"), sem("passed")
        stat_steps, g_done, scale_steps = sem("stat_steps"), sem("g_done"), sem("scale_steps")
        lnv_ready, rstd_ready, xn_ready = sem("lnv_ready"), sem("rstd_ready"), sem("xn_ready")
        in_done, pad_ready, conv_done, taps_added = sem("in_done"), sem("pad_ready"), sem("conv_done"), sem("taps_added")
        row_ready = [sem(f"row_ready{t}") for t in range(ND0)]
        col_ready, rev_ready, col_rev_ready = sem("col_ready"), sem("rev_ready"), sem("col_rev_ready")
        stored = [sem(f"stored{k}") for k in range(ND0 + K0 - 1)]
        block = ctx.enter_context(nc.Block())

        ON_PE = 1

        def own(b, t):
            return b * 2 + t // 2

        def tile(b, t):
            return b * ND0 + t

        @block.sync
        def _(sp):
            sp.dma_start(gmat[:, :], gmat_in).then_inc(const_in, 16)
            sp.dma_start(w_in[:, :, :], w_in_in).then_inc(const_in, 16)
            sp.dma_start(taps[:, :, :], taps_in).then_inc(const_in, 16)
            sp.dma_start(conv_b[:, :], conv_b_in).then_inc(const_in, 16)
            sp.dma_start(ident[:, :], ident_in).then_inc(const_in, 16)
            sp.dma_start(xin[:, :, :], x[0]).then_inc(x_in, 16)

            def image(b):
                for t in range(ND0):
                    for k, src, ready, count in (
                            (0, row[t], row_ready[t], (b + 1) * NCHUNK), (1, col, col_ready, tile(b, t) + 1),
                            (2, row_rev, rev_ready, tile(b, t) + 1), (3, col_rev, col_rev_ready, tile(b, t) + 1)):
                        sp.wait_ge(ready, count)
                        done = stored[t] if k == 0 else stored[ND0 - 1 + k]
                        sp.dma_start(Uv[b, k, t], src[:, :].rearrange("p (c j) -> p c j", j=T)).then_inc(done, 16)

            over_batches(sp, image)
            for t in range(ND0):
                sp.wait_ge(stored[t], 16 * B)
            for k in range(1, K0):
                sp.wait_ge(stored[ND0 - 1 + k], 16 * B * ND0)

        @block.tensor
        def _(pe):
            pe.wait_ge(const_in, 80)
            pe.wait_ge(setup, 1 + ND0)

            def group_means(b):
                pe.wait_ge(stat_steps, (b + 1) * STATS_STEPS)
                pe.matmul(g_ps[:, :], gmat[:, :], packed[:, :], start=True, stop=True).then_inc(g_done, 1)

            def in_proj(b, t):
                for c in range(NCHUNK):
                    m = tile(b, t) * NCHUNK + c
                    bank = (t * NCHUNK + c) % 3
                    wait(pe, pad_ready, m - 2)
                    for half in range(2):
                        last = pe.matmul(in_ps[:, bank, :], w_in[:, half, t * 128:(t + 1) * 128],
                                         xin[:, half, c * T:(c + 1) * T], start=half == 0, stop=half == 1)
                    last.then_inc(in_done, 1)

            def conv(b, c):
                wait(pe, row_ready[ON_PE], b * NCHUNK + c - 3)
                for k in range(TAPS):
                    dy, dx = divmod(k, 3)
                    last = pe.matmul(conv_ps[:, c % 4, :], diag[:, k, :],
                                     pad[ON_PE][:, c * ROWS + dy:c * ROWS + dy + ROWS, dx:dx + W],
                                     start=k == 0, stop=k == TAPS - 1)
                last.then_inc(conv_done, 1)

            def image(b):
                pe.wait_ge(xn_ready, b + 1)
                for t in range(ND0):
                    in_proj(b, t)
                pe.wait_ge(pad_ready, (tile(b, ON_PE) + 1) * NCHUNK)
                for c in range(NCHUNK):
                    conv(b, c)
                    if c == 4 and not is_last(b):
                        group_means(b + 1)

            group_means(0)
            over_batches(pe, image)

        @block.scalar
        def _(act):
            act.wait_ge(const_in, 80)

            def scale(b):
                act.wait_ge(scale_steps, b * SCALE_STEPS + 4)
                inverse_root(act, lnv[:, :], rstd[:, :], var[:, :], lnv_ready, b + 1).then_inc(rstd_ready, 1)

            def take_in(b, t):
                if t == ON_PE:
                    wait(act, conv_done, b * NCHUNK)
                else:
                    wait(act, taps_added, own(b - 1, t) * TAPS + TAPS)
                for c in range(NCHUNK):
                    act.wait_ge(in_done, tile(b, t) * NCHUNK + c + 1)
                    act.activation(pad[t][:, 1 + c * ROWS:1 + (c + 1) * ROWS, 1:1 + W],
                                   in_ps[:, (t * NCHUNK + c) % 3, :].rearrange("p (r w) -> p r w", w=W),
                                   ACT.Copy).then_inc(pad_ready, 1)

            def take_conv(b, c):
                m = b * NCHUNK + c
                if c == 0:
                    n = tile(b, ON_PE)
                    wait(act, stored[ON_PE], b * 16)
                    wait(act, col_ready, n - 2)
                    wait(act, rev_ready, n - 2)
                act.wait_ge(conv_done, m + 1)
                act.activation(row[ON_PE][:, c * T:(c + 1) * T], conv_ps[:, c % 4, :], ACT.Silu,
                               bias=conv_b[:, ON_PE:ON_PE + 1]).then_inc(row_ready[ON_PE], 1)

            def take_own(b, t):
                act.wait_ge(taps_added, (own(b, t) + 1) * TAPS)
                for c in range(NCHUNK):
                    part = row[t][:, c * T:(c + 1) * T]
                    act.activation(part, part, ACT.Silu, bias=conv_b[:, t:t + 1]).then_inc(row_ready[t], 1)

            def image(b):
                take_in(b, 0)
                if not (isinstance(b, int) and b == 0):
                    take_own(b - 1, 2)
                take_in(b, 1)
                take_in(b, 2)
                if not is_last(b):
                    act.wait_ge(in_done, (b + 1) * ND0 * NCHUNK)
                    act.dma_start(xin[:, :, :], x[b + 1]).then_inc(x_in, 16)
                take_conv(b, 0)
                take_conv(b, 1)
                take_own(b, 0)
                for c in range(2, 5):
                    take_conv(b, c)
                if not is_last(b):
                    scale(b + 1)
                for c in range(5, NCHUNK):
                    take_conv(b, c)

            act.wait_ge(setup, 1 + ND0)
            scale(0)
            over_batches(act, image)
            take_own(B - 1, 2)

        @block.vector
        def _(dve):
            dve.wait_ge(const_in, 80)
            for t in range(ND0):
                dve.memset(pad[t][:, :, :], 0.0).then_inc(setup, 1)
            for k in range(TAPS):
                last = dve.tensor_scalar(diag[:, k, :], ident[:, :], taps[:, ON_PE, k:k + 1], None, ALU.mult)
            last.then_inc(setup, 1)

            def measure(b):
                dve.wait_ge(x_in, (b + 1) * 16)
                wait(dve, g_done, b)
                group_stats(dve, b, xin, stats, mv, packed, sq, stat_steps, passed)

            def normalise(b):
                dve.wait_ge(g_done, b + 1)
                group_variance(dve, b, g_ps, gm, sq2, var, scale_steps)
                dve.wait_ge(rstd_ready, b + 1)
                dve.wait_ge(scale_steps, b * SCALE_STEPS + 4)
                for half in range(2):
                    last = dve.tensor_scalar(xin[:, half, :], xin[:, half, :], gm[:, half:half + 1],
                                             rstd[:, half:half + 1], ALU.subtract, ALU.mult)
                last.then_inc(xn_ready, 1)

            def conv(b, t):
                n = tile(b, t)
                dve.wait_ge(pad_ready, (n + 1) * NCHUNK)
                wait(dve, stored[t], b * 16)
                wait(dve, col_ready, n - 2)
                wait(dve, rev_ready, n - 2)
                acc = row[t][:, :].rearrange("p (h w) -> p h w", w=W)
                for k in range(TAPS):
                    dy, dx = divmod(k, 3)
                    window = pad[t][:, dy:dy + H, dx:dx + W]
                    if k == 0:
                        dve.tensor_scalar(acc, window, taps[:, t, 0:1], None, ALU.mult).then_inc(taps_added, 1)
                    else:
                        dve.wait_ge(taps_added, own(b, t) * TAPS + k)
                        dve.scalar_tensor_tensor(acc, window, taps[:, t, k:k + 1], acc,
                                                 ALU.mult, ALU.add).then_inc(taps_added, 1)

            def turn(b, t):
                n = tile(b, t)
                dve.wait_ge(row_ready[t], (b + 1) * NCHUNK)
                wait(dve, stored[ND0], n * 16)
                wait(dve, col_rev_ready, n)
                dve.tensor_copy(col[:, :].rearrange("p (w h) -> p w h", h=H),
                                row[t][:, :].rearrange("p (h w) -> p w h", w=W)).then_inc(col_ready, 1)

            def image(b):
                conv(b, 0)
                if not (isinstance(b, int) and b == 0):
                    turn(b - 1, 2)
                if not is_last(b):
                    measure(b + 1)
                turn(b, 0)
                if not is_last(b):
                    normalise(b + 1)
                conv(b, 2)
                turn(b, 1)

            measure(0)
            normalise(0)
            over_batches(dve, image)
            turn(B - 1, 2)

        @block.gpsimd
        def _(pool):
            def image(b):
                for t in range(ND0):
                    n = tile(b, t)
                    pool.wait_ge(row_ready[t], (b + 1) * NCHUNK)
                    wait(pool, stored[ND0 + 1], n * 16)
                    pool.sem_inc(passed, 1)
                    pool.tensor_copy(row_rev[:, :], row[t][:, ::-1]).then_inc(rev_ready, 1)
                    pool.wait_ge(col_ready, n + 1)
                    wait(pool, stored[ND0 + 2], n * 16)
                    pool.sem_inc(passed, 1)
                    pool.tensor_copy(col_rev[:, :], col[:, ::-1]).then_inc(col_rev_ready, 1)

            over_batches(pool, image)


def scan_phase(nc, name, shape, U, Y, w_x, w_dt, w_small, keep, ident_in, sel_in):
    outer, K, nd, ng, rank = shape
    J, NS, NCH = nd * ng, N_STATE // ng, L // T
    seqs = outer * K
    units = seqs * NCH
    fp32, bf16 = mybir.dt.float32, mybir.dt.bfloat16
    SM = nd * (2 + N_STATE)
    LOADS = 5
    AHEAD = 4
    DECAYS = 2 * J
    GROUP = 2 if nd > 1 else 4
    GROUPS = NS // GROUP
    LEAD, COPY_LEAD = (4, 3) if nd > 1 else (3, 2)
    B_BANKS = 2 if nd > 1 else 1
    at = (dict(xproj=0, dt=(1, 2, 3), take=1, take_dt=(2, 3, 4), ex=(3, 4, 5), series=(5, 6, 8), log=(6, 7, 8),
               direct=(11, 12, 13), rest=2, mid=3, low=4, near=(7, 9, 10), pick=(8, 10, 11),
               delta=(13, 14, 15))
          if nd > 1 else
          dict(xproj=0, dt=(1,), take=1, take_dt=(2,), ex=(2,), series=(3,), log=(3,),
               direct=(6,), rest=2, mid=2, low=3, near=(4,), pick=(5,), delta=(7,)))
    SMALL, ROOT_A, ROOT_B, ROOT_C = 1 / 64, 3 ** -0.5, 3 ** 0.5 / 4, 13 / 16

    with ExitStack() as ctx:
        ctx.enter_context(nc.cleanup_on_exit())
        def sb(n, s, dt=fp32):
            return ctx.enter_context(nc.sbuf_tensor(f"{name}_{n}", s, dt))

        def pb(n, s):
            return ctx.enter_context(nc.psum_tensor(f"{name}_{n}", s, fp32))

        def sem(n):
            return nc.alloc_semaphore(f"{name}_{n}")

        u = [sb(f"u{q}", [128, nd, T]) for q in range(2)]
        wx = [sb(f"wx{q}", [128, nd, XROWS + rank]) for q in range(2)]
        wdt = [sb(f"wdt{q}", [128, nd, 128]) for q in range(2)]
        small = [sb(f"small{q}", [128, SM]) for q in range(2)]
        keep_in = [sb(f"keep_in{q}", [128, 1]) for q in range(2)]
        keep_sb = [sb(f"keep{q}", [128, 1]) for q in range(2)]
        negA = [sb(f"negA{q}", [128, nd * N_STATE]) for q in range(2)]
        delta = [sb(f"delta{q}", [128, nd, T]) for q in range(2)]
        du = [sb(f"du{q}", [128, nd, T]) for q in range(2)]
        bc16 = [sb(f"bc16{q}", [96, T], bf16) for q in range(2)]
        yo = [sb(f"yo{q}", [128, nd, T]) for q in range(2)]
        xd = sb("xd", [XROWS + rank, T])
        rest = sb("rest", [64, T])
        work = sb("work", [128, 5, max(nd * T, 2 * N_STATE * 128 // 5 + 1)])
        ex, lnx, near, is_small, relx = (
            work[:, i, 0:nd * T].rearrange("p (t j) -> p t j", j=T) for i in range(5))
        b_sb = sb("b_sb", [128, AHEAD, ng, T])
        dbu = sb("dbu", [128, AHEAD, J, T])
        dA = sb("dA", [128, DECAYS, T])
        h = sb("h", [128, 2 * GROUP, J, T])
        hc = sb("hc", [128, 2, J, T])
        state = sb("state", [128, NS, J])
        ident = sb("ident", [128, 128])
        self32 = work[0:96].rearrange("p a b -> p (a b)")[:, 0:2 * N_STATE * 128]
        sel = sb("sel", [96, 2 * N_STATE, 128], bf16)

        consts = sb("consts", [128, 2])
        c_ps = pb("c_ps", [128, 2, ng, T])
        b_ps = pb("b_ps", [128, B_BANKS, ng, T])
        y_ps = pb("y_ps", [128, nd, T])
        prep_ps = pb("prep_ps", [128, T])

        const_in, sel_ready, passed = sem("const_in"), sem("sel_ready"), sem("passed")
        loaded = [sem(f"loaded{q}") for q in range(2)]
        stored = [sem(f"stored{q}") for q in range(2)]
        xproj_done, xd_ready, dt_done, prep_read = sem("xproj_done"), sem("xd_ready"), sem("dt_done"), sem("prep_read")
        rest_ready, bc_ready = sem("rest_ready"), sem("bc_ready")
        ex_ready, near_ready, log_ready, consts_set, square_done = sem("ex_ready"), sem("near_ready"), sem("log_ready"), sem("consts_set"), sem("square_done")
        negA_ready, abs_done, soft_done, delta_ready, du_ready = (
            sem("negA_ready"), sem("abs_done"), sem("soft_done"), sem("delta_ready"), sem("du_ready"))
        b_done, b_copied, c_done = sem("b_done"), sem("b_copied"), sem("c_done")
        dA_ready, dbu_ready, scanned, hc_ready, summed = (
            sem("dA_ready"), sem("dbu_ready"), sem("scanned"), sem("hc_ready"), sem("summed"))
        state_saved, evacuated, direct_ready = sem("state_saved"), sem("evacuated"), sem("direct_ready")

        def bias_of(q, t):
            return small[q][:, t:t + 1]

        def D_of(q, t):
            return small[q][:, nd + t:nd + t + 1]

        def earlier_stores(g, q):
            return 16 * (g // 2) if isinstance(g, int) else (g - q) * 8

        def over_units(eng, unit):
            unit(0, 0, True)
            unit(1, 1, False)
            with eng.Fori(1, units // 2) as i:
                unit(i * 2, 0, False)
                unit(i * 2 + 1, 1, False)

        block = ctx.enter_context(nc.Block())

        @block.sync
        def _(eng):
            eng.dma_start(ident[:, :], ident_in).then_inc(const_in, 16)
            eng.dma_start(self32, sel_in).then_inc(const_in, 16)

            def load(g, k, c, q):
                eng.wait_ge(du_ready, (g + 1) * nd)
                eng.wait_ge(direct_ready, (g + 1) * nd)
                eng.dma_start(u[q][:, :, :], U[g]).then_inc(loaded[q], 16)
                eng.dma_start(wx[q][:, :, :], w_x[k]).then_inc(loaded[q], 16)
                eng.dma_start(wdt[q][XROWS:XROWS + rank, :, :], w_dt[k]).then_inc(loaded[q], 16)
                eng.dma_start(small[q][:, :], w_small[k]).then_inc(loaded[q], 16)
                eng.dma_start(keep_in[q][:, :], keep[c]).then_inc(loaded[q], 16)

            with eng.Fori(0, outer) as o:
                with eng.Fori(0, K) as k:
                    with eng.Fori(0, NCH // 2) as c2:
                        for q in range(2):
                            load((o * K + k) * NCH + c2 * 2 + q, k, c2 * 2 + q, q)
            eng.wait_ge(du_ready, (units + 1) * nd)
            eng.wait_ge(direct_ready, (units + 1) * nd)
            eng.dma_start(u[0][:, :, :], U[0]).then_inc(loaded[0], 16)
            eng.dma_start(wx[0][:, :, :], w_x[0]).then_inc(loaded[0], 16)
            eng.dma_start(wdt[0][XROWS:XROWS + rank, :, :], w_dt[0]).then_inc(loaded[0], 16)
            eng.dma_start(small[0][:, :], w_small[0]).then_inc(loaded[0], 16)
            eng.dma_start(keep_in[0][:, :], keep[0]).then_inc(loaded[0], 16)
            for q in range(2):
                eng.wait_ge(stored[q], 16 * (units // 2))

        def loads_of(g, q):
            half = g // 2 if isinstance(g, int) else (g - q) // 2
            return 16 * LOADS * (half + 1) if isinstance(half, int) else half * (16 * LOADS) + 16 * LOADS

        @block.tensor
        def _(pe):
            def xproj(g, q, lw):
                pe.wait_ge(loaded[q], lw)
                wait(pe, prep_read, g * (1 + nd))
                for t in range(nd):
                    last = pe.matmul(prep_ps[0:XROWS + rank], wx[q][:, t, :], u[q][:, t, :],
                                     start=t == 0, stop=t == nd - 1)
                last.then_inc(xproj_done, 1)

            def dt(g, q, t):
                pe.wait_ge(xd_ready, g + 1)
                pe.wait_ge(prep_read, g * (1 + nd) + 1 + t)
                pe.matmul(prep_ps[:, :], wdt[q][XROWS:XROWS + rank, t, :], xd[XROWS:XROWS + rank, :],
                          start=True, stop=True).then_inc(dt_done, 1)

            def b_broadcast(g, q, s):
                n = g * NS + s
                if s == 0:
                    pe.wait_ge(bc_ready, g * 2 + 2)
                wait(pe, b_copied, n - B_BANKS + 1)
                for r in range(ng):
                    last = pe.matmul(b_ps[:, s % B_BANKS, r, :], sel[:, s * ng + r, :], bc16[q][:, :],
                                     start=True, stop=True)
                last.then_inc(b_done, 1)

            def c_broadcast(g, q, s):
                n = g * NS + s
                wait(pe, hc_ready, n - 1)
                for r in range(ng):
                    last = pe.matmul(c_ps[:, s % 2, r, :], sel[:, N_STATE + s * ng + r, :], bc16[q][:, :],
                                     start=True, stop=True)
                last.then_inc(c_done, 1)

            def state_sum(g, s):
                n = g * NS + s
                pe.wait_ge(hc_ready, n + 1)
                if s == 0:
                    wait(pe, evacuated, g)
                for j in range(J):
                    r, t = divmod(j, nd)
                    last = pe.matmul(y_ps[:, t, :], ident[:, :], hc[:, s % 2, j, :],
                                     start=s == 0 and r == 0, stop=s == NS - 1 and r == ng - 1)
                last.then_inc(summed, 1)

            def unit(g, q, first):
                o = 1 - q
                for s in range(NS):
                    if s == at["xproj"]:
                        xproj(g + 1, o, loads_of(g + 1, o))
                    for t in range(nd):
                        if s == at["dt"][t]:
                            dt(g + 1, o, t)
                    if s + LEAD < NS:
                        b_broadcast(g, q, s + LEAD)
                    else:
                        b_broadcast(g + 1, o, s + LEAD - NS)
                    if s + 1 < NS:
                        c_broadcast(g, q, s + 1)
                    else:
                        c_broadcast(g + 1, o, 0)
                    if s:
                        state_sum(g, s - 1)
                    elif not first:
                        state_sum(g - 1, NS - 1)

            pe.wait_ge(const_in, 32)
            pe.wait_ge(sel_ready, 1)
            xproj(0, 0, 16 * LOADS)
            for t in range(nd):
                dt(0, 0, t)
            for s in range(LEAD):
                b_broadcast(0, 0, s)
            c_broadcast(0, 0, 0)
            over_units(pe, unit)
            state_sum(units - 1, NS - 1)

        @block.scalar
        def _(act):
            act.preload_act_table_set("natural_log_exp_and_others")
            act.wait_ge(consts_set, 2)
            act.sem_inc(direct_ready, 2 * nd)

            def take_xproj(g, q, lw):
                act.wait_ge(loaded[q], lw)
                act.activation(negA[q][:, :], small[q][:, 2 * nd:], ACT.Exp).then_inc(negA_ready, 1)
                act.wait_ge(negA_ready, g * 3 + 1)
                act.activation(negA[q][:, :], negA[q][:, :], ACT.Copy, scale=-1.0).then_inc(negA_ready, 1)
                act.activation(keep_sb[q][:, :], keep_in[q][:, :], ACT.Copy).then_inc(negA_ready, 1)
                act.wait_ge(xproj_done, g + 1)
                act.activation(xd[:, :], prep_ps[0:XROWS + rank, :], ACT.Copy).then_inc(xd_ready, 1)
                act.activation(bc16[q][:, :], prep_ps[0:96, :], ACT.Copy).then_inc(prep_read, 1)

            def take_direct(g, q, t, stores):
                if t == 0:
                    wait(act, stored[q], stores)
                act.activation(yo[q][:, t, :], u[q][:, t, :], ACT.Copy, scale=D_of(q, t)).then_inc(direct_ready, 1)

            def take_dt(g, q, t):
                n = g * nd + t
                act.wait_ge(dt_done, n + 1)
                wait(act, delta_ready, n - nd + 1)
                act.activation(lnx[:, t, :], prep_ps[:, :], ACT.Abs, bias=bias_of(q, t)).then_inc(abs_done, 1)
                act.activation(relx[:, t, :], prep_ps[:, :], ACT.Relu, bias=bias_of(q, t)).then_inc(prep_read, 1)

            def take_ex(g, t):
                n = g * nd + t
                act.wait_ge(abs_done, n + 1)
                wait(act, log_ready, n - nd + 1)
                act.activation(ex[:, t, :], lnx[:, t, :], ACT.Exp, scale=-1.0).then_inc(ex_ready, 1)

            def take_series(g, t):
                n = g * nd + t
                act.wait_ge(ex_ready, n + 1)
                act.activation(near[:, t, :], ex[:, t, :], ACT.Square, scale=ROOT_A, bias=consts[:, 0:1]).then_inc(square_done, 1)
                act.activation(is_small[:, t, :], ex[:, t, :], ACT.Relu, scale=-1.0, bias=consts[:, 1:2]).then_inc(square_done, 1)

            def take_log(g, t):
                act.wait_ge(ex_ready, g * nd + t + 1)
                act.activation(lnx[:, t, :], ex[:, t, :], ACT.Ln, bias=1.0).then_inc(soft_done, 1)

            def copy_b(g, s):
                n = g * NS + s
                act.wait_ge(b_done, n + 1)
                wait(act, dbu_ready, n - AHEAD + 1)
                act.activation(b_sb[:, s % AHEAD, :, :], b_ps[:, s % B_BANKS, :, :], ACT.Copy).then_inc(b_copied, 1)

            def decay(g, q, s, j):
                r, t = divmod(j, nd)
                n = (g * NS + s) * J + j
                if s == 0 and j == 0:
                    act.wait_ge(delta_ready, (g + 1) * nd)
                    act.wait_ge(negA_ready, g * 3 + 3)
                wait(act, scanned, n - DECAYS + 1)
                a = t * N_STATE + s * ng + r
                act.activation(dA[:, (s * J + j) % DECAYS, :], delta[q][:, t, :], ACT.Exp,
                               scale=negA[q][:, a:a + 1]).then_inc(dA_ready, 1)

            def save_states(g, q, i):
                act.wait_ge(scanned, (g * NS + (i + 1) * GROUP) * J)
                slots = slice(i % 2 * GROUP, (i % 2 + 1) * GROUP)
                act.activation(state[:, i * GROUP:(i + 1) * GROUP, :], h[:, slots, :, T - 1], ACT.Copy,
                               scale=keep_sb[q][:, 0:1]).then_inc(state_saved, 1)

            def store(g, q):
                act.wait_ge(evacuated, g + 1)
                act.dma_start(Y[g], yo[q][:, :, :]).then_inc(stored[q], 16)

            def unit(g, q, first):
                o = 1 - q
                for s in range(NS):
                    if s == 1 and not first:
                        save_states(g - 1, o, GROUPS - 1)
                    elif s > 1 and s % GROUP == 1:
                        save_states(g, q, s // GROUP - 1)
                    for j in range(J):
                        decay(g, q, s, j)
                    if s + COPY_LEAD < NS:
                        copy_b(g, s + COPY_LEAD)
                    else:
                        copy_b(g + 1, s + COPY_LEAD - NS)
                    if s == at["take"]:
                        take_xproj(g + 1, o, loads_of(g + 1, o))
                    for t in range(nd):
                        if s == at["take_dt"][t]:
                            take_dt(g + 1, o, t)
                        if s == at["ex"][t]:
                            take_ex(g + 1, t)
                        if s == at["series"][t]:
                            take_series(g + 1, t)
                        if s == at["log"][t]:
                            take_log(g + 1, t)
                        if s == at["direct"][t]:
                            take_direct(g + 1, o, t, earlier_stores(g + 1, o))
                    if s == 4 and not first:
                        store(g - 1, o)

            act.wait_ge(sel_ready, 1)
            take_xproj(0, 0, 16 * LOADS)
            for t in range(nd):
                take_dt(0, 0, t)
            for t in range(nd):
                take_ex(0, t)
            for t in range(nd):
                take_series(0, t)
                take_log(0, t)
                take_direct(0, 0, t, 0)
            for s in range(COPY_LEAD):
                copy_b(0, s)
            over_units(act, unit)
            save_states(units - 1, 1, GROUPS - 1)
            store(units - 1, 1)

        @block.gpsimd
        def _(pool):
            pool.sem_inc(du_ready, 2 * nd)

            def input_of(g, q, s):
                n = g * NS + s
                pool.wait_ge(b_copied, n + 1)
                if s == 0:
                    pool.wait_ge(du_ready, (g + 3) * nd)
                wait(pool, scanned, (n - AHEAD + 1) * J)
                a, b = du[q][:, :, :], b_sb[:, s % AHEAD, :, :]
                a, b = (a, b.broadcast_to([128, nd, T])) if ng == 1 else (a.broadcast_to([128, ng, T]), b)
                pool.tensor_tensor(dbu[:, s % AHEAD, :, :], a, b, ALU.mult).then_inc(dbu_ready, 1)

            def take_delta(g, q, t):
                n = g * nd + t
                pool.wait_ge(log_ready, n + 1)
                pool.wait_ge(prep_read, g * (1 + nd) + 2 + t)
                if t == 0:
                    wait(pool, dA_ready, (g - 1) * NS * J)
                    wait(pool, dbu_ready, (g - 1) * NS)
                pool.tensor_tensor(delta[q][:, t, :], relx[:, t, :], lnx[:, t, :], ALU.add).then_inc(delta_ready, 1)
                pool.wait_ge(delta_ready, n + 1)
                pool.tensor_tensor(du[q][:, t, :], delta[q][:, t, :], u[q][:, t, :], ALU.mult).then_inc(du_ready, 1)

            def unit(g, q, first):
                for s in range(1, NS):
                    input_of(g, q, s)
                    for t in range(nd):
                        if s == at["delta"][t]:
                            take_delta(g + 1, 1 - q, t)
                input_of(g + 1, 1 - q, 0)

            for t in range(nd):
                take_delta(0, 0, t)
            input_of(0, 0, 0)
            over_units(pool, unit)

        @block.vector
        def _(dve):
            dve.wait_ge(const_in, 32)
            dve.memset(consts[:, 0:1], -ROOT_B).then_inc(consts_set, 1)
            dve.memset(consts[:, 1:2], SMALL).then_inc(consts_set, 1)
            dve.tensor_copy(sel[:, :, :].rearrange("p a b -> p (a b)"), self32).then_inc(sel_ready, 1)

            def take_rest(g, q):
                dve.wait_ge(prep_read, g * (1 + nd) + 1)
                dve.wait_ge(xd_ready, g + 1)
                dve.tensor_tensor(rest[:, :], xd[0:64, :], bc16[q][0:64, :], ALU.subtract).then_inc(rest_ready, 1)

            def take_mid(g, q):
                dve.wait_ge(rest_ready, g + 1)
                dve.tensor_copy(bc16[q][0:64, :], rest[:, :]).then_inc(bc_ready, 1)

            def take_low(g, q):
                dve.wait_ge(bc_ready, g * 2 + 1)
                dve.tensor_tensor(bc16[q][32:64, :], rest[32:64, :], bc16[q][32:64, :], ALU.subtract).then_inc(bc_ready, 1)

            def take_near(g, t):
                n = g * nd + t
                dve.wait_ge(square_done, 2 * n + 2)
                dve.scalar_tensor_tensor(near[:, t, :], near[:, t, :], ROOT_C, ex[:, t, :],
                                         ALU.add, ALU.mult).then_inc(near_ready, 1)

            def pick(g, t):
                n = g * nd + t
                dve.wait_ge(near_ready, n + 1)
                dve.wait_ge(soft_done, n + 1)
                dve.sem_inc(passed, 1)
                dve.copy_predicated(lnx[:, t, :], is_small[:, t, :].bitcast(mybir.dt.uint32),
                                    near[:, t, :]).then_inc(log_ready, 1)

            def scan(g, q, s, j, initial):
                n = g * NS + s
                if j == 0:
                    dve.wait_ge(dbu_ready, n + 1)
                    wait(dve, hc_ready, n - 2 * GROUP + 1)
                    if s % GROUP == 0:
                        wait(dve, state_saved, g * GROUPS + s // GROUP - 1)
                dve.wait_ge(dA_ready, n * J + j + 1)
                dve.tensor_tensor_scan(h[:, s % (2 * GROUP), j, :], dA[:, (s * J + j) % DECAYS, :],
                                       dbu[:, s % AHEAD, j, :], initial, ALU.mult, ALU.add).then_inc(scanned, 1)

            def times_c(g, s):
                n = g * NS + s
                dve.wait_ge(scanned, (n + 1) * J)
                dve.wait_ge(c_done, n + 1)
                wait(dve, summed, n - 1)
                c = c_ps[:, s % 2, :, :]
                if ng == 1:
                    c = c.broadcast_to([128, nd, T])
                dve.tensor_tensor(hc[:, s % 2, :, :], h[:, s % (2 * GROUP), :, :], c, ALU.mult).then_inc(hc_ready, 1)

            def evacuate(g, q):
                dve.wait_ge(direct_ready, (g + 3) * nd)
                dve.wait_ge(summed, (g + 1) * NS)
                dve.tensor_tensor(yo[q][:, :, :], yo[q][:, :, :], y_ps[:, :, :], ALU.add).then_inc(evacuated, 1)

            def unit(g, q, first):
                o = 1 - q
                for s in range(NS):
                    for j in range(J):
                        scan(g, q, s, j, 0.0 if first else state[:, s, j:j + 1])
                        if j == 0 and s:
                            times_c(g, s - 1)
                        elif j == 0 and not first:
                            times_c(g - 1, NS - 1)
                        if j == 1 and s == 1 and not first:
                            evacuate(g - 1, o)
                    if s == at["rest"]:
                        take_rest(g + 1, o)
                    if s == at["mid"]:
                        take_mid(g + 1, o)
                    if s == at["low"]:
                        take_low(g + 1, o)
                    for t in range(nd):
                        if s == at["near"][t]:
                            take_near(g + 1, t)
                        if s == at["pick"][t]:
                            pick(g + 1, t)

            take_rest(0, 0)
            take_mid(0, 0)
            take_low(0, 0)
            for t in range(nd):
                take_near(0, t)
                pick(0, t)
            over_units(dve, unit)
            times_c(units - 1, NS - 1)
            evacuate(units - 1, 1)


def layer0_output(nc, Y, x, x1, ln_in, ln_w_in, ln_b_in, w_out_in):
    fp32 = mybir.dt.float32
    Yv = Y.rearrange("(b k c) p t j -> b k t p c j", b=B, k=K0)
    with ExitStack() as ctx:
        ctx.enter_context(nc.cleanup_on_exit())
        def sb(n, s, dt=fp32):
            return ctx.enter_context(nc.sbuf_tensor(f"m0_{n}", s, dt))

        def pb(n, s):
            return ctx.enter_context(nc.psum_tensor(f"m0_{n}", s, fp32))

        def sem(n):
            return nc.alloc_semaphore(f"m0_{n}")

        yk = [sb(f"y{k}", [128, L // 2]) for k in range(K0)]
        ysum = sb("ysum", [128, 2, ND0, L])
        xin = sb("xin", [HALF, 2, 2, T])
        cen, sq = sb("cen", [128, 2, ND0, T]), sb("sq", [128, ND0, T])
        yn = sb("yn", [128, ND0, T])
        lnv, rstd = sb("lnv", [128, T]), sb("rstd", [128, T])
        res = sb("res", [HALF, 2, 2, T])
        ones, w_out = sb("ones", [128, 128]), sb("w_out", [128, ND0, CH])
        ln_w, ln_b, eps = sb("ln_w", [128, ND0]), sb("ln_b", [128, ND0]), sb("eps", [128, 1])
        mean_ps, var_ps, out_ps = pb("mean_ps", [128, 2, T]), pb("var_ps", [128, 2, T]), pb("out_ps", [HALF, 2, 2, T])

        const_in, passed = sem("const_in"), sem("passed")
        x_in = [sem(f"x_in{p}") for p in range(2)]
        y_in = [sem(f"y_in{k}") for k in range(K0)]
        rows_added, cols_added = sem("rows_added"), sem("cols_added")
        mean_done, cen_ready, sq_ready, var_done = sem("mean_done"), sem("cen_ready"), sem("sq_ready"), sem("var_done")
        lnv_ready, rstd_ready, scaled = sem("lnv_ready"), sem("rstd_ready"), sem("scaled")
        yn_ready, out_done, res_ready, eps_set = sem("yn_ready"), sem("out_done"), sem("res_ready"), sem("eps_set")
        stored = [sem(f"stored{p}") for p in range(2)]
        cols_done = sem("cols_done")
        block = ctx.enter_context(nc.Block())

        def over_images(eng, body):
            body(0, 0)
            with eng.Fori(1, B // 2) as i:
                body(i * 2 - 1, 1)
                body(i * 2, 0)
            body(B - 1, 1)

        @block.sync
        def _(sp):
            for dst, src in ((ones[:, :], ln_in), (w_out[:, :, :], w_out_in), (ln_w[:, :], ln_w_in), (ln_b[:, :], ln_b_in)):
                sp.dma_start(dst, src).then_inc(const_in, 16)

            def load(b, k, t, hf):
                n = (b * ND0 + t) * 2 + hf
                wait(sp, cols_done if k == 1 else cols_added if k == 3 else rows_added, n)
                sp.sem_inc(passed, 1)
                part = hf if k < 2 else 1 - hf
                sp.dma_start(yk[k][:, :].rearrange("p (c j) -> p c j", j=T),
                             Yv[b, k, t][:, part * NCHUNK // 2:(part + 1) * NCHUNK // 2, :]).then_inc(y_in[k], 16)

            def image(b, q):
                for t in range(ND0):
                    for hf in range(2):
                        for k in (0, 2, 1, 3):
                            load(b, k, t, hf)

            over_images(sp, image)
            for p in range(2):
                sp.wait_ge(stored[p], 16 * B * NCHUNK // 2)

        @block.tensor
        def _(pe):
            pe.wait_ge(const_in, 64)

            def mean(b, q, c):
                m = b * NCHUNK + c
                wait(pe, cen_ready, m - 1)
                for t in range(ND0):
                    last = pe.matmul(mean_ps[:, c % 2, :], ones[:, :], ysum[:, q, t, c * T:(c + 1) * T],
                                     start=t == 0, stop=t == ND0 - 1)
                last.then_inc(mean_done, 1)

            def variance(b, c):
                m = b * NCHUNK + c
                pe.wait_ge(sq_ready, m + 1)
                wait(pe, rstd_ready, m - 1)
                for t in range(ND0):
                    last = pe.matmul(var_ps[:, c % 2, :], ones[:, :], sq[:, t, :], start=t == 0, stop=t == ND0 - 1)
                last.then_inc(var_done, 1)

            def project(b, c):
                m = b * NCHUNK + c
                pe.wait_ge(yn_ready, m + 1)
                wait(pe, res_ready, m - 1)
                for half in range(2):
                    for t in range(ND0):
                        last = pe.matmul(out_ps[:, c % 2, half, :], w_out[:, t, half * HALF:(half + 1) * HALF],
                                         yn[:, t, :], start=t == 0, stop=t == ND0 - 1)
                last.then_inc(out_done, 1)

            def image(b, q):
                pe.wait_ge(cols_done, (b + 1) * 2 * ND0)
                for c in range(NCHUNK + 2):
                    if c < NCHUNK:
                        mean(b, q, c)
                    if 1 <= c <= NCHUNK:
                        variance(b, c - 1)
                    if c >= 2:
                        project(b, c - 2)

            over_images(pe, image)

        @block.scalar
        def _(act):
            act.wait_ge(const_in, 64)
            act.wait_ge(eps_set, 1)
            act.preload_act_table_set("natural_log_exp_and_others")

            def squares(b, c):
                m = b * NCHUNK + c
                act.wait_ge(cen_ready, m + 1)
                wait(act, var_done, m)
                act.activation(sq[:, :, :], cen[:, c % 2, :, :], ACT.Square).then_inc(sq_ready, 1)

            def root(b, c):
                m = b * NCHUNK + c
                act.wait_ge(var_done, m + 1)
                act.activation(lnv[:, :], var_ps[:, c % 2, :], ACT.Ln, bias=eps[:, :]).then_inc(lnv_ready, 1)
                act.wait_ge(lnv_ready, m + 1)
                wait(act, scaled, m)
                act.activation(rstd[:, :], lnv[:, :], ACT.Exp, scale=-0.5).then_inc(rstd_ready, 1)

            def affine(b, c):
                m = b * NCHUNK + c
                act.wait_ge(scaled, m + 1)
                wait(act, out_done, m)
                for t in range(ND0):
                    last = act.activation(yn[:, t, :], cen[:, c % 2, t, :], ACT.Identity,
                                          scale=ln_w[:, t:t + 1], bias=ln_b[:, t:t + 1])
                last.then_inc(yn_ready, 1)

            def load_x(b, c):
                m = b * NCHUNK + c
                wait(act, res_ready, m - 1)
                act.dma_start(xin[:, c % 2, :, :], x[b][:, :, c * T:(c + 1) * T]).then_inc(x_in[c % 2], 16)

            def store(b, c):
                m = b * NCHUNK + c
                act.wait_ge(res_ready, m + 1)
                act.dma_start(x1[b][:, :, c * T:(c + 1) * T], res[:, c % 2, :, :]).then_inc(stored[c % 2], 16)

            def image(b, q):
                for c in range(NCHUNK + 3):
                    if c < NCHUNK:
                        squares(b, c)
                    if 1 <= c <= NCHUNK:
                        root(b, c - 1)
                        affine(b, c - 1)
                    if c >= 3:
                        store(b, c - 3)
                    if c < NCHUNK:
                        load_x(b, c)

            over_images(act, image)

        @block.vector
        def _(dve):
            dve.memset(eps[:, :], LN_EPS).then_inc(eps_set, 1)

            def add_rows(b, q, t, hf):
                n = (b * ND0 + t) * 2 + hf
                dve.wait_ge(y_in[0], (n + 1) * 16)
                dve.wait_ge(y_in[2], (n + 1) * 16)
                wait(dve, cen_ready, (b - 1) * NCHUNK)
                dve.tensor_tensor(ysum[:, q, t, hf * L // 2:(hf + 1) * L // 2], yk[0][:, :], yk[2][:, ::-1],
                                  ALU.add).then_inc(rows_added, 1)

            def add_columns(b, q, t, hf):
                n = (b * ND0 + t) * 2 + hf
                dve.wait_ge(rows_added, (b * ND0 + t + 1) * 2)
                dve.wait_ge(cols_added, n + 1)
                half = ysum[:, q, t, :].rearrange("p (h w) -> p h w", w=W)[:, :, hf * W // 2:(hf + 1) * W // 2]
                dve.tensor_tensor(half, half, yk[1][:, :].rearrange("p (w h) -> p h w", h=H), ALU.add).then_inc(cols_done, 1)

            def centre(b, q, c):
                m = b * NCHUNK + c
                dve.wait_ge(mean_done, m + 1)
                wait(dve, yn_ready, m - 1)
                dve.tensor_tensor(cen[:, c % 2, :, :], ysum[:, q, :, c * T:(c + 1) * T],
                                  mean_ps[:, c % 2, :].unsqueeze(1).broadcast_to([128, ND0, T]),
                                  ALU.subtract).then_inc(cen_ready, 1)

            def scale(b, c):
                m = b * NCHUNK + c
                dve.wait_ge(rstd_ready, m + 1)
                dve.wait_ge(sq_ready, m + 1)
                dve.wait_ge(cen_ready, m + 1)
                dve.tensor_tensor(cen[:, c % 2, :, :], cen[:, c % 2, :, :],
                                  rstd[:, :].unsqueeze(1).broadcast_to([128, ND0, T]), ALU.mult).then_inc(scaled, 1)

            def residual(b, c):
                m = b * NCHUNK + c
                dve.wait_ge(out_done, m + 1)
                dve.wait_ge(x_in[c % 2], b * (16 * NCHUNK // 2) + (c // 2 + 1) * 16)
                wait(dve, stored[c % 2], b * (16 * NCHUNK // 2) + (c // 2) * 16)
                dve.tensor_tensor(res[:, c % 2, :, :], out_ps[:, c % 2, :, :], xin[:, c % 2, :, :],
                                  ALU.add).then_inc(res_ready, 1)

            STEPS = NCHUNK + 2

            def image(b, q):
                for c in range(STEPS):
                    if c < NCHUNK:
                        centre(b, q, c)
                    if 1 <= c <= NCHUNK:
                        scale(b, c - 1)
                    if c >= 2:
                        residual(b, c - 2)
                    for step in range(4 * ND0):
                        if step * STEPS // (4 * ND0) == c and not is_last(b):
                            t, part = divmod(step, 4)
                            add = add_rows if part < 2 else add_columns
                            add(b + 1, 1 - q, t, part % 2)

            for t in range(ND0):
                for hf in range(2):
                    add_rows(0, 0, t, hf)
                for hf in range(2):
                    add_columns(0, 0, t, hf)
            over_images(dve, image)

        @block.gpsimd
        def _(pool):
            def image(b, q):
                for t in range(ND0):
                    for hf in range(2):
                        n = (b * ND0 + t) * 2 + hf
                        pool.wait_ge(y_in[1], (n + 1) * 16)
                        pool.wait_ge(y_in[3], (n + 1) * 16)
                        pool.tensor_tensor(yk[1][:, :], yk[1][:, :], yk[3][:, ::-1], ALU.add).then_inc(cols_added, 1)

            over_images(pool, image)


def layer1_features(nc, x1, U, Z, XN, gmat_in, w_pair_in, w_third_in, conv_b_in, ones_in, ln_w_in, ln_b_in,
                    w_in_in, w_conv_in, conv1d_b_in):
    fp32 = mybir.dt.float32
    Uv = U.rearrange("(b r c) p o j -> b r p (o c) j", b=B, r=NBR)
    Zv = Z.rearrange("(b r c) p o j -> b r p (o c) j", b=B, r=NBR)
    with ExitStack() as ctx:
        ctx.enter_context(nc.cleanup_on_exit())
        def sb(n, s, dt=fp32):
            return ctx.enter_context(nc.sbuf_tensor(f"f1_{n}", s, dt))

        def pb(n, s):
            return ctx.enter_context(nc.psum_tensor(f"f1_{n}", s, fp32))

        def sem(n):
            return nc.alloc_semaphore(f"f1_{n}")

        xin = sb("xin", [HALF, 2, L])
        pad = sb("pad", [HALF, 2, H + 2, W + 2])
        seq = sb("seq", [128, 2, 2, T])
        cen = sb("cen", [128, 2, 2, T])
        middle = sb("middle", [128, 2, T])
        sq_sb = sb("sq_sb", [128, 2, T])
        lnr, rstd_sb = sb("lnr", [128, 2, T]), sb("rstd_sb", [128, 2, T])
        xn = sb("xn", [128, 2, DCONV - 1 + L])
        u_sb, z_sb = sb("u_sb", [128, 2, L // 2]), sb("z_sb", [128, 2, L // 2])
        gmat, ones = sb("gmat", [HALF, HALF]), sb("ones", [128, 128])
        w_pair, w_third = sb("w_pair", [HALF, 2, TAPS, 2 * CB]), sb("w_third", [HALF, 2, TAPS, CB])
        w_in, w_conv = sb("w_in", [128, 2 * D1]), sb("w_conv", [128, DCONV, D1])
        w_fold = sb("w_fold", [128, DCONV, D1])
        conv_b, conv1d_b = sb("conv_b", [128, 1]), sb("conv1d_b", [128, 1])
        ln_w, ln_b, eps = sb("ln_w", [128, 2]), sb("ln_b", [128, 2]), sb("eps", [128, 1])
        stats, mv = sb("stats", [HALF, 2, NCHUNK, 6]), sb("mv", [HALF, 2, 2])
        packed, sq = sb("packed", [HALF, 4]), sb("sq", [HALF, 2])
        gm, sq2, var, lnv, rstd = (sb("gm", [HALF, 4]), sb("sq2", [HALF, 2]), sb("var", [HALF, 2]),
                                   sb("lnv", [HALF, 2]), sb("rstd", [HALF, 2]))
        bank_ps = pb("bank_ps", [128, 6, T])
        stat_ps = pb("stat_ps", [128, 2, T])
        g_ps = bank_ps[0:HALF, 5, 0:4]

        const_in, x_in, setup, passed = sem("const_in"), sem("x_in"), sem("setup"), sem("passed")
        stat_steps, g_done, scale_steps = sem("stat_steps"), sem("g_done"), sem("scale_steps")
        lnv_ready, rstd_ready, pad_ready = sem("lnv_ready"), sem("rstd_ready"), sem("pad_ready")
        middle_ready = sem("middle_ready")
        conv_done, seq_ready, mean_done, cen_ready = sem("conv_done"), sem("seq_ready"), sem("mean_done"), sem("cen_ready")
        sq_ready, var_done, lnr_ready, root_ready = sem("sq_ready"), sem("var_done"), sem("lnr_ready"), sem("root_ready")
        scaled, xn_ready = sem("scaled"), sem("xn_ready")
        proj_done, proj_read = sem("proj_done"), sem("proj_read")
        xn_stored = sem("xn_stored")
        u_stored = [sem(f"u_stored{p}") for p in range(2)]
        z_stored = [sem(f"z_stored{p}") for p in range(2)]
        block = ctx.enter_context(nc.Block())
        MIDDLE, OUTER = (3, 4, 5), (0, 1, 2, 6, 7, 8)
        PARTS = 2 * NBR
        PC = NCHUNK // 2

        PART_LIST = ((0, 0), (1, 0), (0, 1), (1, 1), (2, 0), (2, 1))

        @block.sync
        def _(sp):
            for dst, src in ((gmat[:, :], gmat_in), (ones[:, :], ones_in), (w_pair[:, :, :, :], w_pair_in),
                             (w_third[:, :, :, :], w_third_in), (w_in[:, :], w_in_in), (w_conv[:, :, :], w_conv_in),
                             (conv_b[:, :], conv_b_in), (conv1d_b[:, :], conv1d_b_in), (ln_w[:, :], ln_w_in),
                             (ln_b[:, :], ln_b_in)):
                sp.dma_start(dst, src).then_inc(const_in, 16)
            sp.dma_start(xin[:, :, :], x1[0]).then_inc(x_in, 16)

            def image(b):
                if not is_last(b):
                    sp.wait_ge(pad_ready, b + 1)
                    sp.dma_start(xin[:, :, :], x1[b + 1]).then_inc(x_in, 16)
                sp.wait_ge(xn_ready, (b + 1) * NCHUNK)
                sp.dma_start(XN[b], xn[:, :, DCONV - 1:]).then_inc(xn_stored, 16)

                for i, (r, hf) in enumerate(PART_LIST):
                    sp.wait_ge(proj_read, ((b * PARTS) + i + 1) * 2 * PC)
                    sp.dma_start(Uv[b, r][:, hf * PC:(hf + 1) * PC, :],
                                 u_sb[:, i % 2, :].rearrange("p (c j) -> p c j", j=T)).then_inc(u_stored[i % 2], 16)
                    sp.dma_start(Zv[b, r][:, hf * PC:(hf + 1) * PC, :],
                                 z_sb[:, i % 2, :].rearrange("p (c j) -> p c j", j=T)).then_inc(z_stored[i % 2], 16)

            over_batches(sp, image)
            sp.wait_ge(xn_stored, 16 * B)
            for p in range(2):
                sp.wait_ge(u_stored[p], 16 * B * PARTS // 2)
                sp.wait_ge(z_stored[p], 16 * B * PARTS // 2)

        @block.tensor
        def _(pe):
            pe.wait_ge(const_in, 160)
            pe.wait_ge(setup, 5)

            def group_means(b):
                pe.wait_ge(stat_steps, (b + 1) * STATS_STEPS)
                pe.matmul(g_ps, gmat[:, :], packed[:, :], start=True, stop=True).then_inc(g_done, 1)

            def conv(b, c, bank, w, rows, taps):
                m = b * NCHUNK + c
                wait(pe, seq_ready, m - 1)
                for half in range(2):
                    for k in taps:
                        dy, dx = divmod(k, 3)
                        last = pe.matmul(bank_ps[0:rows, c % 2 * 3 + bank, :], w[:, half, k, :],
                                         pad[:, half, c * ROWS + dy:c * ROWS + dy + ROWS, dx:dx + W],
                                         start=half == 0 and k == taps[0], stop=half == 1 and k == taps[-1])
                last.then_inc(conv_done, 1)

            def mean(b, c):
                m = b * NCHUNK + c
                pe.wait_ge(seq_ready, m + 1)
                wait(pe, lnr_ready, m)
                for slot in range(2):
                    last = pe.matmul(stat_ps[:, slot, :], ones[:, :], seq[:, c % 2, slot, :], start=True, stop=True)
                last.then_inc(mean_done, 1)

            def variance(b, c):
                m = b * NCHUNK + c
                pe.wait_ge(sq_ready, m + 1)
                for slot in range(2):
                    last = pe.matmul(stat_ps[:, slot, :], ones[:, :], sq_sb[:, slot, :], start=True, stop=True)
                last.then_inc(var_done, 1)

            def project(b, i):
                r, hf = PART_LIST[i]
                lo, slot = (CB if r == 1 else 0), (1 if r == 2 else 0)
                for c in range(PC):
                    m = (b * PARTS + i) * 2 * PC + 2 * c
                    first = (hf * PC + c) * T
                    wait(pe, proj_read, m - 3)
                    bank = c % 2 * 2
                    for k in range(DCONV):
                        last = pe.matmul(bank_ps[:, bank, :], w_fold[lo:lo + CB, k, :],
                                         xn[lo:lo + CB, slot, first + k:first + k + T],
                                         start=k == 0, stop=k == DCONV - 1)
                    last.then_inc(proj_done, 1)
                    wait(pe, proj_read, m - 2)
                    first += DCONV - 1
                    pe.matmul(bank_ps[:, bank + 1, :], w_in[lo:lo + CB, D1:], xn[lo:lo + CB, slot, first:first + T],
                              start=True, stop=True).then_inc(proj_done, 1)

            def image(b):
                pe.wait_ge(pad_ready, b + 1)
                wait(pe, proj_read, b * PARTS * 2 * PC)
                for c in range(NCHUNK):
                    conv(b, c, 0, w_pair, 2 * CB, OUTER)
                    conv(b, c, 1, w_pair, 2 * CB, MIDDLE)
                    if c >= 1:
                        mean(b, c - 1)
                    conv(b, c, 2, w_third, CB, OUTER)
                    if c >= 1:
                        variance(b, c - 1)
                pe.wait_ge(seq_ready, (b + 1) * NCHUNK)
                mean(b, NCHUNK - 1)
                if not is_last(b):
                    group_means(b + 1)
                pe.wait_ge(xn_ready, b * NCHUNK + PC)
                project(b, 0)
                variance(b, NCHUNK - 1)
                project(b, 1)
                pe.wait_ge(xn_ready, (b + 1) * NCHUNK)
                for i in range(2, PARTS):
                    project(b, i)

            group_means(0)
            over_batches(pe, image)

        @block.scalar
        def _(act):
            act.wait_ge(const_in, 160)
            act.wait_ge(setup, 5)

            def scale(b):
                act.wait_ge(scale_steps, b * SCALE_STEPS + 4)
                inverse_root(act, lnv[:, :], rstd[:, :], var[:, :], lnv_ready, b + 1).then_inc(rstd_ready, 1)

            def take_middle(b, c):
                m = b * NCHUNK + c
                act.wait_ge(conv_done, 3 * m + 2)
                wait(act, seq_ready, m - 1)
                act.activation(middle[:, c % 2, :], bank_ps[:, c % 2 * 3 + 1, :], ACT.Identity,
                               bias=conv_b[:, :]).then_inc(middle_ready, 1)

            def squares(b, c):
                m = b * NCHUNK + c
                act.wait_ge(cen_ready, m + 1)
                wait(act, var_done, m)
                act.activation(sq_sb[:, :, :], cen[:, c % 2, :, :], ACT.Square).then_inc(sq_ready, 1)

            def root(b, c):
                m = b * NCHUNK + c
                act.wait_ge(var_done, m + 1)
                act.activation(lnr[:, :, :], stat_ps[:, :, :], ACT.Ln, bias=eps[:, :]).then_inc(lnr_ready, 1)
                act.wait_ge(lnr_ready, m + 1)
                wait(act, scaled, m)
                act.activation(rstd_sb[:, :, :], lnr[:, :, :], ACT.Exp, scale=-0.5).then_inc(root_ready, 1)

            def affine(b, c):
                m = b * NCHUNK + c
                act.wait_ge(scaled, m + 1)
                if c == 0:
                    wait(act, xn_stored, b * 16)
                    wait(act, proj_done, b * PARTS * 2 * PC)
                for slot, at in ((0, c), (1, NCHUNK - 1 - c)):
                    first = DCONV - 1 + at * T
                    last = act.activation(xn[:, slot, first:first + T], cen[:, c % 2, slot, :], ACT.Identity,
                                          scale=ln_w[:, slot:slot + 1], bias=ln_b[:, slot:slot + 1])
                last.then_inc(xn_ready, 1)

            def take_proj(b, i):
                stores = b * (PARTS // 2) + i // 2
                wait(act, u_stored[i % 2], stores * 16)
                wait(act, z_stored[i % 2], stores * 16)
                for c in range(PC):
                    m = (b * PARTS + i) * 2 * PC + 2 * c
                    act.wait_ge(proj_done, m + 1)
                    act.activation(u_sb[:, i % 2, c * T:(c + 1) * T], bank_ps[:, c % 2 * 2, :], ACT.Silu,
                                   bias=conv1d_b[:, :]).then_inc(proj_read, 1)
                    act.wait_ge(proj_done, m + 2)
                    act.activation(z_sb[:, i % 2, c * T:(c + 1) * T], bank_ps[:, c % 2 * 2 + 1, :],
                                   ACT.Silu).then_inc(proj_read, 1)

            def normalise(b, c):
                root(b, c)
                affine(b, c)

            def image(b):
                act.preload_act_table_set("natural_log_exp_and_others")
                for c in range(NCHUNK):
                    take_middle(b, c)
                    if c >= 1:
                        squares(b, c - 1)
                        normalise(b, c - 1)
                squares(b, NCHUNK - 1)
                take_proj(b, 0)
                act.preload_act_table_set("natural_log_exp_and_others")
                normalise(b, NCHUNK - 1)
                if not is_last(b):
                    scale(b + 1)
                for i in range(1, PARTS):
                    take_proj(b, i)

            scale(0)
            over_batches(act, image)

        @block.vector
        def _(dve):
            dve.wait_ge(const_in, 160)
            dve.memset(eps[:, :], LN_EPS).then_inc(setup, 1)
            dve.memset(pad[:, :, :, :], 0.0).then_inc(setup, 1)
            dve.memset(seq[CB:, :, 1, :], 0.0).then_inc(setup, 1)
            dve.memset(xn[:, :, 0:DCONV - 1], 0.0).then_inc(setup, 1)
            for k in range(DCONV):
                last = dve.tensor_tensor(w_fold[:, k, :], w_in[:, 0:D1], w_conv[:, k, :], ALU.mult)
            last.then_inc(setup, 1)

            def measure(b):
                dve.wait_ge(x_in, (b + 1) * 16)
                wait(dve, g_done, b)
                group_stats(dve, b, xin, stats, mv, packed, sq, stat_steps, passed)

            def normalise(b):
                dve.wait_ge(g_done, b + 1)
                group_variance(dve, b, g_ps, gm, sq2, var, scale_steps)
                dve.wait_ge(rstd_ready, b + 1)
                dve.wait_ge(scale_steps, b * SCALE_STEPS + 4)
                dve.wait_ge(setup, 5)
                wait(dve, conv_done, b * 3 * NCHUNK)
                for half in range(2):
                    last = dve.tensor_scalar(pad[:, half, 1:1 + H, 1:1 + W],
                                             xin[:, half, :].rearrange("p (h w) -> p h w", w=W),
                                             gm[:, half:half + 1], rstd[:, half:half + 1], ALU.subtract, ALU.mult)
                last.then_inc(pad_ready, 1)

            def take_conv(b, c):
                m = b * NCHUNK + c
                src = bank_ps[:, c % 2 * 3:c % 2 * 3 + 3, :].rearrange("p s (r w) -> p s r w", w=W)
                mid = middle[:, c % 2, :].rearrange("p (r w) -> p r w", w=W)
                dst = seq[:, c % 2, :, :].rearrange("p s (r w) -> p s r w", w=W)
                dve.wait_ge(middle_ready, m + 1)
                wait(dve, cen_ready, m - 1)
                dve.tensor_tensor(dst[0:CB, 0], src[0:CB, 0], mid[0:CB], ALU.add)
                dve.tensor_tensor(dst[CB:, 0], src[CB:, 0][:, :, ::-1], mid[CB:][:, :, ::-1], ALU.add)
                dve.wait_ge(conv_done, 3 * m + 3)
                dve.tensor_tensor(dst[0:CB, 1], src[0:CB, 2][:, ::-1, :], mid[0:CB][:, ::-1, :],
                                  ALU.add).then_inc(seq_ready, 1)

            def centre(b, c):
                m = b * NCHUNK + c
                dve.wait_ge(mean_done, m + 1)
                dve.wait_ge(seq_ready, m + 1)
                wait(dve, xn_ready, m - 1)
                dve.tensor_tensor(cen[:, c % 2, :, :], seq[:, c % 2, :, :], stat_ps[:, :, :],
                                  ALU.subtract).then_inc(cen_ready, 1)

            def scale(b, c):
                m = b * NCHUNK + c
                dve.wait_ge(root_ready, m + 1)
                dve.wait_ge(cen_ready, m + 1)
                dve.tensor_tensor(cen[:, c % 2, :, :], cen[:, c % 2, :, :], rstd_sb[:, :, :],
                                  ALU.mult).then_inc(scaled, 1)

            def image(b):
                for c in range(NCHUNK + 1):
                    if c >= 1:
                        centre(b, c - 1)
                        scale(b, c - 1)
                    if c < NCHUNK:
                        take_conv(b, c)
                    if c == 1 and not is_last(b):
                        measure(b + 1)
                if not is_last(b):
                    normalise(b + 1)

            measure(0)
            normalise(0)
            over_batches(dve, image)


def layer1_output(nc, Y, Z, XN, x1, out, skip_in, w_out_in, mean_in, ln_w_in, ln_b_in, w_proj_in, proj_b_in):
    fp32 = mybir.dt.float32
    Yv = Y.rearrange("(b r c) p o j -> b c p (o r) j", b=B, r=NBR)
    Zv = Z.rearrange("(b r c) p o j -> b c p (o r) j", b=B, r=NBR)
    out_v = out.rearrange("b (s p) l -> b p s l", p=HALF)
    with ExitStack() as ctx:
        ctx.enter_context(nc.cleanup_on_exit())
        def sb(n, s, dt=fp32):
            return ctx.enter_context(nc.sbuf_tensor(f"m1_{n}", s, dt))

        def pb(n, s):
            return ctx.enter_context(nc.psum_tensor(f"m1_{n}", s, fp32))

        def sem(n):
            return nc.alloc_semaphore(f"m1_{n}")

        yb, zb, gated = sb("yb", [128, 2, NBR, T]), sb("zb", [128, 2, NBR, T]), sb("gated", [128, 2, NBR, T])
        xnb, x1b = sb("xnb", [128, 4, 2, T]), sb("x1b", [HALF, 4, 2, T])
        v, cen, sq = sb("v", [128, 2, 2, T]), sb("cen", [128, 2, 2, T]), sb("sq", [128, 2, T])
        yn = sb("yn", [128, 2, T])
        lnv, rstd = sb("lnv", [128, T]), sb("rstd", [128, T])
        res = sb("res", [HALF, 2, 2, T])
        skip, w_out, mean_w = sb("skip", [128, 1]), sb("w_out", [128, 2, 2 * CB]), sb("mean_w", [128, 2, 128])
        ln_w, ln_b, eps = sb("ln_w", [128, 2]), sb("ln_b", [128, 2]), sb("eps", [128, 1])
        w_proj, proj_b = sb("w_proj", [128, 2, CH]), sb("proj_b", [HALF, 2])
        op_ps, mean_ps, var_ps = pb("op_ps", [128, 2, T]), pb("mean_ps", [128, T]), pb("var_ps", [128, T])
        out_ps = pb("out_ps", [HALF, 2, 2, T])

        const_in, eps_set = sem("const_in"), sem("eps_set")
        yz_in = [sem(f"yz_in{p}") for p in range(2)]
        x_in = [sem(f"x_in{p}") for p in range(4)]
        gated_ready, op_done, v_ready, mean_done, cen_ready = (
            sem("gated_ready"), sem("op_done"), sem("v_ready"), sem("mean_done"), sem("cen_ready"))
        sq_ready, var_done, lnv_ready, rstd_ready, scaled = (
            sem("sq_ready"), sem("var_done"), sem("lnv_ready"), sem("rstd_ready"), sem("scaled"))
        yn_ready, out_done, res_ready = sem("yn_ready"), sem("out_done"), sem("res_ready")
        stored = [sem(f"stored{p}") for p in range(2)]
        block = ctx.enter_context(nc.Block())
        CONSTS = 16 * 7

        @block.sync
        def _(sp):
            for dst, src in ((skip[:, :], skip_in), (w_out[:, :, :], w_out_in), (mean_w[:, :, :], mean_in),
                             (ln_w[:, :], ln_w_in), (ln_b[:, :], ln_b_in), (w_proj[:, :, :], w_proj_in),
                             (proj_b[:, :], proj_b_in)):
                sp.dma_start(dst, src).then_inc(const_in, 16)

            def image(b):
                for c in range(NCHUNK):
                    m = b * NCHUNK + c
                    wait(sp, gated_ready, m - 1)
                    sp.dma_start(yb[:, c % 2, :, :], Yv[b, c]).then_inc(yz_in[c % 2], 16)
                    sp.dma_start(zb[:, c % 2, :, :], Zv[b, c]).then_inc(yz_in[c % 2], 16)
                    wait(sp, res_ready, m - 3)
                    sp.dma_start(xnb[:, c % 4, :, :], XN[b][:, :, c * T:(c + 1) * T]).then_inc(x_in[c % 4], 16)
                    sp.dma_start(x1b[:, c % 4, :, :], x1[b][:, :, c * T:(c + 1) * T]).then_inc(x_in[c % 4], 16)

            over_batches(sp, image)
            for p in range(2):
                sp.wait_ge(stored[p], 16 * B * NCHUNK // 2)

        @block.tensor
        def _(pe):
            pe.wait_ge(const_in, CONSTS)

            def out_proj(b, c):
                m = b * NCHUNK + c
                pe.wait_ge(gated_ready, m + 1)
                wait(pe, v_ready, m)
                for lo, hi, slot, r in ((0, CB, 0, 0), (CB, 2 * CB, 0, 1), (0, 2 * CB, 1, 2)):
                    last = pe.matmul(op_ps[lo:hi, slot, :], w_out[:, 1 if r == 2 else 0, 0:hi - lo],
                                     gated[:, c % 2, r, :], start=True, stop=True)
                last.then_inc(op_done, 1)

            def mean(b, c):
                m = b * NCHUNK + c
                pe.wait_ge(v_ready, m + 1)
                wait(pe, cen_ready, m)
                for slot in range(2):
                    last = pe.matmul(mean_ps[:, :], mean_w[:, slot, :], v[:, c % 2, slot, :], start=slot == 0, stop=slot == 1)
                last.then_inc(mean_done, 1)

            def variance(b, c):
                m = b * NCHUNK + c
                pe.wait_ge(sq_ready, m + 1)
                wait(pe, lnv_ready, m)
                for slot in range(2):
                    last = pe.matmul(var_ps[:, :], mean_w[:, slot, :], sq[:, slot, :], start=slot == 0, stop=slot == 1)
                last.then_inc(var_done, 1)

            def project(b, c):
                m = b * NCHUNK + c
                pe.wait_ge(yn_ready, m + 1)
                wait(pe, res_ready, m - 1)
                for half in range(2):
                    for slot in range(2):
                        last = pe.matmul(out_ps[:, c % 2, half, :], w_proj[:, slot, half * HALF:(half + 1) * HALF],
                                         yn[:, slot, :], start=slot == 0, stop=slot == 1)
                last.then_inc(out_done, 1)

            def image(b):
                for c in range(NCHUNK + 3):
                    if c < NCHUNK:
                        out_proj(b, c)
                    if 1 <= c <= NCHUNK:
                        mean(b, c - 1)
                    if 2 <= c <= NCHUNK + 1:
                        variance(b, c - 2)
                    if c >= 3:
                        project(b, c - 3)

            over_batches(pe, image)

        @block.scalar
        def _(act):
            act.wait_ge(const_in, CONSTS)
            act.wait_ge(eps_set, 1)
            act.preload_act_table_set("natural_log_exp_and_others")

            def squares(b, c):
                m = b * NCHUNK + c
                act.wait_ge(cen_ready, m + 1)
                wait(act, var_done, m)
                act.activation(sq[:, :, :], cen[:, c % 2, :, :], ACT.Square).then_inc(sq_ready, 1)

            def root(b, c):
                m = b * NCHUNK + c
                act.wait_ge(var_done, m + 1)
                act.activation(lnv[:, :], var_ps[:, :], ACT.Ln, bias=eps[:, :]).then_inc(lnv_ready, 1)
                act.wait_ge(lnv_ready, m + 1)
                wait(act, scaled, m)
                act.activation(rstd[:, :], lnv[:, :], ACT.Exp, scale=-0.5).then_inc(rstd_ready, 1)

            def affine(b, c):
                m = b * NCHUNK + c
                act.wait_ge(scaled, m + 1)
                wait(act, out_done, m)
                for slot in range(2):
                    last = act.activation(yn[:, slot, :], cen[:, c % 2, slot, :], ACT.Identity,
                                          scale=ln_w[:, slot:slot + 1], bias=ln_b[:, slot:slot + 1])
                last.then_inc(yn_ready, 1)

            def store(b, c):
                m = b * NCHUNK + c
                act.wait_ge(res_ready, m + 1)
                act.dma_start(out_v[b][:, :, c * T:(c + 1) * T], res[:, c % 2, :, :]).then_inc(stored[c % 2], 16)

            def image(b):
                for c in range(NCHUNK + 3):
                    if 1 <= c <= NCHUNK:
                        squares(b, c - 1)
                    if 2 <= c <= NCHUNK + 1:
                        root(b, c - 2)
                        affine(b, c - 2)
                    if c >= 3:
                        store(b, c - 3)

            over_batches(act, image)

        @block.vector
        def _(dve):
            dve.memset(eps[:, :], LN_EPS).then_inc(eps_set, 1)
            dve.wait_ge(const_in, CONSTS)

            def add_skip(b, c):
                m = b * NCHUNK + c
                dve.wait_ge(op_done, m + 1)
                dve.wait_ge(x_in[c % 4], b * (32 * NCHUNK // 4) + (c // 4 + 1) * 32)
                wait(dve, cen_ready, m - 1)
                dve.scalar_tensor_tensor(v[:, c % 2, :, :], xnb[:, c % 4, :, :], skip[:, 0:1], op_ps[:, :, :],
                                         ALU.mult, ALU.add).then_inc(v_ready, 1)

            def centre(b, c):
                m = b * NCHUNK + c
                dve.wait_ge(mean_done, m + 1)
                wait(dve, yn_ready, m - 1)
                dve.tensor_tensor(cen[:, c % 2, :, :], v[:, c % 2, :, :],
                                  mean_ps[:, :].unsqueeze(1).broadcast_to([128, 2, T]), ALU.subtract).then_inc(cen_ready, 1)

            def scale(b, c):
                m = b * NCHUNK + c
                dve.wait_ge(rstd_ready, m + 1)
                dve.wait_ge(cen_ready, m + 1)
                dve.tensor_tensor(cen[:, c % 2, :, :], cen[:, c % 2, :, :],
                                  rstd[:, :].unsqueeze(1).broadcast_to([128, 2, T]), ALU.mult).then_inc(scaled, 1)

            def residual(b, c):
                m = b * NCHUNK + c
                dve.wait_ge(out_done, m + 1)
                wait(dve, stored[c % 2], b * (16 * NCHUNK // 2) + (c // 2) * 16)
                for half in range(2):
                    last = dve.scalar_tensor_tensor(res[:, c % 2, half, :], out_ps[:, c % 2, half, :],
                                                    proj_b[:, half:half + 1], x1b[:, c % 4, half, :], ALU.add, ALU.add)
                last.then_inc(res_ready, 1)

            def image(b):
                for c in range(NCHUNK + 3):
                    if c < NCHUNK:
                        add_skip(b, c)
                    if 1 <= c <= NCHUNK:
                        centre(b, c - 1)
                    if 2 <= c <= NCHUNK + 1:
                        scale(b, c - 2)
                    if c >= 3:
                        residual(b, c - 3)

            over_batches(dve, image)

        @block.gpsimd
        def _(pool):
            def image(b):
                for c in range(NCHUNK):
                    m = b * NCHUNK + c
                    pool.wait_ge(yz_in[c % 2], b * (32 * NCHUNK // 2) + (c // 2 + 1) * 32)
                    wait(pool, op_done, m - 1)
                    pool.tensor_tensor(gated[:, c % 2, :, :], yb[:, c % 2, :, :], zb[:, c % 2, :, :],
                                       ALU.mult).then_inc(gated_ready, 1)

            over_batches(pool, image)


def build(nc, arg, out):
    fp32 = mybir.dt.float32

    def scratch(name, shape):
        return nc.dram_tensor(name, shape, fp32, kind="Internal").ap()

    units0, units1 = B * K0 * NCHUNK, B * NBR * NCHUNK
    U0, Y0 = scratch("U0", (units0, 128, ND0, T)), scratch("Y0", (units0, 128, ND0, T))
    x1 = scratch("x1", (B, HALF, 2, L))
    U1, Y1, Z1 = (scratch(n, (units1, 128, 1, T)) for n in ("U1", "Y1", "Z1"))
    XN = scratch("XN", (B, 128, 2, L))
    x = arg["x"].rearrange("b (s p) l -> b p s l", p=HALF)

    layer0_features(nc, x, U0, arg["group_mean"], arg["a_in"], arg["a_taps"], arg["a_conv_b"], arg["ident"])
    scan_phase(nc, "s0", (B, K0, ND0, 1, R0), U0, Y0, arg["a_xproj"], arg["a_dt"], arg["a_small"],
               arg["keep"], arg["ident"], arg["select"])
    layer0_output(nc, Y0, x, x1, arg["mean_384"], arg["a_ln_w"], arg["a_ln_b"], arg["a_out"])
    layer1_features(nc, x1, U1, Z1, XN, arg["group_mean"], arg["b_pair"], arg["b_third"], arg["b_conv_b"],
                    arg["mean_64"], arg["b_ln1_w"], arg["b_ln1_b"], arg["b_in"], arg["b_conv1d"], arg["b_conv1d_b"])
    scan_phase(nc, "s1", (B * NBR, 1, 1, 2, R1), U1, Y1, arg["b_xproj"], arg["b_dt"], arg["b_small"],
               arg["keep"], arg["ident"], arg["select"])
    layer1_output(nc, Y1, Z1, XN, x1, out, arg["b_skip"], arg["b_out"], arg["mean_192"], arg["b_ln_w"],
                  arg["b_ln_b"], arg["b_proj"], arg["b_proj_b"])


def kernel(**inputs):
    import numpy as np
    import concourse.bacc as _bacc
    from concourse.bass_utils import run_bass_kernel_spmd as _run

    a = {k: np.asarray(v) for k, v in inputs.items()}
    la = {k[len("L0_conv_"):]: v for k, v in a.items() if k.startswith("L0_conv_")}
    lb = {k[len("L1_conv_"):]: v for k, v in a.items() if k.startswith("L1_conv_")}
    f = a["x"].dtype

    def columns(v, n):
        return np.swapaxes(v.reshape(*v.shape[:-1], n, 128), -1, -2)

    def xproj(w, rank, nd):
        bc = w[:, rank:]
        w = np.concatenate([bc, bc, bc, w[:, :rank]], 1)
        return w.reshape(len(w), XROWS + rank, nd, 128).transpose(0, 3, 2, 1)

    def small(bias, D, A_log, nd):
        k = len(bias)
        logs = A_log.reshape(k, nd, 128, N_STATE).transpose(0, 2, 1, 3).reshape(k, 128, nd * N_STATE)
        return np.concatenate([columns(bias, nd), columns(D, nd), logs], 2)

    def pair(v):
        return np.stack([np.concatenate([v, v]), np.concatenate([v, np.zeros_like(v)])], 1)

    def slots(v):
        return np.stack([v[:128], np.concatenate([v[128:], np.zeros_like(v[:64])])], 1)

    ident = np.eye(128, dtype=f)
    select = np.zeros((XROWS, 2 * N_STATE, 128), f)
    for n in range(2 * N_STATE):
        select[n::2 * N_STATE, n] = 1
    keep = np.ones((NCHUNK, 128, 1), f)
    keep[-1] = 0
    group_mean, mean_64 = np.zeros((HALF, HALF), f), np.zeros((128, 128), f)
    for g in range(0, HALF, CH // 32):
        group_mean[g:g + CH // 32, g:g + CH // 32] = 32 / CH
    for g in range(0, 128, CB):
        mean_64[g:g + CB, g:g + CB] = 1 / CB
    mean_192 = np.zeros((128, 2, 128), f)
    mean_192[:, 0] = 1 / CH
    mean_192[:CH - 128, 1] = 1 / CH

    taps = lb["conv1_w"].reshape(CB, 2, HALF, 3, 3).transpose(2, 1, 3, 4, 0)
    w_out = lb["out_proj_w"].T
    arrays = {
        "x": a["x"].reshape(B, CH, L),
        "ident": ident, "select": select.reshape(XROWS, -1), "keep": keep, "group_mean": group_mean,
        "mean_384": np.full((128, 128), 1 / D0, f), "mean_64": mean_64, "mean_192": mean_192,
        "a_in": la["in_proj_w"].T.reshape(2, HALF, D0).transpose(1, 0, 2),
        "a_taps": la["conv_w"].reshape(ND0, 128, TAPS).transpose(1, 0, 2),
        "a_conv_b": columns(la["conv_b"], ND0),
        "a_xproj": xproj(la["x_proj_weight"], R0, ND0),
        "a_dt": la["dt_projs_weight"].reshape(K0, ND0, 128, R0).transpose(0, 3, 1, 2),
        "a_small": small(la["dt_projs_bias"], la["Ds"].reshape(K0, D0), la["A_logs"], ND0),
        "a_ln_w": columns(la["ln_w"], ND0), "a_ln_b": columns(la["ln_b"], ND0),
        "a_out": la["out_proj_w"].T.reshape(ND0, 128, CH).transpose(1, 0, 2),
        "b_pair": np.concatenate([taps, taps[:, :, :, ::-1]], 4).reshape(HALF, 2, TAPS, 2 * CB),
        "b_third": taps[:, :, ::-1].reshape(HALF, 2, TAPS, CB),
        "b_conv_b": np.concatenate([lb["conv1_b"]] * 2)[:, None],
        "b_ln1_w": pair(lb["norm1_w"]), "b_ln1_b": pair(lb["norm1_b"]),
        "b_in": np.concatenate([lb["in_proj_w"].T] * 2),
        "b_conv1d": np.broadcast_to(lb["convd_w"].T[None], (128, DCONV, D1)),
        "b_conv1d_b": lb["convd_b"][:, None],
        "b_xproj": xproj(lb["x_proj_w"][None], R1, 1),
        "b_dt": lb["dt_proj_w"].T[None, :, None, :],
        "b_small": small(lb["dt_proj_b"][None], lb["D_param"][None], lb["A_log"], 1),
        "b_skip": np.broadcast_to(lb["skip_scale"][None], (128, 1)),
        "b_out": np.stack([np.concatenate([w_out, np.zeros_like(w_out)], 1)] * 2, 1),
        "b_ln_w": slots(lb["norm_w"]), "b_ln_b": slots(lb["norm_b"]),
        "b_proj": slots(lb["proj_w"].T), "b_proj_b": lb["proj_b"].reshape(2, HALF).T,
    }
    nc = _bacc.Bacc("TRN2", target_bir_lowering=False, num_devices=1)
    arrays = {f"in_{k}": np.ascontiguousarray(v) for k, v in arrays.items()}
    arg = {k[3:]: nc.dram_tensor(k, v.shape, mybir.dt.from_np(v.dtype), kind="ExternalInput").ap()
           for k, v in arrays.items()}
    out = nc.dram_tensor("out", (B, CH, L), mybir.dt.float32, kind="ExternalOutput").ap()
    build(nc, arg, out)
    r = _run(nc, [arrays], core_ids=[0])
    return r.results[0]["out"].reshape(B, CH, H, W)
```
